# Optimizing a Trainium2 kernel written in Bass

```python
import numpy as np
import jax
import jax.numpy as jnp

def _softmax(x, axis=-1):
    return jax.nn.softmax(x, axis=axis)

def _gelu(x):
    return jax.nn.gelu(x, approximate=True)

def _silu(x):
    return jax.nn.silu(x)

def _sigmoid(x):
    return jax.nn.sigmoid(x)

def _layernorm(x, axis=-1, eps=1e-05):
    m = jnp.mean(x, axis=axis, keepdims=True)
    v = jnp.var(x, axis=axis, keepdims=True)
    return (x - m) / jnp.sqrt(v + eps)

def _scatter_add(tgt, idx, src, axis=0):
    return tgt.at[idx].add(src)

def _segment_sum(src, seg, n):
    return jax.ops.segment_sum(src, seg, n)
kernel_name = 'mk_metaformer_d2_conv_nchw512_r4_cc1b7e'

def setup_inputs(seed: int=0):
    np.random.seed(seed)
    _w = jnp.asarray

    def _rec_inputs():
        import jax
        import jax.numpy as jnp
        _gk = jax.random.key(seed)
        x = -7.109e-05 + 0.9999 * jax.random.normal(jax.random.fold_in(_gk, 1), (2, 128, 64, 64), jnp.float32)
        return x
    x = _rec_inputs()

    def _L0_conv_setup():
        import jax, jax.numpy as jnp
        import numpy as np
        B, C, H, W = (2, 128, 64, 64)
        EPS = 1e-05

        def _dwconv(x, k):
            return jax.lax.conv_general_dilated(x, k, window_strides=(1, 1), padding='VALID', dimension_numbers=('NCHW', 'OIHW', 'NCHW'), feature_group_count=x.shape[1])

        def _bn_relu(y, gamma, beta):
            m = jnp.mean(y, axis=(0, 2, 3), keepdims=True)
            v = jnp.var(y, axis=(0, 2, 3), keepdims=True)
            yn = (y - m) * jax.lax.rsqrt(v + EPS)
            return jax.nn.relu(yn * gamma.reshape(1, -1, 1, 1) + beta.reshape(1, -1, 1, 1))
        key = jax.random.key(seed)
        ks = jax.random.split(key, 11)
        inp = {'x': jax.random.normal(ks[0], (B, C, H, W), dtype=jnp.float32), 'w1': jax.random.normal(ks[1], (C, 1, H, 1), dtype=jnp.float32) * 0.05, 'w2': jax.random.normal(ks[2], (C, 1, 1, W), dtype=jnp.float32) * 0.05, 'g1': jax.random.uniform(ks[3], (C,), dtype=jnp.float32) + 0.5, 'b1': jax.random.normal(ks[4], (C,), dtype=jnp.float32) * 0.1, 'g2': jax.random.uniform(ks[5], (C,), dtype=jnp.float32) + 0.5, 'b2': jax.random.normal(ks[6], (C,), dtype=jnp.float32) * 0.1, 'lw1': jax.random.normal(ks[7], (2 * C, C), dtype=jnp.float32) * 0.02, 'lb1': jax.random.normal(ks[8], (2 * C,), dtype=jnp.float32) * 0.02, 'lw2': jax.random.normal(ks[9], (C, 2 * C), dtype=jnp.float32) * 0.02, 'lb2': jax.random.normal(ks[10], (C,), dtype=jnp.float32) * 0.02}
        return inp
    _L0_conv_all = _L0_conv_setup()
    _L0_conv_in = {k: v for k, v in _L0_conv_all.items() if k in ('w1', 'w2', 'g1', 'b1', 'g2', 'b2', 'lw1', 'lb1', 'lw2', 'lb2')}
    del _L0_conv_all

    def _L0_ffn_setup():
        import jax, jax.numpy as jnp
        import numpy as np
        TOP_K = 2

        def _moe_forward(x, Wr, br, W1, b1, W2, b2):
            leading = x.shape[:-1]
            d = x.shape[-1]
            E = Wr.shape[0]
            xf = x.reshape(-1, d)
            N = xf.shape[0]
            logits = xf @ Wr.T + br
            routing = jax.nn.softmax(logits, axis=-1)
            sel_w, sel_idx = jax.lax.top_k(routing, TOP_K)
            sel_w = sel_w / jnp.sum(sel_w, axis=-1, keepdims=True)
            combine = jnp.zeros((N, E), dtype=xf.dtype).at[jnp.arange(N)[:, None], sel_idx].add(sel_w)
            h = jax.nn.gelu(jnp.einsum('nd,edf->enf', xf, W1) + b1[:, None, :])
            y = jnp.einsum('enf,efd->end', h, W2) + b2[:, None, :]
            out = jnp.einsum('ne,end->nd', combine, y)
            return out.reshape(*leading, d)
        key = jax.random.key(seed)
        ks = jax.random.split(key, 7)
        d_model, d_ff, E = (128, 512, 8)
        B, S = (2, 512)
        std = 0.02
        return {'x': jax.random.normal(ks[0], (B, S, d_model), dtype=jnp.float32), 'Wr': jax.random.normal(ks[1], (E, d_model), dtype=jnp.float32) * std, 'br': jnp.zeros((E,), dtype=jnp.float32), 'W1': jax.random.normal(ks[2], (E, d_model, d_ff), dtype=jnp.float32) * (1.0 / np.sqrt(d_model)), 'b1': jnp.zeros((E, d_ff), dtype=jnp.float32), 'W2': jax.random.normal(ks[3], (E, d_ff, d_model), dtype=jnp.float32) * (1.0 / np.sqrt(d_ff)), 'b2': jnp.zeros((E, d_model), dtype=jnp.float32)}
    _L0_ffn_all = _L0_ffn_setup()
    _L0_ffn_in = {k: v for k, v in _L0_ffn_all.items() if k in ('Wr', 'br', 'W1', 'b1', 'W2', 'b2')}
    del _L0_ffn_all

    def _L1_conv_setup():
        import jax, jax.numpy as jnp
        import numpy as np
        KERNELS = (1, 3, 5, 7, 9, 11, 13)

        def _maxpool_same(x, k):
            if k == 1:
                return x
            return jax.lax.reduce_window(x, -jnp.inf, jax.lax.max, window_dimensions=(1, 1, k, k), window_strides=(1, 1, 1, 1), padding='SAME')
        key = jax.random.key(seed)
        k_x, k_w1, k_b1, k_w2, k_b2 = jax.random.split(key, 5)
        b, c, h, w = (8, 128, 16, 16)
        c16 = c // 16
        x = jax.random.normal(k_x, (b, c, h, w), dtype=jnp.float32)
        w1 = jax.random.normal(k_w1, (c16, c), dtype=jnp.float32) * (1.0 / np.sqrt(c))
        b1 = jax.random.normal(k_b1, (c16,), dtype=jnp.float32) * 0.1
        w2 = jax.random.normal(k_w2, (c, c16), dtype=jnp.float32) * (1.0 / np.sqrt(c16))
        b2 = jax.random.uniform(k_b2, (c,), dtype=jnp.float32, minval=0.0, maxval=6.0)
        return {'x': x, 'w1': w1, 'b1': b1, 'w2': w2, 'b2': b2}
    _L1_conv_all = _L1_conv_setup()
    _L1_conv_in = {k: v for k, v in _L1_conv_all.items() if k in ('w1', 'b1', 'w2', 'b2')}
    del _L1_conv_all

    def _L1_ffn_setup():
        import jax, jax.numpy as jnp
        import numpy as np
        TOP_K = 2
        key = jax.random.key(seed)
        ks = jax.random.split(key, 4)
        B, S, D, H, E = (2, 1024, 128, 512, 8)
        scale_in = 1.0 / np.sqrt(D)
        scale_h = 1.0 / np.sqrt(H)
        return {'x': jax.random.normal(ks[0], (B, S, D), dtype=jnp.float32), 'gate_w': jax.random.normal(ks[1], (D, E), dtype=jnp.float32) * scale_in, 'gate_b': jnp.zeros((E,), dtype=jnp.float32), 'w1': jax.random.normal(ks[2], (E, D, H), dtype=jnp.float32) * scale_in, 'b1': jnp.zeros((E, H), dtype=jnp.float32), 'w2': jax.random.normal(ks[3], (E, H, D), dtype=jnp.float32) * scale_h, 'b2': jnp.zeros((E, D), dtype=jnp.float32)}
    _L1_ffn_all = _L1_ffn_setup()
    _L1_ffn_in = {k: v for k, v in _L1_ffn_all.items() if k in ('gate_w', 'gate_b', 'w1', 'b1', 'w2', 'b2')}
    del _L1_ffn_all
    return {'x': x, 'L0_conv_w1': _L0_conv_in['w1'], 'L0_conv_w2': _L0_conv_in['w2'], 'L0_conv_g1': _L0_conv_in['g1'], 'L0_conv_b1': _L0_conv_in['b1'], 'L0_conv_g2': _L0_conv_in['g2'], 'L0_conv_b2': _L0_conv_in['b2'], 'L0_conv_lw1': _L0_conv_in['lw1'], 'L0_conv_lb1': _L0_conv_in['lb1'], 'L0_conv_lw2': _L0_conv_in['lw2'], 'L0_conv_lb2': _L0_conv_in['lb2'], 'L0_ffn_Wr': _L0_ffn_in['Wr'], 'L0_ffn_br': _L0_ffn_in['br'], 'L0_ffn_W1': _L0_ffn_in['W1'], 'L0_ffn_b1': _L0_ffn_in['b1'], 'L0_ffn_W2': _L0_ffn_in['W2'], 'L0_ffn_b2': _L0_ffn_in['b2'], 'L1_conv_w1': _L1_conv_in['w1'], 'L1_conv_b1': _L1_conv_in['b1'], 'L1_conv_w2': _L1_conv_in['w2'], 'L1_conv_b2': _L1_conv_in['b2'], 'L1_ffn_gate_w': _L1_ffn_in['gate_w'], 'L1_ffn_gate_b': _L1_ffn_in['gate_b'], 'L1_ffn_w1': _L1_ffn_in['w1'], 'L1_ffn_b1': _L1_ffn_in['b1'], 'L1_ffn_w2': _L1_ffn_in['w2'], 'L1_ffn_b2': _L1_ffn_in['b2']}

def reference(x, L0_conv_w1, L0_conv_w2, L0_conv_g1, L0_conv_b1, L0_conv_g2, L0_conv_b2, L0_conv_lw1, L0_conv_lb1, L0_conv_lw2, L0_conv_lb2, L0_ffn_Wr, L0_ffn_br, L0_ffn_W1, L0_ffn_b1, L0_ffn_W2, L0_ffn_b2, L1_conv_w1, L1_conv_b1, L1_conv_w2, L1_conv_b2, L1_ffn_gate_w, L1_ffn_gate_b, L1_ffn_w1, L1_ffn_b1, L1_ffn_w2, L1_ffn_b2):
    import jax
    import jax.numpy as jnp

    def _L0_conv_ref(x, w1, w2, g1, b1, g2, b2, lw1, lb1, lw2, lb2):
        import jax, jax.numpy as jnp
        import numpy as np
        B, C, H, W = (2, 128, 64, 64)
        EPS = 1e-05

        def _dwconv(x, k):
            return jax.lax.conv_general_dilated(x, k, window_strides=(1, 1), padding='VALID', dimension_numbers=('NCHW', 'OIHW', 'NCHW'), feature_group_count=x.shape[1])

        def _bn_relu(y, gamma, beta):
            m = jnp.mean(y, axis=(0, 2, 3), keepdims=True)
            v = jnp.var(y, axis=(0, 2, 3), keepdims=True)
            yn = (y - m) * jax.lax.rsqrt(v + EPS)
            return jax.nn.relu(yn * gamma.reshape(1, -1, 1, 1) + beta.reshape(1, -1, 1, 1))
        b, c, h, w = x.shape
        xl1 = _bn_relu(_dwconv(x, w1), g1, b1)
        xl2 = _bn_relu(_dwconv(x, w2), g2, b2)
        dot_cb = jnp.einsum('bck,bck->cb', xl1[:, :, 0, :], xl2[:, :, :, 0])
        num = dot_cb.reshape(b, c)
        num = num @ lw1.T + lb1
        num = num @ lw2.T + lb2
        num = jax.nn.softmax(num, axis=1)
        return x * num[:, :, None, None]

    def _L0_ffn_ref(x, Wr, br, W1, b1, W2, b2):
        import jax, jax.numpy as jnp
        import numpy as np
        TOP_K = 2

        def _moe_forward(x, Wr, br, W1, b1, W2, b2):
            leading = x.shape[:-1]
            d = x.shape[-1]
            E = Wr.shape[0]
            xf = x.reshape(-1, d)
            N = xf.shape[0]
            logits = xf @ Wr.T + br
            routing = jax.nn.softmax(logits, axis=-1)
            sel_w, sel_idx = jax.lax.top_k(routing, TOP_K)
            sel_w = sel_w / jnp.sum(sel_w, axis=-1, keepdims=True)
            combine = jnp.zeros((N, E), dtype=xf.dtype).at[jnp.arange(N)[:, None], sel_idx].add(sel_w)
            h = jax.nn.gelu(jnp.einsum('nd,edf->enf', xf, W1) + b1[:, None, :])
            y = jnp.einsum('enf,efd->end', h, W2) + b2[:, None, :]
            out = jnp.einsum('ne,end->nd', combine, y)
            return out.reshape(*leading, d)
        return _moe_forward(x, Wr, br, W1, b1, W2, b2)

    def _L1_conv_ref(x, w1, b1, w2, b2):
        import jax, jax.numpy as jnp
        import numpy as np
        KERNELS = (1, 3, 5, 7, 9, 11, 13)

        def _maxpool_same(x, k):
            if k == 1:
                return x
            return jax.lax.reduce_window(x, -jnp.inf, jax.lax.max, window_dimensions=(1, 1, k, k), window_strides=(1, 1, 1, 1), padding='SAME')
        b, c, h, w = x.shape
        n_k = len(KERNELS)
        gap = jnp.mean(x, axis=(2, 3))
        hmid = jax.nn.relu(jnp.einsum('bc,ec->be', gap, w1) + b1)
        score = jnp.einsum('be,ce->bc', hmid, w2) + b2
        s = jax.nn.relu(score)
        q_s = jnp.clip(jnp.floor(jax.lax.stop_gradient(s)), 0, n_k - 2).astype(jnp.int32)
        q_b = q_s + 1
        pools = jnp.stack([_maxpool_same(x, k) for k in KERNELS], axis=2)
        s_out = jnp.take_along_axis(pools, q_s[:, :, None, None, None], axis=2)[:, :, 0]
        b_out = jnp.take_along_axis(pools, q_b[:, :, None, None, None], axis=2)[:, :, 0]
        frac_b = (s - q_s.astype(s.dtype))[:, :, None, None]
        frac_s = (q_b.astype(s.dtype) - s)[:, :, None, None]
        return frac_b * b_out + frac_s * s_out + x

    def _L1_ffn_ref(x, gate_w, gate_b, w1, b1, w2, b2):
        import jax, jax.numpy as jnp
        import numpy as np
        TOP_K = 2
        B, S, D = x.shape
        E = gate_w.shape[1]
        flat_x = x.reshape(-1, D)
        gate_logits = flat_x @ gate_w + gate_b
        raw_weights = jax.nn.softmax(gate_logits, axis=-1)
        top_w, top_idx = jax.lax.top_k(raw_weights, TOP_K)
        one_hot = jax.nn.one_hot(top_idx, E, dtype=flat_x.dtype)
        gate_output = (one_hot * top_w[..., None]).sum(axis=-2)
        h = jax.nn.gelu(jnp.einsum('td,edh->teh', flat_x, w1) + b1, approximate=False)
        expert_out = jnp.einsum('teh,ehd->ted', h, w2) + b2
        combined = jnp.einsum('ted,te->td', expert_out, gate_output)
        return combined.reshape(B, S, -1)

    def _gn(v, G=32, eps=1e-05):
        B_, C_, H_, W_ = v.shape
        g = v.reshape(B_, G, C_ // G, H_, W_)
        m = jnp.mean(g, axis=(2, 3, 4), keepdims=True)
        s = jnp.var(g, axis=(2, 3, 4), keepdims=True)
        return ((g - m) / jnp.sqrt(s + eps)).reshape(v.shape)

    def _ln_c(v, eps=1e-06):
        m = jnp.mean(v, axis=1, keepdims=True)
        s = jnp.var(v, axis=1, keepdims=True)
        return (v - m) / jnp.sqrt(s + eps)

    def _ln_t(v, eps=1e-05):
        m = jnp.mean(v, axis=-1, keepdims=True)
        s = jnp.var(v, axis=-1, keepdims=True)
        return (v - m) / jnp.sqrt(s + eps)

    def _to_tokens(v):
        B_, C_, H_, W_ = v.shape
        return v.reshape(B_, C_, H_ * W_).transpose(0, 2, 1)

    def _from_tokens(t, like):
        B_, C_, H_, W_ = like.shape
        return t.transpose(0, 2, 1).reshape(B_, C_, H_, W_)
    x = x + _L0_conv_ref(_ln_c(x), L0_conv_w1, L0_conv_w2, L0_conv_g1, L0_conv_b1, L0_conv_g2, L0_conv_b2, L0_conv_lw1, L0_conv_lb1, L0_conv_lw2, L0_conv_lb2)
    t = _to_tokens(x)
    t = t + _L0_ffn_ref(_ln_t(t), L0_ffn_Wr, L0_ffn_br, L0_ffn_W1, L0_ffn_b1, L0_ffn_W2, L0_ffn_b2)
    x = _from_tokens(t, x)
    x = x + _L1_conv_ref(_ln_c(x), L1_conv_w1, L1_conv_b1, L1_conv_w2, L1_conv_b2)
    t = _to_tokens(x)
    t = t + _L1_ffn_ref(_ln_t(t), L1_ffn_gate_w, L1_ffn_gate_b, L1_ffn_w1, L1_ffn_b1, L1_ffn_w2, L1_ffn_b2)
    x = _from_tokens(t, x)
    return x

_drawn_inputs = setup_inputs


def setup_inputs(seed=0):
    import zlib

    import numpy as np

    out = dict(_drawn_inputs(seed))
    spreads = {'L0_ffn_br': (0.0, 0.1),
     'L0_ffn_b1': (0.0, 0.1),
     'L0_ffn_b2': (0.0, 0.1),
     'L1_ffn_gate_b': (0.0, 0.494),
     'L1_ffn_b1': (0.0, 0.8),
     'L1_ffn_b2': (0.0, 0.555)}
    factors = {'L0_conv_w1': 9.415,
     'L0_conv_w2': 11.219,
     'L0_conv_g1': 3.623,
     'L0_conv_b1': 5.53,
     'L0_conv_g2': 3.778,
     'L0_conv_b2': 21.026,
     'L0_conv_lb1': 64.0,
     'L0_conv_lb2': 40.974,
     'L1_conv_w1': 2.799}
    for name, (base, spread) in spreads.items():
        noise = np.random.default_rng([zlib.crc32(name.encode()), seed]).standard_normal(out[name].shape)
        drawn = base * np.exp(spread * noise) if base else spread * noise
        out[name] = jnp.asarray(drawn.astype(out[name].dtype))
    for name, factor in factors.items():
        out[name] = (out[name] * factor).astype(out[name].dtype)
    return out
```

```python
from contextlib import ExitStack, contextmanager

import numpy as np

import concourse.bass as bass
from concourse import mybir

ALU = mybir.AluOpType
ACT = mybir.ActivationFunctionType
AX = mybir.AxisListType
F32 = mybir.dt.float32
BF16 = mybir.dt.bfloat16
I32 = mybir.dt.int32
U32 = mybir.dt.uint32

P = 128
IMAGES, SIDE = 2, 64
TOKENS = SIDE * SIDE
BLOCKS = TOKENS // P
GROUP = 4
GROUPS = BLOCKS // GROUP
EXPERTS, CHOICES, HIDDEN = 8, 2, 512
CHUNKS = HIDDEN // P
PAIRS = CHOICES * TOKENS
SLOTS = 256
HALVES = SLOTS // P
TILES = (PAIRS - EXPERTS) // SLOTS + EXPERTS
EMPTY = 2 * PAIRS
RING = 4
KERNELS = 7
UNITS = 4
BIAS = CHUNKS + 1
PEEL = 7
AHEAD = 4
TURNS = (TILES - AHEAD - PEEL) // RING


class Count:

    def __init__(self, sem=None, eng=None, start=0):
        self.sem, self.eng, self.n, self.x = sem, eng, start, None

    def value(self, back=0):
        n = self.n - back
        return n if self.x is None else self.x + n

    def step(self, ins=None):
        self.n += 1
        if ins is not None:
            ins.then_inc(self.sem, 1)

    def wait(self, back=0):
        self.eng.wait_ge(self.sem, self.value(back))


@contextmanager
def rounds(eng, times, *counts):
    first = [c.n for c, _ in counts]
    with eng.Fori(0, times) as i:
        for c, per in counts:
            c.x = i * per
        yield i
    for (c, per), n in zip(counts, first):
        assert c.n - n == per, (c.sem, c.n - n, per)
        c.x, c.n = None, n + per * times


class Tile:

    def __init__(self, unit, j, i=None):
        self.unit, self.at, self.s, self.i = unit, j, unit * TILES + j, i

    def j(self, d=0):
        return self.at + d if self.i is None else self.i * RING + (self.at + d)

    def has(self, d=0):
        return self.i is not None or 0 <= self.at + d < TILES

    def old(self, d):
        return self.s + d >= 0

    def done(self, d=0, per=1, part=None):
        n = (self.s + d) * per + (per if part is None else part)
        return n if self.i is None else self.i * (RING * per) + n

    def slot(self, n, d=0):
        return (self.s + d) % n

    def landed(self, d=0, each=1):
        n = ((self.s + d) // RING + 1) * 16 * each
        return n if self.i is None else self.i * (16 * each) + n


def tile_steps(eng, unit, step):
    for j in range(PEEL):
        step(Tile(unit, j))
    with eng.Fori(0, TURNS) as i:
        for k in range(RING):
            step(Tile(unit, PEEL + k, i))
    for j in range(PEEL + TURNS * RING, TILES + 2):
        step(Tile(unit, j))


def build(nc, x, L0_conv_w1, L0_conv_w2, L0_conv_g1, L0_conv_b1, L0_conv_g2, L0_conv_b2, L0_conv_lw1, L0_conv_lb1,
          L0_conv_lw2, L0_conv_lb2, L0_ffn_Wr, L0_ffn_br, L0_ffn_W1, L0_ffn_b1, L0_ffn_W2, L0_ffn_b2, L1_conv_w1,
          L1_conv_b1, L1_conv_w2, L1_conv_b2, L1_ffn_gate_w, L1_ffn_gate_b, L1_ffn_w1, L1_ffn_b1, L1_ffn_w2,
          L1_ffn_b2, out):
    with ExitStack() as ctx:
        def sb(name, shape, dt=F32):
            return ctx.enter_context(nc.sbuf_tensor(name, shape, dt))

        def ps(name, shape, dt=F32):
            return ctx.enter_context(nc.psum_tensor(name, shape, dt))

        def sem(name):
            return ctx.enter_context(nc.semaphore(name))

        xn_rows = [nc.dram_tensor(f"xn_rows{u}", [TOKENS, P], F32).ap() for u in range(UNITS)]
        y_rows = [nc.dram_tensor(f"y_rows{u}", [PAIRS, P], F32).ap() for u in range(UNITS)]

        state = [sb(f"state{b}", [P, TOKENS]) for b in range(IMAGES)]
        tok = [sb(f"tok{b}", [P, BLOCKS, P]) for b in range(IMAGES)]
        work = [sb(f"work{i}", [P, TOKENS]) for i in range(3)]
        work_tok = [w[:].rearrange("p (t c) -> p t c", t=BLOCKS) for w in work]

        ident = sb("ident", [P, P])
        ones = sb("ones", [P, P], BF16)
        before = sb("before", [P, P], BF16)
        spread = sb("spread", [P, IMAGES, IMAGES, P])
        lane = sb("lane", [P, P], BF16)
        block_no = sb("block_no", [P, TILES * HALVES], BF16)
        tile_no = sb("tile_no", [P, TILES])
        expert_no = sb("expert_no", [P, EXPERTS])
        rank_no = sb("rank_no", [P, EXPERTS])
        resets = sb("resets", [P, EXPERTS, BLOCKS])
        row_hi = sb("row_hi", [P, CHOICES])
        row_lo = sb("row_lo", [P, BLOCKS])
        step_no = sb("step_no", [P, KERNELS])
        conv_w = sb("conv_w", [P, 2, SIDE])
        gamma = sb("gamma", [P, 2])
        beta = sb("beta", [P, 2])
        lw1 = sb("lw1", [P, 2, P])
        lw2 = sb("lw2", [P, 2, P])
        lw1T = sb("lw1T", [P, 2, P])
        lw2T = sb("lw2T", [P, 2, P])
        lb1 = sb("lb1", [P, 2])
        lb2 = sb("lb2", [P, 1])
        router = sb("router", [EXPERTS, 2, P])
        gate_w = sb("gate_w", [P, EXPERTS])
        router_sum = sb("router_sum", [EXPERTS, 2])
        routerT = sb("routerT", [P, 2, EXPERTS])
        router_b = sb("router_b", [P, 2, EXPERTS])
        bias = [sb(f"bias{l}", [P, BIAS, EXPERTS]) for l in range(2)]
        bias1 = [sb(f"bias1_{l}", [P, EXPERTS, CHUNKS]) for l in range(2)]
        bias2 = [sb(f"bias2_{l}", [EXPERTS, P]) for l in range(2)]
        mix_w1 = sb("mix_w1", [EXPERTS, P])
        mix_w1T = sb("mix_w1T", [P, EXPERTS])
        mix_w2 = sb("mix_w2", [P, EXPERTS])
        mix_w2T = sb("mix_w2T", [EXPERTS, P])
        mix_b1 = sb("mix_b1", [EXPERTS, 1])
        mix_b2 = sb("mix_b2", [P, 1])

        stats = sb("stats", [P, BLOCKS, 6])
        mean = sb("mean", [P, BLOCKS])
        rstd = sb("rstd", [P, BLOCKS])
        var = sb("var", [P, BLOCKS])
        tmp_s = sb("tmp_s", [P, BLOCKS])
        lines = sb("lines", [P, 2, IMAGES, SIDE])
        line_mul = sb("line_mul", [P, 2])
        line_add = sb("line_add", [P, 2])
        dots = sb("dots", [P, IMAGES])
        gates = sb("gates", [P, 5, IMAGES])
        soft = sb("soft", [IMAGES, 3, P])
        soft_s = sb("soft_s", [IMAGES, 4])
        hid = sb("hid", [P, 2, IMAGES])
        z = sb("z", [P, BLOCKS, EXPERTS])
        za = sb("za", [P, BLOCKS, EXPERTS])
        zb = sb("zb", [P, BLOCKS, EXPERTS])
        prob = sb("prob", [P, BLOCKS, EXPERTS])
        top = sb("top", [P, 4, BLOCKS])
        chosen = sb("chosen", [P, CHOICES, EXPERTS, BLOCKS])
        chosen_any = sb("chosen_any", [P, EXPERTS, BLOCKS], BF16)
        share = [sb(f"share{b}", [P, CHOICES, BLOCKS]) for b in range(IMAGES)]
        prefix = sb("prefix", [P, EXPERTS, BLOCKS])
        upto = sb("upto", [P, EXPERTS, BLOCKS])
        total = sb("total", [P, EXPERTS, BLOCKS])
        n_tiles = sb("n_tiles", [P, 4, EXPERTS])
        n_tiles_i = sb("n_tiles_i", [P, EXPERTS], I32)
        place = sb("place", [P, 3, BLOCKS])
        place_i = sb("place_i", [P, 3, BLOCKS], I32)
        hot_lane = sb("hot_lane", [P, BLOCKS, P], BF16)
        hot_block = sb("hot_block", [P, BLOCKS, 2, TILES * HALVES], BF16)
        tile_cmp = sb("tile_cmp", [P, TILES, EXPERTS])
        tile_e = sb("tile_e", [P, TILES])
        rows_f = sb("rows_f", [P, 4, TILES * HALVES])
        bias_mul = sb("bias_mul", [P, TILES, BIAS, EXPERTS])
        tile_expert = [sb(f"tile_expert{i}", [P, TILES], I32) for i in range(2)]
        tile_rows = [sb(f"tile_rows{i}", [P, TILES, 2, HALVES]) for i in range(2)]
        tile_bias = [sb(f"tile_bias{i}", [P, TILES, BIAS]) for i in range(2)]
        gap = sb("gap", [P, 1])
        mix_h = sb("mix_h", [EXPERTS, 1])
        mix_s = sb("mix_s", [P, 4])
        mix_hot = sb("mix_hot", [P, 3, KERNELS])

        g_slot = sb("g_slot", [P, RING, HALVES], U32)
        s_slot = sb("s_slot", [P, RING, HALVES], U32)
        b_slot = sb("b_slot", [P, 2, BIAS])
        xg = sb("xg", [P, RING, HALVES, P])
        xT = sb("xT", [P, 2, SLOTS])
        w1s = sb("w1s", [P, RING, HIDDEN])
        w2s = sb("w2s", [P, RING, CHUNKS, P])
        hT = sb("hT", [P, 2, CHUNKS, SLOTS])
        yT = sb("yT", [P, 2, SLOTS])
        yr = sb("yr", [P, RING, HALVES, P])

        xT_ps = ps("xT_ps", [P, 512])
        h_ps = [ps(f"h_ps{i}", [P, 2, SLOTS]) for i in range(2)]
        yT_ps = ps("yT_ps", [P, 512])
        yr_ps = ps("yr_ps", [P, 4, P])
        turn_ps = ps("turn_ps", [P, 2, 512])
        acc_ps = ps("acc_ps", [P, 512])

        s_par = sem("params_loaded")
        s_x = [[sem(f"image{b}_part{q}_loaded") for q in range(2)] for b in range(IMAGES)]
        s_const = sem("constants_made")
        s_own = sem("vector_steps")
        s_own_a = sem("scalar_steps")
        s_turned = sem("turn_bank_filled")
        s_freed = sem("turn_bank_freed")
        s_acc = sem("acc_bank_filled")
        s_acc_free = sem("acc_bank_freed")
        s_ready = sem("vector_result_for_tensor")
        s_ln = sem("normalised_group_for_tensor")
        s_state = sem("state_for_tensor")
        s_exp_in = sem("exp_input_ready")
        s_exp = sem("exp_done")
        s_xn = sem("normalised_rows_ready")
        s_xn_st = [sem(f"normalised_rows_stored{u}") for u in range(UNITS)]
        s_table = sem("tile_tables_ready")
        s_hot = sem("one_hots_ready")
        s_hot_used = sem("one_hots_used")
        s_g_idx = sem("gather_rows_set")
        s_gath = [sem(f"gathered{i}") for i in range(RING)]
        s_w = [sem(f"weights_loaded{i}") for i in range(RING)]
        s_xt_ps = sem("x_turned")
        s_xt_sb = sem("x_turned_copied")
        s_h_ps = sem("hidden_made")
        s_h_sb = sem("hidden_activated")
        s_y_ps = sem("expert_out_made")
        s_y_sb = sem("expert_out_copied")
        s_yr_ps = sem("out_rows_turned")
        s_yr_sb = sem("out_rows_copied")
        s_scat = [sem(f"scattered{i}") for i in range(RING)]
        s_begun = sem("indirect_dmas_begun")
        s_buf = sem("work_buffers_free")
        s_y_in = [sem(f"expert_rows_loaded{u}") for u in range(UNITS)]
        s_out = sem("image_out_ready")
        s_done = sem("output_stored")

        W1 = [L0_ffn_W1, L1_ffn_w1]
        W2 = [L0_ffn_W2, L1_ffn_w2]

        small = [
            (conv_w[:, 0, :], L0_conv_w1.rearrange("c a h b -> c (a h b)")),
            (conv_w[:, 1, :], L0_conv_w2.rearrange("c a b w -> c (a b w)")),
            (gamma[:, 0:1], L0_conv_g1.rearrange("(c a) -> c a", a=1)),
            (gamma[:, 1:2], L0_conv_g2.rearrange("(c a) -> c a", a=1)),
            (beta[:, 0:1], L0_conv_b1.rearrange("(c a) -> c a", a=1)),
            (beta[:, 1:2], L0_conv_b2.rearrange("(c a) -> c a", a=1)),
            (lw1[:, 0, :], L0_conv_lw1[0:P, :]),
            (lw1[:, 1, :], L0_conv_lw1[P:2 * P, :]),
            (lw2[:, :, :], L0_conv_lw2.rearrange("c (a j) -> c a j", a=2)),
            (lb1[:, 0:1], L0_conv_lb1[0:P].rearrange("(c a) -> c a", a=1)),
            (lb1[:, 1:2], L0_conv_lb1[P:2 * P].rearrange("(c a) -> c a", a=1)),
            (lb2[:, :], L0_conv_lb2.rearrange("(c a) -> c a", a=1)),
            (router[:, 0, :], L0_ffn_Wr),
            (gate_w[:, :], L1_ffn_gate_w),
            (router_b[:, 0, :], L0_ffn_br.partition_broadcast(P)),
            (router_b[:, 1, :], L1_ffn_gate_b.partition_broadcast(P)),
            (bias1[0][:, :, :], L0_ffn_b1.rearrange("e (p c) -> p e c", c=CHUNKS)),
            (bias1[1][:, :, :], L1_ffn_b1.rearrange("e (p c) -> p e c", c=CHUNKS)),
            (bias2[0][:, :], L0_ffn_b2),
            (bias2[1][:, :], L1_ffn_b2),
            (mix_w1[:, :], L1_conv_w1),
            (mix_w2[:, :], L1_conv_w2),
            (mix_b1[:, :], L1_conv_b1.rearrange("(c a) -> c a", a=1)),
            (mix_b2[:, :], L1_conv_b2.rearrange("(c a) -> c a", a=1)),
        ]
        CONSTS = 14

        block = ctx.enter_context(nc.Block())

        @block.sync
        def _(sp):
            def load_weights(t, d):
                layer, i = divmod(t.unit, IMAGES)
                if t.old(d - RING):
                    sp.wait_ge(s_y_ps, t.done(d - RING))
                e = sp.value_load(tile_expert[i][0:1, bass.ds(t.j(d), 1)], min_val=0, max_val=EXPERTS - 1)
                s = t.slot(RING, d)
                sp.dma_start(w1s[:, s, :], W1[layer][bass.ds(e, 1)].rearrange("a d f -> (a d) f")) \
                    .then_inc(s_w[s], 16)
                sp.dma_start(w2s[:, s, :, :], W2[layer][bass.ds(e, 1)].rearrange("a (p c) d -> (a p) c d", c=CHUNKS)) \
                    .then_inc(s_w[s], 16)

            def store_normalised(u):
                sp.wait_ge(s_xn, u + 1)
                sp.dma_start(xn_rows[u].rearrange("(p t) c -> p t c", t=BLOCKS), work_tok[0]) \
                    .then_inc(s_xn_st[u], 16)

            def weights(u):
                sp.wait_ge(s_table, u + 1)
                for d in range(AHEAD - 1):
                    load_weights(Tile(u, 0), d)

                def step(t):
                    if t.has(AHEAD - 1):
                        load_weights(t, AHEAD - 1)
                tile_steps(sp, u, step)

            def load_outputs(u):
                last = Tile(u, TILES - 1)
                for d in range(RING):
                    sp.wait_ge(s_scat[last.slot(RING, -d)], last.landed(-d, HALVES))
                sp.wait_ge(s_buf, u + 1)
                for k in range(CHOICES):
                    sp.dma_start(work_tok[1 + k], y_rows[u].rearrange("(k p t) c -> k p t c", k=CHOICES, t=BLOCKS)[k]) \
                        .then_inc(s_y_in[u], 16)

            for b in range(IMAGES):
                for q in range(2):
                    h = TOKENS // 2
                    sp.dma_start(state[b][:, q * h:(q + 1) * h],
                                 x[b].rearrange("c h w -> c (h w)")[:, q * h:(q + 1) * h]).then_inc(s_x[b][q], 16)
                if b == 0:
                    for to, source in small:
                        sp.dma_start(to, source).then_inc(s_par, 16)
            for layer in range(2):
                for b in range(IMAGES):
                    store_normalised(2 * layer + b)
                for b in range(IMAGES):
                    weights(2 * layer + b)
                for b in range(IMAGES):
                    load_outputs(2 * layer + b)
                    if layer:
                        sp.wait_ge(s_out, b + 1)
                        sp.dma_start(out[b].rearrange("c h w -> c (h w)"), state[b][:]).then_inc(s_done, 16)
            sp.wait_ge(s_done, 16 * IMAGES)

        @block.gpsimd
        def _(pool):
            big = dict(allow_small_or_imprecise_dtypes=True)
            pool.memset(ident[:], 0.0).then_inc(s_const, 1)
            pool.memset(ones[:], 1.0).then_inc(s_const, 1)
            pool.memset(spread[:], 0.0).then_inc(s_const, 1)
            pool.memset(resets[:], 1.0).then_inc(s_const, 1)
            pool.wait_ge(s_const, 4)
            pool.affine_select(out=ident[:], in_=ident[:], compare_op=ALU.not_equal, fill=1.0, base=0,
                               pattern=[[-1, P]], channel_multiplier=1).then_inc(s_const, 1)
            pool.affine_select(out=before[:], in_=ones[:], compare_op=ALU.is_ge, fill=0.0, base=-1,
                               pattern=[[1, P]], channel_multiplier=-1).then_inc(s_const, 1)
            pool.affine_select(out=spread[:], in_=spread[:], compare_op=ALU.not_equal, fill=1.0, base=0,
                               pattern=[[P, IMAGES], [-1, IMAGES], [1, P]], channel_multiplier=-2).then_inc(s_const, 1)
            pool.memset(resets[:, :, 0:1], 0.0).then_inc(s_const, 1)
            pool.iota(lane[:], [[1, P]], base=0, channel_multiplier=0, **big).then_inc(s_const, 1)
            pool.iota(block_no[:], [[1, TILES * HALVES]], base=0, channel_multiplier=0, **big).then_inc(s_const, 1)
            pool.iota(tile_no[:], [[1, TILES]], base=0, channel_multiplier=0, **big).then_inc(s_const, 1)
            pool.iota(row_hi[:], [[TOKENS, CHOICES]], base=0, channel_multiplier=BLOCKS, **big).then_inc(s_const, 1)
            pool.iota(row_lo[:], [[1, BLOCKS]], base=1, channel_multiplier=0, **big).then_inc(s_const, 1)
            pool.iota(rank_no[:], [[-1, EXPERTS]], base=EXPERTS, channel_multiplier=0, **big).then_inc(s_const, 1)
            pool.iota(expert_no[:], [[1, EXPERTS]], base=0, channel_multiplier=0, **big).then_inc(s_const, 1)
            pool.iota(step_no[:], [[1, KERNELS]], base=0, channel_multiplier=0, **big).then_inc(s_const, 1)

            def gather(t, d):
                s = t.slot(RING, d)
                pool.wait_ge(s_g_idx, t.done(d))
                pool.sem_inc(s_begun, 1)
                for h in range(HALVES):
                    pool.indirect_dma_start(xg[:, s, h, :], None, xn_rows[t.unit],
                                            bass.IndirectOffsetOnAxis(ap=g_slot[:, s, h:h + 1], axis=0)) \
                        .then_inc(s_gath[s], 16)

            def scatter(t, d):
                s = t.slot(RING, d)
                pool.wait_ge(s_yr_sb, t.done(d))
                pool.sem_inc(s_begun, 1)
                for h in range(HALVES):
                    pool.indirect_dma_start(y_rows[t.unit], bass.IndirectOffsetOnAxis(ap=s_slot[:, s, h:h + 1], axis=0),
                                            yr[:, s, h, :], None, bounds_check=PAIRS - 1, oob_is_err=False) \
                        .then_inc(s_scat[s], 16)

            for u in range(UNITS):
                pool.wait_ge(s_xn_st[u], 16)
                for d in range(AHEAD - 1):
                    gather(Tile(u, 0), d)

                def step(t):
                    if t.has(AHEAD - 1):
                        gather(t, AHEAD - 1)
                    if t.has(-2):
                        scatter(t, -2)
                tile_steps(pool, u, step)

        @block.scalar
        def _(act):
            own = Count(s_own_a, act)

            def set_gather(t, d):
                act.activation(g_slot[:, t.slot(RING, d), :], tile_rows[t.unit % 2][:, bass.ds(t.j(d), 1), 0, :]
                               .rearrange("p a h -> p (a h)"), ACT.Copy).then_inc(s_g_idx, 1)

            def copy_x(t, d):
                act.wait_ge(s_xt_ps, t.done(d))
                if t.old(d - 2):
                    act.wait_ge(s_h_ps, t.done(d - 2, 2))
                act.activation(xT[:, t.slot(2, d), :], xT_ps[:, 0:SLOTS], ACT.Copy).then_inc(s_xt_sb, 1)

            def activate(t):
                s = t.slot(2)
                if t.old(-2):
                    act.wait_ge(s_y_sb, t.done(-2))
                own.step(act.activation(b_slot[:, s, :], tile_bias[t.unit % 2][:, bass.ds(t.j(), 1), :]
                                        .rearrange("p a n -> p (a n)"), ACT.Copy))
                act.wait_ge(s_own_a, own_value(t))
                func = ACT.Gelu if t.unit // IMAGES else ACT.Gelu_apprx_tanh
                for c in range(CHUNKS):
                    if c % 2 == 0:
                        act.wait_ge(s_h_ps, t.done(0, 2, c // 2 + 1))
                    ins = act.activation(hT[:, s, c, :], h_ps[c // 2][:, c % 2, :], func, bias=b_slot[:, s, c:c + 1])
                    if c % 2:
                        ins.then_inc(s_h_sb, 1)

            def copy_y(t, d):
                s = t.slot(2, d)
                act.wait_ge(s_y_ps, t.done(d))
                if t.old(d - 2):
                    act.wait_ge(s_yr_ps, t.done(d - 2))
                act.activation(yT[:, s, :], yT_ps[:, 0:SLOTS], ACT.Identity, bias=b_slot[:, s, CHUNKS:BIAS]) \
                    .then_inc(s_y_sb, 1)

            def copy_rows(t, d):
                s = t.slot(RING, d)
                if t.old(d - RING):
                    act.wait_ge(s_scat[s], t.landed(d - RING, HALVES))
                act.activation(s_slot[:, s, :], tile_rows[t.unit % 2][:, bass.ds(t.j(d), 1), 1, :]
                               .rearrange("p a h -> p (a h)"), ACT.Copy)
                act.wait_ge(s_yr_ps, t.done(d))
                act.activation(yr[:, s, :, :], yr_ps[:, 0:HALVES, :], ACT.Copy).then_inc(s_yr_sb, 1)

            base = [0]

            def own_value(t):
                return t.done() + base[0]

            def tiles(u):
                act.wait_ge(s_table, u + 1)
                base[0] = own.n - u * TILES
                for d in range(AHEAD):
                    if Tile(u, 0).old(d - RING):
                        pass
                    set_gather(Tile(u, 0), d)
                first = Tile(u, 0)
                copy_x(first, 0)

                def step(t):
                    if t.has(AHEAD):
                        set_gather(t, AHEAD)
                    if t.has(1):
                        copy_x(t, 1)
                    if t.has(0):
                        activate(t)
                    if t.has(-1):
                        copy_y(t, -1)
                    if t.has(-2):
                        copy_rows(t, -2)
                n = own.n
                tile_steps(act, u, step)
                own.n = n + TILES

            act.wait_ge(s_exp_in, 1)
            act.activation(soft[:, 1, :], soft[:, 0, :], ACT.Exp, bias=soft_s[:, 1:2], accum_out=soft_s[:, 2:3]) \
                .then_inc(s_exp, 1)
            for layer in range(2):
                for b in range(IMAGES):
                    act.wait_ge(s_exp_in, 2 + 2 * layer + b)
                    act.activation(prob[:], za[:], ACT.Exp).then_inc(s_exp, 1)
                for b in range(IMAGES):
                    tiles(2 * layer + b)

        @block.tensor
        def _(pe):
            turn = Count(s_freed, pe)
            acc = Count(s_acc_free, pe)

            def use():
                n = turn.n
                turn.n += 1
                pe.wait_ge(s_freed, n + 1)
                return turn_ps[:, n % 2, :]

            def turn_blocks(source, group, to_tokens=True):
                bank = use()
                for k in range(GROUP):
                    t = group * GROUP + k
                    mm = pe.transpose(bank[:, k * P:(k + 1) * P], source(t), ident[:])
                mm.then_inc(s_turned, 1)

            def channel(b):
                return lambda t: state[b][:, t * P:(t + 1) * P]

            def router_products(b, layer, group):
                for k in range(GROUP):
                    t = group * GROUP + k
                    mm = pe.matmul(acc_ps[:, t * EXPERTS:(t + 1) * EXPERTS], channel(b)(t), routerT[:, layer, :],
                                   start=True, stop=True)
                return mm

            def route(u):
                layer, b = divmod(u, IMAGES)
                pe.wait_ge(s_state, u + 1)
                pe.wait_ge(s_acc_free, 2 * u + 1)
                for g in range(GROUPS):
                    turn_blocks(channel(b), g)
                    mm = router_products(b, layer, g)
                mm.then_inc(s_acc, 1)
                wait_ready()
                for lhs in (before, ones):
                    bank = use()
                    pe.matmul(bank[:, 0:EXPERTS * BLOCKS], lhs[:], chosen_any[:].rearrange("p e t -> p (e t)"),
                              start=True, stop=True).then_inc(s_turned, 1)
                pe.wait_ge(s_acc_free, 2 * u + 2)
                n = TILES * HALVES
                for k in range(CHOICES):
                    pe.wait_ge(s_hot, u * CHOICES + k + 1)
                    for t in range(BLOCKS):
                        mm = pe.matmul(acc_ps[:, 0:2 * n], hot_lane[:, t, :], hot_block[:, t, :, :]
                                       .rearrange("p a q -> p (a q)"), start=(k == 0 and t == 0),
                                       stop=(k == CHOICES - 1 and t == BLOCKS - 1))
                    mm.then_inc(s_hot_used, 1)

            ready = [0]

            def wait_ready():
                ready[0] += 1
                pe.wait_ge(s_ready, ready[0])

            def turn_x(t, d):
                pe.wait_ge(s_gath[t.slot(RING, d)], t.landed(d, HALVES))
                if t.old(d - 1):
                    pe.wait_ge(s_xt_sb, t.done(d - 1))
                for h in range(HALVES):
                    mm = pe.transpose(xT_ps[:, h * P:(h + 1) * P], xg[:, t.slot(RING, d), h, :], ident[:])
                mm.then_inc(s_xt_ps, 1)

            def up(t):
                pe.wait_ge(s_xt_sb, t.done())
                pe.wait_ge(s_w[t.slot(RING)], t.landed(0, 2))
                for c in range(CHUNKS):
                    if c % 2 == 0 and t.old(-1):
                        pe.wait_ge(s_h_sb, t.done(-1, 2, c // 2 + 1))
                    mm = pe.matmul(h_ps[c // 2][:, c % 2, :], w1s[:, t.slot(RING), c:HIDDEN:CHUNKS],
                                   xT[:, t.slot(2), :], start=True, stop=True)
                    if c % 2:
                        mm.then_inc(s_h_ps, 1)

            def down(t, d):
                s = t.slot(2, d)
                if t.old(d - 1):
                    pe.wait_ge(s_y_sb, t.done(d - 1))
                for c in range(CHUNKS):
                    if c % 2 == 0:
                        pe.wait_ge(s_h_sb, t.done(d, 2, c // 2 + 1))
                    mm = pe.matmul(yT_ps[:, 0:SLOTS], w2s[:, t.slot(RING, d), c, :], hT[:, s, c, :],
                                   start=(c == 0), stop=(c == CHUNKS - 1))
                mm.then_inc(s_y_ps, 1)

            def turn_y(t, d):
                s = t.slot(2, d)
                pe.wait_ge(s_y_sb, t.done(d))
                if t.old(d - 1):
                    pe.wait_ge(s_yr_sb, t.done(d - 1))
                for h in range(HALVES):
                    mm = pe.transpose(yr_ps[:, h, :], yT[:, s, h * P:(h + 1) * P], ident[:])
                mm.then_inc(s_yr_ps, 1)

            def tiles(u):
                turn_x(Tile(u, 0), 0)

                def step(t):
                    if t.has(1):
                        turn_x(t, 1)
                    if t.has(0):
                        up(t)
                    if t.has(-1):
                        down(t, -1)
                    if t.has(-2):
                        turn_y(t, -2)
                tile_steps(pe, u, step)

            pe.wait_ge(s_const, CONSTS + 2)
            pe.wait_ge(s_par, 16 * len(small))
            bank = use()
            for j in range(2):
                pe.transpose(bank[:, j * P:(j + 1) * P], lw1[:, j, :], ident[:])
                mm = pe.transpose(bank[:, (2 + j) * P:(3 + j) * P], lw2[:, j, :], ident[:])
            mm.then_inc(s_turned, 1)
            bank = use()
            pe.transpose(bank[0:EXPERTS, 0:P], gate_w[:], ident[:])
            pe.transpose(bank[:, P:P + EXPERTS], mix_w1[:], ident[0:EXPERTS, 0:EXPERTS])
            pe.transpose(bank[0:EXPERTS, 2 * P:3 * P], mix_w2[:], ident[:])
            pe.transpose(bank[:, 3 * P:3 * P + EXPERTS], bias2[0][:], ident[0:EXPERTS, 0:EXPERTS])
            pe.transpose(bank[:, 3 * P + EXPERTS:3 * P + 2 * EXPERTS], bias2[1][:], ident[0:EXPERTS, 0:EXPERTS]) \
                .then_inc(s_turned, 1)
            wait_ready()
            bank = use()
            for layer in range(2):
                mm = pe.transpose(bank[:, layer * EXPERTS:(layer + 1) * EXPERTS], router[:, layer, :],
                                  ident[0:EXPERTS, 0:EXPERTS])
            mm.then_inc(s_turned, 1)

            ln = [0]

            def turn_back(source, groups=range(GROUPS)):
                for g in groups:
                    ln[0] += 1
                    pe.wait_ge(s_ln, ln[0])
                    turn_blocks(source, g)

            for b in range(IMAGES):
                for g in range(GROUPS):
                    if g % (GROUPS // 2) == 0:
                        pe.wait_ge(s_x[b][g // (GROUPS // 2)], 16)
                    turn_blocks(channel(b), g)
                turn_back(lambda t: tok[b][:, t, :])
            wait_ready()
            bank = use()
            for row in range(IMAGES):
                for b in range(IMAGES):
                    mm = pe.matmul(bank[:, row:row + 1], spread[:, row, b, :], dots[:, b:b + 1],
                                   start=(b == 0), stop=(b == IMAGES - 1))
            mm.then_inc(s_turned, 1)
            wait_ready()
            bank = use()
            for j in range(2):
                mm = pe.matmul(bank[:, j * IMAGES:(j + 1) * IMAGES], lw1T[:, j, :], gates[:, 0, :], start=True, stop=True)
            mm.then_inc(s_turned, 1)
            wait_ready()
            bank = use()
            for j in range(2):
                mm = pe.matmul(bank[:, 0:IMAGES], lw2T[:, j, :], hid[:, j, :], start=(j == 0), stop=(j == 1))
            mm.then_inc(s_turned, 1)
            wait_ready()
            bank = use()
            pe.transpose(bank[0:IMAGES, 0:P], gates[:, 1, :], ident[:]).then_inc(s_turned, 1)
            wait_ready()
            bank = use()
            pe.transpose(bank[:, 0:IMAGES], soft[:, 2, :], ident[0:IMAGES, 0:IMAGES]).then_inc(s_turned, 1)

            for b in range(IMAGES):
                route(b)
            for b in range(IMAGES):
                tiles(b)
            for b in range(IMAGES):
                turn_back(lambda t: work_tok[0][:, t, :])
                turn_back(lambda t: tok[b][:, t, :])
                wait_ready()
                bank = use()
                pe.matmul(bank[0:EXPERTS, 0:1], mix_w1T[:], gap[:], start=True, stop=True).then_inc(s_turned, 1)
                wait_ready()
                bank = use()
                pe.matmul(bank[:, 0:1], mix_w2T[:], mix_h[:], start=True, stop=True).then_inc(s_turned, 1)
            for b in range(IMAGES):
                route(2 + b)
            for b in range(IMAGES):
                tiles(2 + b)
            for b in range(IMAGES):
                turn_back(lambda t: tok[b][:, t, :])

        @block.vector
        def _(dve):
            own = Count(s_own, dve)
            turned = Count(s_turned, dve)

            def op(ins):
                own.step(ins)
                own.wait()

            def read(n=None):
                bank = turned.n % 2
                turned.step()
                turned.wait()
                return turn_ps[:, bank, :]

            def rsqrt(v, y, tmp):
                op(dve.tensor_scalar(tmp.bitcast(I32), v.bitcast(I32), 1, None, ALU.logical_shift_right))
                op(dve.tensor_scalar(y.bitcast(I32), tmp.bitcast(I32), -1.0, float(0x5F3759DF), ALU.mult, ALU.add))
                for _ in range(3):
                    op(dve.tensor_tensor(tmp, y, y, ALU.mult))
                    op(dve.scalar_tensor_tensor(tmp, tmp, -0.5, v, ALU.mult, ALU.mult))
                    op(dve.scalar_tensor_tensor(y, tmp, 1.5, y, ALU.add, ALU.mult))

            def moments(st, n, m, v, tmp, eps):
                op(dve.tensor_tensor(tmp, st[:, :, 1], st[:, :, 4], ALU.subtract))
                op(dve.tensor_tensor(m, st[:, :, 1], st[:, :, 4], ALU.add))
                op(dve.tensor_scalar(m, m, 0.5, None, ALU.mult))
                op(dve.scalar_tensor_tensor(tmp, tmp, 0.25, tmp, ALU.mult, ALU.mult))
                op(dve.tensor_tensor(v, st[:, :, 2], st[:, :, 5], ALU.add))
                op(dve.scalar_tensor_tensor(v, v, 1.0 / (2 * n), tmp, ALU.mult, ALU.add))
                op(dve.tensor_scalar(v, v, eps, None, ALU.add))

            def token_stats(eps):
                moments(stats[:], P // 2, mean[:], var[:], tmp_s[:], eps)
                rsqrt(var[:], rstd[:], tmp_s[:])

            def to_tokens(b):
                with rounds(dve, GROUPS // 2, (turned, 2)) as i:
                    for k in range(2):
                        bank = read()
                        at = i * (2 * GROUP) + k * GROUP
                        dve.tensor_copy(tok[b][:, bass.ds(at, GROUP), :], bank.rearrange("p (t c) -> p t c", t=GROUP))
                        for g in range(GROUP):
                            ins = dve.bn_stats(stats[:, bass.ds(at + g, 1), :].rearrange("p a s -> p (a s)"),
                                               bank[:, g * P:(g + 1) * P])
                        ins.then_inc(s_freed, 1)
                dve.wait_ge(s_freed, 2 + turned.n)

            def to_channels(dst):
                with rounds(dve, GROUPS // 2, (turned, 2)) as i:
                    for k in range(2):
                        bank = read()
                        dve.tensor_copy(dst[:, bass.ds(i * 1024 + k * 512, 512)], bank).then_inc(s_freed, 1)
                dve.wait_ge(s_freed, 2 + turned.n)

            def normalise(src, dst, signal):
                with rounds(dve, GROUPS, (own, 0 if signal else 1)) as i:
                    for g in range(GROUP):
                        at = i * GROUP + g
                        ins = dve.tensor_scalar(dst[:, bass.ds(at, 1), :].rearrange("p a c -> p (a c)"),
                                                src[:, bass.ds(at, 1), :].rearrange("p a c -> p (a c)"),
                                                mean[:, bass.ds(at, 1)], rstd[:, bass.ds(at, 1)],
                                                ALU.subtract, ALU.mult)
                    if signal:
                        ins.then_inc(s_ln, 1)
                    else:
                        own.step(ins)
                if not signal:
                    own.wait()

            def bc(ap, shape):
                return ap.to_broadcast(shape)

            dve.sem_inc(s_freed, 2)
            dve.sem_inc(s_acc_free, 1)
            dve.wait_ge(s_const, CONSTS + 2)
            dve.wait_ge(s_par, 16 * len(small))
            bank = read()
            dve.tensor_copy(lw1T[:].rearrange("p a j -> p (a j)"), bank[:, 0:2 * P])
            dve.tensor_copy(lw2T[:].rearrange("p a j -> p (a j)"), bank[:, 2 * P:4 * P]).then_inc(s_freed, 1)
            bank = read()
            dve.tensor_copy(router[:, 1, :], bank[0:EXPERTS, 0:P])
            dve.tensor_copy(mix_w1T[:], bank[:, P:P + EXPERTS])
            dve.tensor_copy(mix_w2T[:], bank[0:EXPERTS, 2 * P:3 * P])
            for layer in range(2):
                at = 3 * P + layer * EXPERTS
                op(dve.tensor_copy(bias[layer][:, CHUNKS, :], bank[:, at:at + EXPERTS]))
            for layer in range(2):
                ins = dve.tensor_copy(bias[layer][:, 0:CHUNKS, :], bias1[layer][:].rearrange("p e c -> p c e"))
            ins.then_inc(s_freed, 1)
            op(dve.tensor_reduce(router_sum[:], router[:], AX.X, ALU.add))
            op(dve.tensor_scalar(router_sum[:], router_sum[:], -1.0 / P, None, ALU.mult))
            dve.tensor_scalar(router[:, 0, :], router[:, 0, :], router_sum[:, 0:1], None, ALU.add)
            dve.tensor_scalar(router[:, 1, :], router[:, 1, :], router_sum[:, 1:2], None, ALU.add).then_inc(s_ready, 1)
            bank = read()
            dve.tensor_copy(routerT[:].rearrange("p l e -> p (l e)"), bank[:, 0:2 * EXPERTS]).then_inc(s_freed, 1)

            for b in range(IMAGES):
                to_tokens(b)
                token_stats(1e-6)
                normalise(tok[b], tok[b], True)
                to_channels(work[b])
                img = work[b][:].rearrange("p (h w) -> p h w", h=SIDE)
                mul = work[2][:].rearrange("p (h w) -> p h w", h=SIDE)
                op(dve.tensor_tensor(mul, img, bc(conv_w[:, 0, :].unsqueeze(2), [P, SIDE, SIDE]), ALU.mult))
                op(dve.tensor_reduce(lines[:, 0, b, :], mul.rearrange("p h w -> p w h"), AX.X, ALU.add))
                op(dve.tensor_tensor(mul, img, bc(conv_w[:, 1, :].unsqueeze(1), [P, SIDE, SIDE]), ALU.mult))
                op(dve.tensor_reduce(lines[:, 1, b, :], mul, AX.X, ALU.add))
            for k in range(2):
                op(dve.bn_stats(stats[:, k, :], lines[:, k, :, :].rearrange("p b s -> p (b s)")))
            moments(stats[:, 0:2, :], SIDE, mean[:, 0:2], var[:, 0:2], tmp_s[:, 0:2], 1e-5)
            rsqrt(var[:, 0:2], rstd[:, 0:2], tmp_s[:, 0:2])
            op(dve.tensor_tensor(line_mul[:], gamma[:], rstd[:, 0:2], ALU.mult))
            op(dve.tensor_tensor(line_add[:], mean[:, 0:2], line_mul[:], ALU.mult))
            op(dve.tensor_tensor(line_add[:], beta[:], line_add[:], ALU.subtract))
            for k in range(2):
                line = lines[:, k, :, :].rearrange("p b s -> p (b s)")
                op(dve.tensor_scalar(line, line, line_mul[:, k:k + 1], line_add[:, k:k + 1], ALU.mult, ALU.add))
                op(dve.tensor_scalar(line, line, 0.0, None, ALU.max))
            op(dve.tensor_tensor(lines[:, 0, :, :], lines[:, 0, :, :], lines[:, 1, :, :], ALU.mult))
            dve.tensor_reduce(dots[:], lines[:, 0, :, :], AX.X, ALU.add).then_inc(s_ready, 1)
            bank = read()
            op(dve.tensor_copy(gates[:, 0, :], bank[:, 0:IMAGES]))
            dve.sem_inc(s_freed, 1)
            dve.sem_inc(s_ready, 1)
            bank = read()
            op(dve.tensor_tensor(hid[:], bank[:, 0:2 * IMAGES].rearrange("p (a b) -> p a b", a=2),
                                 bc(lb1[:].unsqueeze(2), [P, 2, IMAGES]), ALU.add))
            dve.sem_inc(s_ready, 1)
            dve.sem_inc(s_freed, 1)
            bank = read()
            op(dve.tensor_scalar(gates[:, 1, :], bank[:, 0:IMAGES], lb2[:], None, ALU.add))
            dve.sem_inc(s_ready, 1)
            dve.sem_inc(s_freed, 1)
            bank = read()
            op(dve.tensor_copy(soft[:, 0, :], bank[0:IMAGES, 0:P]))
            op(dve.tensor_reduce(soft_s[:, 0:1], soft[:, 0, :], AX.X, ALU.max))
            dve.tensor_scalar(soft_s[:, 1:2], soft_s[:, 0:1], -1.0, None, ALU.mult).then_inc(s_exp_in, 1)
            dve.wait_ge(s_exp, 1)
            op(dve.reciprocal(soft_s[:, 3:4], soft_s[:, 2:3]))
            op(dve.tensor_scalar(soft[:, 2, :], soft[:, 1, :], soft_s[:, 3:4], None, ALU.mult))
            dve.sem_inc(s_ready, 1)
            dve.sem_inc(s_freed, 1)
            bank = read()
            op(dve.tensor_copy(gates[:, 2, :], bank[:, 0:IMAGES]))
            dve.sem_inc(s_freed, 1)
            for b in range(IMAGES):
                dve.scalar_tensor_tensor(state[b][:], work[b][:], gates[:, 2, b:b + 1], state[b][:],
                                         ALU.mult, ALU.add).then_inc(s_state, 1)

            def one_hot_top(src, k):
                op(dve.tensor_reduce(top[:, 1, :], src[:], AX.X, ALU.max))
                op(dve.tensor_tensor(zb[:], src[:], bc(top[:, 1, :].unsqueeze(2), [P, BLOCKS, EXPERTS]), ALU.is_ge))
                op(dve.tensor_tensor(zb[:], zb[:], bc(rank_no[:].unsqueeze(1), [P, BLOCKS, EXPERTS]), ALU.mult))
                op(dve.tensor_reduce(top[:, 1, :], zb[:], AX.X, ALU.max))
                op(dve.tensor_tensor(chosen[:, k, :, :].rearrange("p e t -> p t e"), zb[:],
                                     bc(top[:, 1, :].unsqueeze(2), [P, BLOCKS, EXPERTS]), ALU.is_equal))

            def route(u):
                layer, b = divmod(u, IMAGES)
                hot = u % 2
                to_tokens(b)
                token_stats(1e-5)
                if u:
                    dve.wait_ge(s_xn_st[u - 1], 16)
                normalise(tok[b], work_tok[0], False)
                dve.sem_inc(s_xn, 1)
                dve.wait_ge(s_acc, u + 1)
                op(dve.tensor_tensor(z[:], acc_ps[:, 0:BLOCKS * EXPERTS].rearrange("p (t e) -> p t e", e=EXPERTS),
                                     bc(rstd[:].unsqueeze(2), [P, BLOCKS, EXPERTS]), ALU.mult))
                dve.sem_inc(s_acc_free, 1)
                op(dve.tensor_tensor(z[:], z[:], bc(router_b[:, layer, :].unsqueeze(1), [P, BLOCKS, EXPERTS]), ALU.add))
                op(dve.tensor_reduce(top[:, 0, :], z[:], AX.X, ALU.max))
                dve.tensor_tensor(za[:], z[:], bc(top[:, 0, :].unsqueeze(2), [P, BLOCKS, EXPERTS]), ALU.subtract) \
                    .then_inc(s_exp_in, 1)
                one_hot_top(z, 0)
                first = chosen[:, 0, :, :].rearrange("p e t -> p t e")
                op(dve.scalar_tensor_tensor(z[:], first, -3.0e38, z[:], ALU.mult, ALU.add))
                one_hot_top(z, 1)
                dve.tensor_tensor(chosen_any[:], chosen[:, 0, :, :], chosen[:, 1, :, :], ALU.add).then_inc(s_ready, 1)
                dve.wait_ge(s_exp, u + 2)
                op(dve.tensor_reduce(top[:, 2, :], prob[:], AX.X, ALU.add))
                op(dve.reciprocal(top[:, 2, :], top[:, 2, :]))
                op(dve.tensor_tensor(prob[:], prob[:], bc(top[:, 2, :].unsqueeze(2), [P, BLOCKS, EXPERTS]), ALU.mult))
                for k in range(CHOICES):
                    op(dve.tensor_tensor(za[:], prob[:], chosen[:, k, :, :].rearrange("p e t -> p t e"), ALU.mult))
                    op(dve.tensor_reduce(share[b][:, k, :], za[:], AX.X, ALU.add))
                if layer == 0:
                    op(dve.tensor_tensor(top[:, 3, :], share[b][:, 0, :], share[b][:, 1, :], ALU.add))
                    op(dve.reciprocal(top[:, 3, :], top[:, 3, :]))
                    op(dve.tensor_tensor(share[b][:], share[b][:], bc(top[:, 3, :].unsqueeze(1), [P, CHOICES, BLOCKS]),
                                         ALU.mult))
                bank = read()
                op(dve.tensor_copy(prefix[:].rearrange("p e t -> p (e t)"), bank[:, 0:EXPERTS * BLOCKS]))
                dve.sem_inc(s_freed, 1)
                bank = read()
                op(dve.tensor_copy(total[:].rearrange("p e t -> p (e t)"), bank[:, 0:EXPERTS * BLOCKS]))
                dve.sem_inc(s_freed, 1)
                op(dve.tensor_tensor_scan(upto[:].rearrange("p e t -> p (e t)"), resets[:].rearrange("p e t -> p (e t)"),
                                          total[:].rearrange("p e t -> p (e t)"), 0.0, ALU.mult, ALU.add))
                counts = upto[:, :, BLOCKS - 1]
                op(dve.tensor_scalar(n_tiles_i[:], counts, float(SLOTS - 1), None, ALU.add))
                op(dve.tensor_scalar(n_tiles_i[:], n_tiles_i[:], SLOTS.bit_length() - 1, None, ALU.logical_shift_right))
                op(dve.tensor_copy(n_tiles[:, 0, :], n_tiles_i[:]))
                op(dve.memset(n_tiles[:, 1, :], 1.0))
                op(dve.tensor_tensor_scan(n_tiles[:, 2, :], n_tiles[:, 1, :], n_tiles[:, 0, :], 0.0, ALU.mult, ALU.add))
                op(dve.tensor_tensor(n_tiles[:, 3, :], n_tiles[:, 2, :], n_tiles[:, 0, :], ALU.subtract))
                op(dve.tensor_scalar(n_tiles[:, 3, :], n_tiles[:, 3, :], float(SLOTS), None, ALU.mult))
                op(dve.tensor_tensor(upto[:], upto[:], total[:], ALU.subtract))
                op(dve.tensor_tensor(upto[:], upto[:], prefix[:], ALU.add))
                op(dve.tensor_tensor(upto[:], upto[:], bc(n_tiles[:, 3, :].unsqueeze(2), [P, EXPERTS, BLOCKS]), ALU.add))
                for k in range(CHOICES):
                    op(dve.tensor_tensor(total[:], upto[:], chosen[:, k, :, :], ALU.mult))
                    op(dve.tensor_reduce(place[:, 0, :], total[:].rearrange("p e t -> p t e"), AX.X, ALU.add))
                    op(dve.tensor_copy(place_i[:, 0, :], place[:, 0, :]))
                    op(dve.tensor_scalar(place_i[:, 1, :], place_i[:, 0, :], P - 1, None, ALU.bitwise_and))
                    op(dve.tensor_scalar(place_i[:, 2, :], place_i[:, 0, :], P.bit_length() - 1, None,
                                         ALU.logical_shift_right))
                    op(dve.tensor_copy(place[:, 1:3, :], place_i[:, 1:3, :]))
                    if u or k:
                        dve.wait_ge(s_hot_used, u * CHOICES + k)
                    n = TILES * HALVES
                    op(dve.tensor_tensor(hot_lane[:], bc(lane[:].unsqueeze(1), [P, BLOCKS, P]),
                                         bc(place[:, 1, :].unsqueeze(2), [P, BLOCKS, P]), ALU.is_equal))
                    op(dve.tensor_tensor(hot_block[:, :, 0, :], bc(block_no[:].unsqueeze(1), [P, BLOCKS, n]),
                                         bc(place[:, 2, :].unsqueeze(2), [P, BLOCKS, n]), ALU.is_equal))
                    op(dve.tensor_tensor(hot_block[:, :, 1, :], hot_block[:, :, 0, :],
                                         bc(row_lo[:].unsqueeze(2), [P, BLOCKS, n]), ALU.mult))
                    dve.tensor_scalar(hot_block[:, :, 0, :], hot_block[:, :, 0, :], row_hi[:, k:k + 1], None,
                                      ALU.mult).then_inc(s_hot, 1)
                op(dve.tensor_tensor(tile_cmp[:], bc(n_tiles[:, 2, :].unsqueeze(1), [P, TILES, EXPERTS]),
                                     bc(tile_no[:].unsqueeze(2), [P, TILES, EXPERTS]), ALU.is_le))
                op(dve.tensor_reduce(tile_e[:], tile_cmp[:], AX.X, ALU.add))
                op(dve.tensor_scalar(tile_e[:], tile_e[:], float(EXPERTS - 1), None, ALU.min))
                op(dve.tensor_copy(tile_expert[hot][:], tile_e[:]))
                op(dve.tensor_tensor(tile_cmp[:], bc(tile_e[:].unsqueeze(2), [P, TILES, EXPERTS]),
                                     bc(expert_no[:].unsqueeze(1), [P, TILES, EXPERTS]), ALU.is_equal))
                for c in range(BIAS):
                    op(dve.tensor_tensor(bias_mul[:, :, c, :], tile_cmp[:],
                                         bc(bias[layer][:, c, :].unsqueeze(1), [P, TILES, EXPERTS]), ALU.mult))
                op(dve.tensor_reduce(tile_bias[hot][:], bias_mul[:], AX.X, ALU.add))
                dve.wait_ge(s_hot_used, (u + 1) * CHOICES)
                n = TILES * HALVES
                op(dve.tensor_copy(rows_f[:, 0:2, :], acc_ps[:, 0:2 * n].rearrange("p (a q) -> p a q", a=2)))
                dve.sem_inc(s_acc_free, 1)
                op(dve.tensor_tensor(rows_f[:, 0, :], rows_f[:, 0, :], rows_f[:, 1, :], ALU.add))
                op(dve.tensor_scalar(rows_f[:, 1, :], rows_f[:, 0, :], 0.0, float(EMPTY), ALU.is_equal, ALU.mult))
                op(dve.scalar_tensor_tensor(rows_f[:, 0, :], rows_f[:, 0, :], -1.0, rows_f[:, 1, :], ALU.add, ALU.add))
                op(dve.tensor_copy(tile_rows[hot][:, :, 1, :], rows_f[:, 0, :].rearrange("p (j h) -> p j h", h=HALVES)))
                op(dve.tensor_scalar(rows_f[:, 1, :], rows_f[:, 0, :], float(TOKENS), -float(TOKENS), ALU.is_ge, ALU.mult))
                op(dve.tensor_tensor(rows_f[:, 1, :], rows_f[:, 1, :], rows_f[:, 0, :], ALU.add))
                op(dve.tensor_scalar(tile_rows[hot][:, :, 0, :], rows_f[:, 1, :].rearrange("p (j h) -> p j h", h=HALVES),
                                     float(TOKENS - 1), None, ALU.min))
                dve.sem_inc(s_table, 1)

            def combine(u):
                b = u % IMAGES
                dve.sem_inc(s_buf, 1)
                dve.wait_ge(s_y_in[u], 16 * CHOICES)
                for k in range(CHOICES):
                    last = k == CHOICES - 1 and u >= IMAGES
                    with rounds(dve, GROUPS, (own, 0 if last else 1)) as i:
                        for g in range(GROUP):
                            at = i * GROUP + g
                            one = tok[b][:, bass.ds(at, 1), :].rearrange("p a c -> p (a c)")
                            ins = dve.scalar_tensor_tensor(
                                one, work_tok[1 + k][:, bass.ds(at, 1), :].rearrange("p a c -> p (a c)"),
                                share[b][:, k, bass.ds(at, 1)], one, ALU.mult, ALU.add)
                        if last:
                            ins.then_inc(s_ln, 1)
                        else:
                            own.step(ins)
                    if not last:
                        own.wait()

            def mix(b):
                with rounds(dve, GROUPS, (own, 1)) as i:
                    for g in range(GROUP):
                        at = i * GROUP + g
                        ins = dve.bn_stats(stats[:, bass.ds(at, 1), :].rearrange("p a s -> p (a s)"),
                                     tok[b][:, bass.ds(at, 1), :].rearrange("p a c -> p (a c)"))
                    own.step(ins)
                own.wait()
                token_stats(1e-6)
                dve.wait_ge(s_xn_st[1], 16)
                normalise(tok[b], work_tok[0], True)
                to_channels(work[1])
                with rounds(dve, GROUPS) as i:
                    ap = tok[b][:, bass.ds(i * GROUP, GROUP), :]
                    dve.tensor_tensor(ap, ap, work_tok[0][:, bass.ds(i * GROUP, GROUP), :], ALU.add).then_inc(s_ln, 1)
                to_channels(state[b])
                op(dve.tensor_reduce(gap[:], work[1][:], AX.X, ALU.add))
                dve.tensor_scalar(gap[:], gap[:], 1.0 / TOKENS, None, ALU.mult).then_inc(s_ready, 1)
                bank = read()
                op(dve.tensor_scalar(mix_h[:], bank[0:EXPERTS, 0:1], mix_b1[:], 0.0, ALU.add, ALU.max))
                dve.sem_inc(s_freed, 1)
                dve.sem_inc(s_ready, 1)
                bank = read()
                op(dve.tensor_scalar(mix_s[:, 0:1], bank[:, 0:1], mix_b2[:], 0.0, ALU.add, ALU.max))
                dve.sem_inc(s_freed, 1)
                op(dve.tensor_scalar(mix_hot[:, 0, :], step_no[:], mix_s[:, 0:1], None, ALU.is_le))
                op(dve.tensor_reduce(mix_s[:, 1:2], mix_hot[:, 0, 1:KERNELS - 1], AX.X, ALU.add))
                op(dve.tensor_tensor(mix_s[:, 2:3], mix_s[:, 0:1], mix_s[:, 1:2], ALU.subtract))
                op(dve.tensor_scalar(mix_s[:, 3:4], mix_s[:, 1:2], 1.0, mix_s[:, 0:1], ALU.add, ALU.subtract))
                op(dve.tensor_scalar(mix_hot[:, 0, :], step_no[:], mix_s[:, 1:2], mix_s[:, 3:4], ALU.is_equal, ALU.mult))
                op(dve.tensor_scalar(mix_hot[:, 1, :], step_no[:], -1.0, mix_s[:, 1:2], ALU.add, ALU.is_equal))
                op(dve.tensor_scalar(mix_hot[:, 1, :], mix_hot[:, 1, :], mix_s[:, 2:3], None, ALU.mult))
                op(dve.tensor_tensor(mix_hot[:, 0, :], mix_hot[:, 0, :], mix_hot[:, 1, :], ALU.add))
                op(dve.scalar_tensor_tensor(state[b][:], work[1][:], mix_hot[:, 0, 0:1], state[b][:], ALU.mult, ALU.add))
                pool_in = work[1][:].rearrange("p (h w) -> p h w", h=SIDE)
                across = work[2][:].rearrange("p (h w) -> p h w", h=SIDE)
                last, edge = SIDE - 1, SIDE - 2

                def grow(k):
                    dve.tensor_tensor(across[:, :, 1:last], pool_in[:, :, 0:edge], pool_in[:, :, 2:SIDE], ALU.max)
                    op(dve.tensor_copy(across[:, :, 0:SIDE:last], pool_in[:, :, 1:last:edge - 1]))
                    if k == 1:
                        op(dve.tensor_tensor(across, across, pool_in, ALU.max))
                    dve.tensor_tensor(pool_in[:, 1:last, :], across[:, 0:edge, :], across[:, 2:SIDE, :], ALU.max)
                    op(dve.tensor_copy(pool_in[:, 0:SIDE:last, :], across[:, 1:last:edge - 1, :]))
                    if k == 1:
                        op(dve.tensor_tensor(pool_in, across, pool_in, ALU.max))
                    ins = dve.scalar_tensor_tensor(state[b][:], work[1][:], mix_hot[:, 0, k:k + 1], state[b][:],
                                                   ALU.mult, ALU.add)
                    op(ins)
                for k in range(1, KERNELS):
                    grow(k)
                dve.sem_inc(s_state, 1)

            for b in range(IMAGES):
                route(b)
            for b in range(IMAGES):
                combine(b)
                mix(b)
            for b in range(IMAGES):
                route(2 + b)
            for b in range(IMAGES):
                combine(2 + b)
                to_channels(state[b])
                dve.sem_inc(s_out, 1)


_INS = ['x', 'L0_conv_w1', 'L0_conv_w2', 'L0_conv_g1', 'L0_conv_b1', 'L0_conv_g2', 'L0_conv_b2', 'L0_conv_lw1',
        'L0_conv_lb1', 'L0_conv_lw2', 'L0_conv_lb2', 'L0_ffn_Wr', 'L0_ffn_br', 'L0_ffn_W1', 'L0_ffn_b1', 'L0_ffn_W2',
        'L0_ffn_b2', 'L1_conv_w1', 'L1_conv_b1', 'L1_conv_w2', 'L1_conv_b2', 'L1_ffn_gate_w', 'L1_ffn_gate_b',
        'L1_ffn_w1', 'L1_ffn_b1', 'L1_ffn_w2', 'L1_ffn_b2']


def kernel(**inputs):
    import concourse.bacc as bacc
    from concourse.bass_utils import run_bass_kernel_spmd

    nc = bacc.Bacc("TRN2", target_bir_lowering=False, num_devices=1)
    arrays, args = {}, {}
    for name in _INS:
        a = np.ascontiguousarray(inputs[name])
        arrays[f"in_{name}"] = a
        args[name] = nc.dram_tensor(f"in_{name}", a.shape, mybir.dt.from_np(a.dtype), kind="ExternalInput").ap()
    out = nc.dram_tensor("out_0", (IMAGES, P, SIDE, SIDE), F32, kind="ExternalOutput").ap()
    build(nc, out=out, **args)
    r = run_bass_kernel_spmd(nc, [arrays], core_ids=[0])
    return r.results[0]["out_0"]
```

```python
from contextlib import ExitStack, contextmanager

import numpy as np

import concourse.bass as bass
from concourse import mybir

ALU = mybir.AluOpType
ACT = mybir.ActivationFunctionType
AX = mybir.AxisListType
F32 = mybir.dt.float32
BF16 = mybir.dt.bfloat16
I32 = mybir.dt.int32
U32 = mybir.dt.uint32

P = 128
IMAGES, SIDE = 2, 64
TOKENS = SIDE * SIDE
BLOCKS = TOKENS // P
GROUP = 4
GROUPS = BLOCKS // GROUP
EXPERTS, CHOICES, HIDDEN = 8, 2, 512
CHUNKS = HIDDEN // P
PAIRS = CHOICES * TOKENS
SLOTS = 256
HALVES = SLOTS // P
TILES = (PAIRS - EXPERTS) // SLOTS + EXPERTS
EMPTY = 2 * PAIRS
RING = 4
KERNELS = 7
UNITS = 4
BIAS = CHUNKS + 1
PEEL = 7
AHEAD = 4
TURNS = (TILES - AHEAD - PEEL) // RING

RUNS = [(0, 1), (2,), (3,)]

WHEN = [
    [(7, "route_turn", 1), (11, "route_slots", 1), (15, "route_store", 1), (15, "route_invert", 1)],
    [(3, "outputs", 0), (15, "mix_turn", 0), (19, "mix_score", 0), (39, "outputs", 1), (39, "route_turn", 2),
     (39, "route_slots", 2), (39, "route_store", 2), (39, "route_invert", 2)],
    [(7, "mix_turn", 1), (11, "mix_score", 1), (31, "route_turn", 3), (39, "route_slots", 3),
     (39, "route_store", 3), (39, "route_invert", 3)],
    [(0, "outputs", 2), (11, "last_turn", 0), (15, "last_store", 0), (39, "outputs", 3), (39, "last_turn", 1),
     (39, "last_store", 1)],
]


class Count:

    def __init__(self, sem=None, eng=None, start=0):
        self.sem, self.eng, self.n, self.x = sem, eng, start, None

    def value(self, back=0):
        n = self.n - back
        return n if self.x is None else self.x + n

    def step(self, ins=None):
        self.n += 1
        if ins is not None:
            ins.then_inc(self.sem, 1)

    def wait(self, back=0):
        self.eng.wait_ge(self.sem, self.value(back))


@contextmanager
def rounds(eng, times, *counts):
    first = [c.n for c, _ in counts]
    with eng.Fori(0, times) as i:
        for c, per in counts:
            c.x = i * per
        yield i
    for (c, per), n in zip(counts, first):
        assert c.n - n == per, (c.sem, c.n - n, per)
        c.x, c.n = None, n + per * times


class Tile:

    def __init__(self, unit, j, i=None):
        self.s, self.i = unit * TILES + j, i
        run = next(r for r in RUNS if unit in r)
        self.first, self.last = run[0] * TILES, (run[-1] + 1) * TILES - 1
        self.loop_unit, self.loop_at = unit, j

    def at(self, d=0):
        if self.i is not None:
            return self.loop_unit, self.i * RING + (self.loop_at + d)
        return divmod(self.s + d, TILES)

    def has(self, d=0):
        return self.i is not None or self.first <= self.s + d <= self.last

    def old(self, d):
        return self.s + d >= 0

    def done(self, d=0, per=1, part=None):
        n = (self.s + d) * per + (per if part is None else part)
        return n if self.i is None else self.i * (RING * per) + n

    def slot(self, n, d=0):
        return (self.s + d) % n

    def landed(self, d=0, each=1):
        n = ((self.s + d) // RING + 1) * 16 * each
        return n if self.i is None else self.i * (16 * each) + n


def tile_steps(eng, unit, step, between):
    def insert(j):
        if j in between:
            between[j]()

    for j in range(PEEL):
        insert(j)
        step(Tile(unit, j))
    j = PEEL
    while j < PEEL + TURNS * RING:
        insert(j)
        end = j + RING
        while end < PEEL + TURNS * RING and end not in between:
            end += RING
        with eng.Fori(0, (end - j) // RING) as i:
            for k in range(RING):
                step(Tile(unit, j + k, i))
        j = end
    for j in range(j, TILES + 2 * ends_run(unit)):
        if j < TILES:
            insert(j)
        step(Tile(unit, j))
    insert(TILES)


def begins_run(u):
    return any(u == r[0] for r in RUNS)


def ends_run(u):
    return any(u == r[-1] for r in RUNS)


def plan(u, **work):
    found = {}
    for at, name, *args in WHEN[u]:
        if name in work:
            before = found.get(at)
            found[at] = (lambda before=before, f=work[name], args=args: (before and before(), f(*args)))
    return found


def build(nc, x, L0_conv_w1, L0_conv_w2, L0_conv_g1, L0_conv_b1, L0_conv_g2, L0_conv_b2, L0_conv_lw1, L0_conv_lb1,
          L0_conv_lw2, L0_conv_lb2, L0_ffn_Wr, L0_ffn_br, L0_ffn_W1, L0_ffn_b1, L0_ffn_W2, L0_ffn_b2, L1_conv_w1,
          L1_conv_b1, L1_conv_w2, L1_conv_b2, L1_ffn_gate_w, L1_ffn_gate_b, L1_ffn_w1, L1_ffn_b1, L1_ffn_w2,
          L1_ffn_b2, out):
    with ExitStack() as ctx:
        def sb(name, shape, dt=F32):
            return ctx.enter_context(nc.sbuf_tensor(name, shape, dt))

        def ps(name, shape, dt=F32):
            return ctx.enter_context(nc.psum_tensor(name, shape, dt))

        def sem(name):
            return ctx.enter_context(nc.semaphore(name))

        xn_rows = [nc.dram_tensor(f"xn_rows{u}", [TOKENS, P], F32).ap() for u in range(UNITS)]
        y_rows = [nc.dram_tensor(f"y_rows{u}", [PAIRS, P], F32).ap() for u in range(UNITS)]

        state = [sb(f"state{b}", [P, TOKENS]) for b in range(IMAGES)]
        tok = [sb(f"tok{b}", [P, BLOCKS, P]) for b in range(IMAGES)]
        work = [sb(f"work{i}", [P, TOKENS]) for i in range(3)]
        work_tok = [w[:].rearrange("p (t c) -> p t c", t=BLOCKS) for w in work]

        ident = sb("ident", [P, P])
        ones = sb("ones", [P, P], BF16)
        before = sb("before", [P, P], BF16)
        lane = sb("lane", [P, P, BLOCKS], BF16)
        block_no = sb("block_no", [P, TILES * HALVES, BLOCKS], BF16)
        tile_no = sb("tile_no", [P, TILES])
        expert_no = sb("expert_no", [P, EXPERTS])
        rank_no = sb("rank_no", [P, EXPERTS])
        resets = sb("resets", [P, EXPERTS, BLOCKS])
        row_hi = sb("row_hi", [P, CHOICES])
        row_lo = sb("row_lo", [P, BLOCKS], BF16)
        step_no = sb("step_no", [P, KERNELS])
        conv_w = sb("conv_w", [P, 2, SIDE])
        gamma = sb("gamma", [P, 2])
        beta = sb("beta", [P, 2])
        lb1 = sb("lb1", [P, 2])
        lb2 = sb("lb2", [P, 1])
        router = sb("router", [EXPERTS, 2, P])
        gate_w = sb("gate_w", [P, EXPERTS])
        router_sum = sb("router_sum", [EXPERTS, 2])
        routerT = sb("routerT", [P, 2, EXPERTS])
        router_b = sb("router_b", [P, 2, EXPERTS])
        bias = [sb(f"bias{l}", [P, BIAS, EXPERTS]) for l in range(2)]
        bias1 = [sb(f"bias1_{l}", [P, EXPERTS, CHUNKS]) for l in range(2)]
        bias2 = [sb(f"bias2_{l}", [EXPERTS, P]) for l in range(2)]
        mix_w1 = sb("mix_w1", [EXPERTS, P])
        mix_w1T = sb("mix_w1T", [P, EXPERTS])
        mix_w2 = sb("mix_w2", [P, EXPERTS])
        mix_w2T = sb("mix_w2T", [EXPERTS, P])
        mix_b1 = sb("mix_b1", [EXPERTS, 1])
        mix_b2 = sb("mix_b2", [P, 1])

        stats = sb("stats", [P, BLOCKS, 6])
        mean = sb("mean", [P, BLOCKS])
        rstd = sb("rstd", [P, BLOCKS])
        var = sb("var", [P, BLOCKS])
        tmp_s = sb("tmp_s", [P, BLOCKS])
        line_mul = sb("line_mul", [P, 2])
        line_add = sb("line_add", [P, 2])
        dots = sb("dots", [P, IMAGES])
        gates = sb("gates", [P, 5, IMAGES])
        soft = sb("soft", [IMAGES, 3, P])
        soft_s = sb("soft_s", [IMAGES, 4])
        hid = sb("hid", [P, 2, IMAGES])
        z = sb("z", [P, BLOCKS, EXPERTS])
        za = sb("za", [P, BLOCKS, EXPERTS])
        zb = sb("zb", [P, BLOCKS, EXPERTS])
        prob = sb("prob", [P, BLOCKS, EXPERTS])
        top = sb("top", [P, 4, BLOCKS])
        chosen = sb("chosen", [P, CHOICES, EXPERTS, BLOCKS])
        chosen_any = sb("chosen_any", [P, EXPERTS, BLOCKS], BF16)
        share = [sb(f"share{b}", [P, CHOICES, BLOCKS]) for b in range(IMAGES)]
        prefix = sb("prefix", [P, EXPERTS, BLOCKS])
        upto = sb("upto", [P, EXPERTS, BLOCKS])
        total = sb("total", [P, EXPERTS, BLOCKS])
        n_tiles = sb("n_tiles", [P, 4, EXPERTS])
        n_tiles_i = sb("n_tiles_i", [P, EXPERTS], I32)
        place = sb("place", [P, 3, BLOCKS])
        place_i = sb("place_i", [P, 3, BLOCKS], I32)
        shared = sb("shared", [P, P * BLOCKS // 2])
        hot_lane = shared[:].bitcast(BF16).rearrange("p (q t) -> p q t", t=BLOCKS)
        lw1, lw2, lw1T, lw2T = [shared[:, i * 2 * P:(i + 1) * 2 * P].rearrange("p (a j) -> p a j", a=2)
                                for i in range(4)]
        spread = shared[:, 8 * P:12 * P].rearrange("p (a b j) -> p a b j", a=IMAGES, b=IMAGES)
        lines = shared[:, 12 * P:14 * P].rearrange("p (k b s) -> p k b s", k=2, b=IMAGES)
        hot_block = sb("hot_block", [P, 2, TILES * HALVES, BLOCKS], BF16)
        place_b = sb("place_b", [P, 2, BLOCKS], BF16)
        tile_cmp = sb("tile_cmp", [P, TILES, EXPERTS])
        tile_e = sb("tile_e", [P, TILES])
        rows_f = sb("rows_f", [P, 2, TILES * HALVES])
        bias_mul = sb("bias_mul", [P, TILES, EXPERTS])
        tile_expert = [sb(f"tile_expert{i}", [P, TILES], I32) for i in range(2)]
        tile_rows = [sb(f"tile_rows{i}", [P, TILES, 2, HALVES]) for i in range(2)]
        tile_bias = [sb(f"tile_bias{i}", [P, TILES, BIAS]) for i in range(2)]
        gap = sb("gap", [P, 1])
        mix_h = sb("mix_h", [EXPERTS, 1])
        mix_s = sb("mix_s", [P, 4])
        mix_hot = sb("mix_hot", [P, 3, KERNELS])

        g_slot = sb("g_slot", [P, RING, HALVES], U32)
        s_slot = sb("s_slot", [P, RING, HALVES], U32)
        b_slot = sb("b_slot", [P, 2, BIAS])
        xg = sb("xg", [P, RING, HALVES, P])
        xT = sb("xT", [P, 2, SLOTS])
        w1s = sb("w1s", [P, RING, HIDDEN])
        w2s = sb("w2s", [P, RING, CHUNKS, P])
        hT = sb("hT", [P, 2, CHUNKS, SLOTS])
        yT = sb("yT", [P, 2, SLOTS])
        yr = sb("yr", [P, RING, HALVES, P])

        xT_ps = ps("xT_ps", [P, 512])
        h_ps = [ps(f"h_ps{i}", [P, 2, SLOTS]) for i in range(2)]
        yT_ps = ps("yT_ps", [P, 512])
        yr_ps = ps("yr_ps", [P, 4, P])
        turn_ps = ps("turn_ps", [P, 2, 512])
        acc_ps = ps("acc_ps", [P, 512])

        s_par = sem("params_loaded")
        s_x = [[sem(f"image{b}_part{q}_loaded") for q in range(2)] for b in range(IMAGES)]
        s_const = sem("constants_made")
        s_own = sem("vector_steps")
        s_bias = sem("bias_slot_set")
        s_turned = sem("turn_bank_filled")
        s_freed = [sem(f"turn_bank{i}_freed") for i in range(2)]
        s_acc = sem("acc_bank_filled")
        s_acc_free = sem("acc_bank_freed")
        s_ready = sem("vector_result_for_tensor")
        s_ln = sem("normalised_group_for_tensor")
        s_state = sem("state_for_tensor")
        s_exp_in = sem("exp_input_ready")
        s_exp = sem("exp_done")
        s_xn = sem("normalised_rows_ready")
        s_xn_st = [sem(f"normalised_rows_stored{u}") for u in range(UNITS)]
        s_table = sem("tile_tables_ready")
        s_hot = sem("one_hots_ready")
        s_hot_used = sem("one_hots_used")
        s_g_idx = sem("gather_rows_set")
        s_gath = [sem(f"gathered{i}") for i in range(RING)]
        s_w = [sem(f"weights_loaded{i}") for i in range(RING)]
        s_xt_ps = sem("x_turned")
        s_xt_sb = sem("x_turned_copied")
        s_h_ps = sem("hidden_made")
        s_h_sb = sem("hidden_activated")
        s_y_ps = sem("expert_out_made")
        s_y_sb = sem("expert_out_copied")
        s_yr_ps = sem("out_rows_turned")
        s_yr_sb = sem("out_rows_copied")
        s_scat = [sem(f"scattered{i}") for i in range(RING)]
        s_begun = sem("indirect_dmas_begun")
        s_buf = sem("work_buffers_free")
        s_y_in = [sem(f"expert_rows_loaded{u}") for u in range(UNITS)]
        s_out = sem("image_out_ready")
        s_done = sem("output_stored")

        W1 = [L0_ffn_W1, L1_ffn_w1]
        W2 = [L0_ffn_W2, L1_ffn_w2]

        small = [
            (conv_w[:, 0, :], L0_conv_w1.rearrange("c a h b -> c (a h b)")),
            (conv_w[:, 1, :], L0_conv_w2.rearrange("c a b w -> c (a b w)")),
            (gamma[:, 0:1], L0_conv_g1.rearrange("(c a) -> c a", a=1)),
            (gamma[:, 1:2], L0_conv_g2.rearrange("(c a) -> c a", a=1)),
            (beta[:, 0:1], L0_conv_b1.rearrange("(c a) -> c a", a=1)),
            (beta[:, 1:2], L0_conv_b2.rearrange("(c a) -> c a", a=1)),
            (lw1[:, 0, :], L0_conv_lw1[0:P, :]),
            (lw1[:, 1, :], L0_conv_lw1[P:2 * P, :]),
            (lw2[:, :, :], L0_conv_lw2.rearrange("c (a j) -> c a j", a=2)),
            (lb1[:, 0:1], L0_conv_lb1[0:P].rearrange("(c a) -> c a", a=1)),
            (lb1[:, 1:2], L0_conv_lb1[P:2 * P].rearrange("(c a) -> c a", a=1)),
            (lb2[:, :], L0_conv_lb2.rearrange("(c a) -> c a", a=1)),
            (router[:, 0, :], L0_ffn_Wr),
            (gate_w[:, :], L1_ffn_gate_w),
            (router_b[:, 0, :], L0_ffn_br.partition_broadcast(P)),
            (router_b[:, 1, :], L1_ffn_gate_b.partition_broadcast(P)),
            (bias1[0][:, :, :], L0_ffn_b1.rearrange("e (p c) -> p e c", c=CHUNKS)),
            (bias1[1][:, :, :], L1_ffn_b1.rearrange("e (p c) -> p e c", c=CHUNKS)),
            (bias2[0][:, :], L0_ffn_b2),
            (bias2[1][:, :], L1_ffn_b2),
            (mix_w1[:, :], L1_conv_w1),
            (mix_w2[:, :], L1_conv_w2),
            (mix_b1[:, :], L1_conv_b1.rearrange("(c a) -> c a", a=1)),
            (mix_b2[:, :], L1_conv_b2.rearrange("(c a) -> c a", a=1)),
        ]
        CONSTS = 14

        block = ctx.enter_context(nc.Block())

        @block.sync
        def _(sp):
            def load_weights(t, d):
                unit, at = t.at(d)
                layer, i = divmod(unit, IMAGES)
                if t.old(d - RING):
                    sp.wait_ge(s_y_ps, t.done(d - RING))
                e = sp.value_load(tile_expert[i][0:1, bass.ds(at, 1)], min_val=0, max_val=EXPERTS - 1)
                s = t.slot(RING, d)
                sp.dma_start(w1s[:, s, :], W1[layer][bass.ds(e, 1)].rearrange("a d f -> (a d) f")) \
                    .then_inc(s_w[s], 16)
                sp.dma_start(w2s[:, s, :, :], W2[layer][bass.ds(e, 1)].rearrange("a (p c) d -> (a p) c d", c=CHUNKS)) \
                    .then_inc(s_w[s], 16)

            def store_normalised(u):
                sp.wait_ge(s_xn, u + 1)
                sp.dma_start(xn_rows[u].rearrange("(p t) c -> p t c", t=BLOCKS), work_tok[0]) \
                    .then_inc(s_xn_st[u], 16)

            def load_outputs(u):
                last = Tile(u, TILES - 1)
                for d in range(RING):
                    sp.wait_ge(s_scat[last.slot(RING, -d)], last.landed(-d, HALVES))
                sp.wait_ge(s_buf, u + 1)
                for k in range(CHOICES):
                    sp.dma_start(work_tok[1 + k], y_rows[u].rearrange("(k p t) c -> k p t c", k=CHOICES, t=BLOCKS)[k]) \
                        .then_inc(s_y_in[u], 16)

            def store_image(b):
                sp.wait_ge(s_out, b + 1)
                sp.dma_start(out[b].rearrange("c h w -> c (h w)"), state[b][:]).then_inc(s_done, 16)

            def weights(u):
                if begins_run(u):
                    sp.wait_ge(s_table, u + 1)
                    for d in range(AHEAD - 1):
                        load_weights(Tile(u, 0), d)

                def step(t):
                    if t.has(AHEAD - 1):
                        if t.i is None and t.at(AHEAD - 1) == (u + 1, 0):
                            sp.wait_ge(s_table, u + 2)
                        load_weights(t, AHEAD - 1)
                tile_steps(sp, u, step, plan(u, route_store=store_normalised, outputs=load_outputs,
                                             last_store=store_image))

            for b in range(IMAGES):
                for q in range(2):
                    h = TOKENS // 2
                    sp.dma_start(state[b][:, q * h:(q + 1) * h],
                                 x[b].rearrange("c h w -> c (h w)")[:, q * h:(q + 1) * h]).then_inc(s_x[b][q], 16)
                if b == 0:
                    for to, source in small:
                        sp.dma_start(to, source).then_inc(s_par, 16)
            store_normalised(0)
            for u in range(UNITS):
                weights(u)
            sp.wait_ge(s_done, 16 * IMAGES)

        @block.gpsimd
        def _(pool):
            big = dict(allow_small_or_imprecise_dtypes=True)
            pool.memset(ident[:], 0.0).then_inc(s_const, 1)
            pool.memset(ones[:], 1.0).then_inc(s_const, 1)
            pool.memset(spread, 0.0).then_inc(s_const, 1)
            pool.memset(resets[:], 1.0).then_inc(s_const, 1)
            pool.wait_ge(s_const, 4)
            pool.affine_select(out=ident[:], in_=ident[:], compare_op=ALU.not_equal, fill=1.0, base=0,
                               pattern=[[-1, P]], channel_multiplier=1).then_inc(s_const, 1)
            pool.affine_select(out=before[:], in_=ones[:], compare_op=ALU.is_ge, fill=0.0, base=-1,
                               pattern=[[1, P]], channel_multiplier=-1).then_inc(s_const, 1)
            pool.affine_select(out=spread, in_=spread, compare_op=ALU.not_equal, fill=1.0, base=0,
                               pattern=[[P, IMAGES], [-1, IMAGES], [1, P]], channel_multiplier=-2).then_inc(s_const, 1)
            pool.memset(resets[:, :, 0:1], 0.0).then_inc(s_const, 1)
            pool.iota(lane[:], [[1, P], [0, BLOCKS]], base=0, channel_multiplier=0, **big).then_inc(s_const, 1)
            pool.iota(block_no[:], [[1, TILES * HALVES], [0, BLOCKS]], base=0, channel_multiplier=0, **big).then_inc(s_const, 1)
            pool.iota(tile_no[:], [[1, TILES]], base=0, channel_multiplier=0, **big).then_inc(s_const, 1)
            pool.iota(row_hi[:], [[TOKENS, CHOICES]], base=0, channel_multiplier=BLOCKS, **big).then_inc(s_const, 1)
            pool.iota(row_lo[:], [[1, BLOCKS]], base=1, channel_multiplier=0, **big).then_inc(s_const, 1)
            pool.iota(rank_no[:], [[-1, EXPERTS]], base=EXPERTS, channel_multiplier=0, **big).then_inc(s_const, 1)
            pool.iota(expert_no[:], [[1, EXPERTS]], base=0, channel_multiplier=0, **big).then_inc(s_const, 1)
            pool.iota(step_no[:], [[1, KERNELS]], base=0, channel_multiplier=0, **big).then_inc(s_const, 1)

            def gather(t, d):
                s = t.slot(RING, d)
                pool.wait_ge(s_g_idx, t.done(d))
                pool.sem_inc(s_begun, 1)
                for h in range(HALVES):
                    pool.indirect_dma_start(xg[:, s, h, :], None, xn_rows[t.at(d)[0]],
                                            bass.IndirectOffsetOnAxis(ap=g_slot[:, s, h:h + 1], axis=0)) \
                        .then_inc(s_gath[s], 16)

            def scatter(t, d):
                s = t.slot(RING, d)
                pool.wait_ge(s_yr_sb, t.done(d))
                pool.sem_inc(s_begun, 1)
                for h in range(HALVES):
                    pool.indirect_dma_start(y_rows[t.at(d)[0]],
                                            bass.IndirectOffsetOnAxis(ap=s_slot[:, s, h:h + 1], axis=0),
                                            yr[:, s, h, :], None, bounds_check=PAIRS - 1, oob_is_err=False) \
                        .then_inc(s_scat[s], 16)

            for u in range(UNITS):
                if begins_run(u):
                    pool.wait_ge(s_xn_st[u], 16)
                    for d in range(AHEAD - 1):
                        gather(Tile(u, 0), d)

                def step(t):
                    if t.has(AHEAD - 1):
                        if t.i is None and t.at(AHEAD - 1) == (u + 1, 0):
                            pool.wait_ge(s_xn_st[u + 1], 16)
                        gather(t, AHEAD - 1)
                    if t.has(-2):
                        scatter(t, -2)
                tile_steps(pool, u, step, plan(u))

        @block.scalar
        def _(act):
            turned = Count(s_turned, act)

            def copy_turned(to, source=lambda bank: bank):
                for g in range(1, GROUPS, 2):
                    turned.step()
                    s = turned.n % 2
                    turned.step()
                    turned.wait()
                    act.activation(to(g), source(turn_ps[:, s, :]), ACT.Copy).then_inc(s_freed[s], 1)

            def to_tokens(b):
                copy_turned(lambda g: tok[b][:, g * GROUP:(g + 1) * GROUP, :],
                            lambda bank: bank.rearrange("p (t c) -> p t c", t=GROUP))

            def to_channels(dst):
                copy_turned(lambda g: dst[:, g * 512:(g + 1) * 512])

            def set_gather(t, d):
                unit, at = t.at(d)
                act.activation(g_slot[:, t.slot(RING, d), :], tile_rows[unit % 2][:, bass.ds(at, 1), 0, :]
                               .rearrange("p a h -> p (a h)"), ACT.Copy).then_inc(s_g_idx, 1)

            def copy_x(t, d):
                act.wait_ge(s_xt_ps, t.done(d))
                if t.old(d - 2):
                    act.wait_ge(s_h_ps, t.done(d - 2, 2))
                act.activation(xT[:, t.slot(2, d), :], xT_ps[:, 0:SLOTS], ACT.Copy).then_inc(s_xt_sb, 1)

            def activate(t):
                s = t.slot(2)
                unit, at = t.at()
                if t.old(-2):
                    act.wait_ge(s_y_sb, t.done(-2))
                act.activation(b_slot[:, s, :], tile_bias[unit % 2][:, bass.ds(at, 1), :]
                               .rearrange("p a n -> p (a n)"), ACT.Copy).then_inc(s_bias, 1)
                act.wait_ge(s_bias, t.done())
                func = ACT.Gelu if unit // IMAGES else ACT.Gelu_apprx_tanh
                for c in range(CHUNKS):
                    if c % 2 == 0:
                        act.wait_ge(s_h_ps, t.done(0, 2, c // 2 + 1))
                    ins = act.activation(hT[:, s, c, :], h_ps[c // 2][:, c % 2, :], func, bias=b_slot[:, s, c:c + 1])
                    if c % 2:
                        ins.then_inc(s_h_sb, 1)

            def copy_y(t, d):
                s = t.slot(2, d)
                act.wait_ge(s_y_ps, t.done(d))
                if t.old(d - 2):
                    act.wait_ge(s_yr_ps, t.done(d - 2))
                act.activation(yT[:, s, :], yT_ps[:, 0:SLOTS], ACT.Identity, bias=b_slot[:, s, CHUNKS:BIAS]) \
                    .then_inc(s_y_sb, 1)

            def copy_rows(t, d):
                s = t.slot(RING, d)
                unit, at = t.at(d)
                if t.old(d - RING):
                    act.wait_ge(s_scat[s], t.landed(d - RING, HALVES))
                act.activation(s_slot[:, s, :], tile_rows[unit % 2][:, bass.ds(at, 1), 1, :]
                               .rearrange("p a h -> p (a h)"), ACT.Copy)
                act.wait_ge(s_yr_ps, t.done(d))
                act.activation(yr[:, s, :, :], yr_ps[:, 0:HALVES, :], ACT.Copy).then_inc(s_yr_sb, 1)

            def route_slots(u):
                act.wait_ge(s_exp_in, 2 + u)
                act.activation(prob[:], za[:], ACT.Exp).then_inc(s_exp, 1)
                turned.n += 2

            def route_turn(u):
                to_tokens(u % IMAGES)

            def mix_turn(b):
                to_channels(work[1])
                to_channels(state[b])

            def mix_score(b):
                turned.n += 2

            def last_turn(b):
                to_channels(state[b])

            def tiles(u):
                if begins_run(u):
                    act.wait_ge(s_table, u + 1)
                    for d in range(AHEAD):
                        set_gather(Tile(u, 0), d)
                    copy_x(Tile(u, 0), 0)

                def step(t):
                    if t.has(AHEAD):
                        if t.i is None and t.at(AHEAD) == (u + 1, 0):
                            act.wait_ge(s_table, u + 2)
                        set_gather(t, AHEAD)
                    if t.has(1):
                        copy_x(t, 1)
                    if t.has(0):
                        activate(t)
                    if t.has(-1):
                        copy_y(t, -1)
                    if t.has(-2):
                        copy_rows(t, -2)
                tile_steps(act, u, step, plan(u, route_turn=route_turn, route_slots=route_slots, mix_turn=mix_turn,
                                              mix_score=mix_score, last_turn=last_turn))

            turned.n += 3
            for b in range(IMAGES):
                to_tokens(b)
                to_channels(work[b])
            act.wait_ge(s_exp_in, 1)
            act.activation(soft[:, 1, :], soft[:, 0, :], ACT.Exp, bias=soft_s[:, 1:2], accum_out=soft_s[:, 2:3]) \
                .then_inc(s_exp, 1)
            turned.n += 5
            route_turn(0)
            route_slots(0)
            for u in range(UNITS):
                tiles(u)

        @block.tensor
        def _(pe):
            used = [0]

            def use():
                n = used[0]
                used[0] += 1
                pe.wait_ge(s_freed[n % 2], n // 2 + 1)
                return turn_ps[:, n % 2, :]

            def turn_blocks(source, group, to_tokens=True):
                bank = use()
                for k in range(GROUP):
                    t = group * GROUP + k
                    mm = pe.transpose(bank[:, k * P:(k + 1) * P], source(t), ident[:])
                mm.then_inc(s_turned, 1)

            def channel(b):
                return lambda t: state[b][:, t * P:(t + 1) * P]

            def router_products(b, layer, group):
                for k in range(GROUP):
                    t = group * GROUP + k
                    mm = pe.matmul(acc_ps[:, t * EXPERTS:(t + 1) * EXPERTS], channel(b)(t), routerT[:, layer, :],
                                   start=True, stop=True)
                return mm

            def route_turn(u):
                layer, b = divmod(u, IMAGES)
                pe.wait_ge(s_state, u + 1)
                pe.wait_ge(s_acc_free, 2 * u + 1)
                for g in range(GROUPS):
                    turn_blocks(channel(b), g)
                    mm = router_products(b, layer, g)
                mm.then_inc(s_acc, 1)

            def route_slots(u):
                wait_ready()
                for lhs in (before, ones):
                    bank = use()
                    pe.matmul(bank[:, 0:EXPERTS * BLOCKS], lhs[:], chosen_any[:].rearrange("p e t -> p (e t)"),
                              start=True, stop=True).then_inc(s_turned, 1)

            def route_invert(u):
                pe.wait_ge(s_acc_free, 2 * u + 2)
                n = TILES * HALVES
                for k in range(CHOICES):
                    pe.wait_ge(s_hot, u * CHOICES + k + 1)
                    for t in range(BLOCKS):
                        mm = pe.matmul(acc_ps[:, 0:2 * n], hot_lane[:, :, t], hot_block[:, :, :, t]
                                       .rearrange("p a q -> p (a q)"), start=(k == 0 and t == 0),
                                       stop=(k == CHOICES - 1 and t == BLOCKS - 1))
                    mm.then_inc(s_hot_used, 1)

            ready = [0]

            def wait_ready():
                ready[0] += 1
                pe.wait_ge(s_ready, ready[0])

            def turn_x(t, d):
                pe.wait_ge(s_gath[t.slot(RING, d)], t.landed(d, HALVES))
                if t.old(d - 1):
                    pe.wait_ge(s_xt_sb, t.done(d - 1))
                for h in range(HALVES):
                    mm = pe.transpose(xT_ps[:, h * P:(h + 1) * P], xg[:, t.slot(RING, d), h, :], ident[:])
                mm.then_inc(s_xt_ps, 1)

            def up(t):
                pe.wait_ge(s_xt_sb, t.done())
                pe.wait_ge(s_w[t.slot(RING)], t.landed(0, 2))
                for c in range(CHUNKS):
                    if c % 2 == 0 and t.old(-1):
                        pe.wait_ge(s_h_sb, t.done(-1, 2, c // 2 + 1))
                    mm = pe.matmul(h_ps[c // 2][:, c % 2, :], w1s[:, t.slot(RING), c:HIDDEN:CHUNKS],
                                   xT[:, t.slot(2), :], start=True, stop=True)
                    if c % 2:
                        mm.then_inc(s_h_ps, 1)

            def down(t, d):
                s = t.slot(2, d)
                if t.old(d - 1):
                    pe.wait_ge(s_y_sb, t.done(d - 1))
                for c in range(CHUNKS):
                    if c % 2 == 0:
                        pe.wait_ge(s_h_sb, t.done(d, 2, c // 2 + 1))
                    mm = pe.matmul(yT_ps[:, 0:SLOTS], w2s[:, t.slot(RING, d), c, :], hT[:, s, c, :],
                                   start=(c == 0), stop=(c == CHUNKS - 1))
                mm.then_inc(s_y_ps, 1)

            def turn_y(t, d):
                s = t.slot(2, d)
                pe.wait_ge(s_y_sb, t.done(d))
                if t.old(d - 1):
                    pe.wait_ge(s_yr_sb, t.done(d - 1))
                for h in range(HALVES):
                    mm = pe.transpose(yr_ps[:, h, :], yT[:, s, h * P:(h + 1) * P], ident[:])
                mm.then_inc(s_yr_ps, 1)

            def mix_turn(b):
                turn_back(lambda t: work_tok[0][:, t, :])
                turn_back(lambda t: tok[b][:, t, :])

            def mix_score(b):
                wait_ready()
                bank = use()
                pe.matmul(bank[0:EXPERTS, 0:1], mix_w1T[:], gap[:], start=True, stop=True).then_inc(s_turned, 1)
                wait_ready()
                bank = use()
                pe.matmul(bank[:, 0:1], mix_w2T[:], mix_h[:], start=True, stop=True).then_inc(s_turned, 1)

            def last_turn(b):
                turn_back(lambda t: tok[b][:, t, :])

            def tiles(u):
                if begins_run(u):
                    turn_x(Tile(u, 0), 0)

                def step(t):
                    if t.has(1):
                        turn_x(t, 1)
                    if t.has(0):
                        up(t)
                    if t.has(-1):
                        down(t, -1)
                    if t.has(-2):
                        turn_y(t, -2)
                tile_steps(pe, u, step, plan(u, route_turn=route_turn, route_slots=route_slots,
                                             route_invert=route_invert, mix_turn=mix_turn, mix_score=mix_score,
                                             last_turn=last_turn))

            pe.wait_ge(s_const, CONSTS + 2)
            pe.wait_ge(s_par, 16 * len(small))
            bank = use()
            for j in range(2):
                pe.transpose(bank[:, j * P:(j + 1) * P], lw1[:, j, :], ident[:])
                mm = pe.transpose(bank[:, (2 + j) * P:(3 + j) * P], lw2[:, j, :], ident[:])
            mm.then_inc(s_turned, 1)
            bank = use()
            pe.transpose(bank[0:EXPERTS, 0:P], gate_w[:], ident[:])
            pe.transpose(bank[:, P:P + EXPERTS], mix_w1[:], ident[0:EXPERTS, 0:EXPERTS])
            pe.transpose(bank[0:EXPERTS, 2 * P:3 * P], mix_w2[:], ident[:])
            pe.transpose(bank[:, 3 * P:3 * P + EXPERTS], bias2[0][:], ident[0:EXPERTS, 0:EXPERTS])
            pe.transpose(bank[:, 3 * P + EXPERTS:3 * P + 2 * EXPERTS], bias2[1][:], ident[0:EXPERTS, 0:EXPERTS]) \
                .then_inc(s_turned, 1)
            wait_ready()
            bank = use()
            for layer in range(2):
                mm = pe.transpose(bank[:, layer * EXPERTS:(layer + 1) * EXPERTS], router[:, layer, :],
                                  ident[0:EXPERTS, 0:EXPERTS])
            mm.then_inc(s_turned, 1)

            ln = [0]

            def turn_back(source, groups=range(GROUPS)):
                for g in groups:
                    ln[0] += 1
                    pe.wait_ge(s_ln, ln[0])
                    turn_blocks(source, g)

            for b in range(IMAGES):
                for g in range(GROUPS):
                    if g % (GROUPS // 2) == 0:
                        pe.wait_ge(s_x[b][g // (GROUPS // 2)], 16)
                    turn_blocks(channel(b), g)
                turn_back(lambda t: tok[b][:, t, :])
            wait_ready()
            bank = use()
            for row in range(IMAGES):
                for b in range(IMAGES):
                    mm = pe.matmul(bank[:, row:row + 1], spread[:, row, b, :], dots[:, b:b + 1],
                                   start=(b == 0), stop=(b == IMAGES - 1))
            mm.then_inc(s_turned, 1)
            wait_ready()
            bank = use()
            for j in range(2):
                mm = pe.matmul(bank[:, j * IMAGES:(j + 1) * IMAGES], lw1T[:, j, :], gates[:, 0, :], start=True, stop=True)
            mm.then_inc(s_turned, 1)
            wait_ready()
            bank = use()
            for j in range(2):
                mm = pe.matmul(bank[:, 0:IMAGES], lw2T[:, j, :], hid[:, j, :], start=(j == 0), stop=(j == 1))
            mm.then_inc(s_turned, 1)
            wait_ready()
            bank = use()
            pe.transpose(bank[0:IMAGES, 0:P], gates[:, 1, :], ident[:]).then_inc(s_turned, 1)
            wait_ready()
            bank = use()
            pe.transpose(bank[:, 0:IMAGES], soft[:, 2, :], ident[0:IMAGES, 0:IMAGES]).then_inc(s_turned, 1)

            route_turn(0)
            route_slots(0)
            route_invert(0)
            for u in range(UNITS):
                tiles(u)

        @block.vector
        def _(dve):
            own = Count(s_own, dve)
            turned = Count(s_turned, dve)

            def op(ins):
                own.step(ins)
                own.wait()

            def read(n=None):
                bank = turned.n % 2
                turned.step()
                turned.wait()
                return turn_ps[:, bank, :]

            def rsqrt(v, y, tmp):
                op(dve.tensor_scalar(tmp.bitcast(I32), v.bitcast(I32), 1, None, ALU.logical_shift_right))
                op(dve.tensor_scalar(y.bitcast(I32), tmp.bitcast(I32), -1.0, float(0x5F3759DF), ALU.mult, ALU.add))
                for _ in range(3):
                    op(dve.tensor_tensor(tmp, y, y, ALU.mult))
                    op(dve.scalar_tensor_tensor(tmp, tmp, -0.5, v, ALU.mult, ALU.mult))
                    op(dve.scalar_tensor_tensor(y, tmp, 1.5, y, ALU.add, ALU.mult))

            def moments(st, n, m, v, tmp, eps):
                op(dve.tensor_tensor(tmp, st[:, :, 1], st[:, :, 4], ALU.subtract))
                op(dve.tensor_tensor(m, st[:, :, 1], st[:, :, 4], ALU.add))
                op(dve.tensor_scalar(m, m, 0.5, None, ALU.mult))
                op(dve.scalar_tensor_tensor(tmp, tmp, 0.25, tmp, ALU.mult, ALU.mult))
                op(dve.tensor_tensor(v, st[:, :, 2], st[:, :, 5], ALU.add))
                op(dve.scalar_tensor_tensor(v, v, 1.0 / (2 * n), tmp, ALU.mult, ALU.add))
                op(dve.tensor_scalar(v, v, eps, None, ALU.add))

            def token_stats(eps):
                moments(stats[:], P // 2, mean[:], var[:], tmp_s[:], eps)
                rsqrt(var[:], rstd[:], tmp_s[:])

            def copied(n=None):
                for i in range(2):
                    dve.wait_ge(s_freed[i], (turned.n + 1 - i) // 2 + 1)

            def to_tokens(b):
                for g in range(GROUPS):
                    s = turned.n % 2
                    if g % 2 == 0:
                        dve.tensor_copy(tok[b][:, g * GROUP:(g + 1) * GROUP, :],
                                        read().rearrange("p (t c) -> p t c", t=GROUP)).then_inc(s_freed[s], 1)
                    else:
                        turned.step()
                    dve.wait_ge(s_freed[s], (turned.n - 1) // 2 + 2)
                    for t in range(g * GROUP, (g + 1) * GROUP):
                        ins = dve.bn_stats(stats[:, t, :], tok[b][:, t, :])
                op(ins)

            def to_channels(dst):
                for g in range(0, GROUPS, 2):
                    s = turned.n % 2
                    dve.tensor_copy(dst[:, g * 512:(g + 1) * 512], read()).then_inc(s_freed[s], 1)
                    turned.step()
                copied()

            def normalise(src, dst, signal):
                for g in range(GROUPS):
                    for t in range(g * GROUP, (g + 1) * GROUP):
                        ins = dve.tensor_scalar(dst[:, t, :], src[:, t, :], mean[:, t:t + 1], rstd[:, t:t + 1],
                                                ALU.subtract, ALU.mult)
                    if signal:
                        ins.then_inc(s_ln, 1)
                if not signal:
                    op(ins)

            def bc(ap, shape):
                return ap.to_broadcast(shape)

            for i in range(2):
                dve.sem_inc(s_freed[i], 1)
            dve.sem_inc(s_acc_free, 1)
            dve.wait_ge(s_const, CONSTS + 2)
            dve.wait_ge(s_par, 16 * len(small))
            bank = read()
            dve.tensor_copy(lw1T.rearrange("p a j -> p (a j)"), bank[:, 0:2 * P])
            dve.tensor_copy(lw2T.rearrange("p a j -> p (a j)"), bank[:, 2 * P:4 * P]).then_inc(s_freed[(turned.n - 1) % 2], 1)
            bank = read()
            dve.tensor_copy(router[:, 1, :], bank[0:EXPERTS, 0:P])
            dve.tensor_copy(mix_w1T[:], bank[:, P:P + EXPERTS])
            dve.tensor_copy(mix_w2T[:], bank[0:EXPERTS, 2 * P:3 * P])
            for layer in range(2):
                at = 3 * P + layer * EXPERTS
                op(dve.tensor_copy(bias[layer][:, CHUNKS, :], bank[:, at:at + EXPERTS]))
            for layer in range(2):
                ins = dve.tensor_copy(bias[layer][:, 0:CHUNKS, :], bias1[layer][:].rearrange("p e c -> p c e"))
            ins.then_inc(s_freed[(turned.n - 1) % 2], 1)
            op(dve.tensor_reduce(router_sum[:], router[:], AX.X, ALU.add))
            op(dve.tensor_scalar(router_sum[:], router_sum[:], -1.0 / P, None, ALU.mult))
            dve.tensor_scalar(router[:, 0, :], router[:, 0, :], router_sum[:, 0:1], None, ALU.add)
            dve.tensor_scalar(router[:, 1, :], router[:, 1, :], router_sum[:, 1:2], None, ALU.add).then_inc(s_ready, 1)
            bank = read()
            dve.tensor_copy(routerT[:].rearrange("p l e -> p (l e)"), bank[:, 0:2 * EXPERTS]).then_inc(s_freed[(turned.n - 1) % 2], 1)

            for b in range(IMAGES):
                to_tokens(b)
                token_stats(1e-6)
                normalise(tok[b], tok[b], True)
                to_channels(work[b])
                img = work[b][:].rearrange("p (h w) -> p h w", h=SIDE)
                mul = work[2][:].rearrange("p (h w) -> p h w", h=SIDE)
                op(dve.tensor_tensor(mul, img, bc(conv_w[:, 0, :].unsqueeze(2), [P, SIDE, SIDE]), ALU.mult))
                op(dve.tensor_reduce(lines[:, 0, b, :], mul.rearrange("p h w -> p w h"), AX.X, ALU.add))
                op(dve.tensor_tensor(mul, img, bc(conv_w[:, 1, :].unsqueeze(1), [P, SIDE, SIDE]), ALU.mult))
                op(dve.tensor_reduce(lines[:, 1, b, :], mul, AX.X, ALU.add))
            for k in range(2):
                op(dve.bn_stats(stats[:, k, :], lines[:, k, :, :].rearrange("p b s -> p (b s)")))
            moments(stats[:, 0:2, :], SIDE, mean[:, 0:2], var[:, 0:2], tmp_s[:, 0:2], 1e-5)
            rsqrt(var[:, 0:2], rstd[:, 0:2], tmp_s[:, 0:2])
            op(dve.tensor_tensor(line_mul[:], gamma[:], rstd[:, 0:2], ALU.mult))
            op(dve.tensor_tensor(line_add[:], mean[:, 0:2], line_mul[:], ALU.mult))
            op(dve.tensor_tensor(line_add[:], beta[:], line_add[:], ALU.subtract))
            for k in range(2):
                line = lines[:, k, :, :].rearrange("p b s -> p (b s)")
                op(dve.tensor_scalar(line, line, line_mul[:, k:k + 1], line_add[:, k:k + 1], ALU.mult, ALU.add))
                op(dve.tensor_scalar(line, line, 0.0, None, ALU.max))
            op(dve.tensor_tensor(lines[:, 0, :, :], lines[:, 0, :, :], lines[:, 1, :, :], ALU.mult))
            dve.tensor_reduce(dots[:], lines[:, 0, :, :], AX.X, ALU.add).then_inc(s_ready, 1)
            bank = read()
            op(dve.tensor_copy(gates[:, 0, :], bank[:, 0:IMAGES]))
            dve.sem_inc(s_freed[(turned.n - 1) % 2], 1)
            dve.sem_inc(s_ready, 1)
            bank = read()
            op(dve.tensor_tensor(hid[:], bank[:, 0:2 * IMAGES].rearrange("p (a b) -> p a b", a=2),
                                 bc(lb1[:].unsqueeze(2), [P, 2, IMAGES]), ALU.add))
            dve.sem_inc(s_ready, 1)
            dve.sem_inc(s_freed[(turned.n - 1) % 2], 1)
            bank = read()
            op(dve.tensor_scalar(gates[:, 1, :], bank[:, 0:IMAGES], lb2[:], None, ALU.add))
            dve.sem_inc(s_ready, 1)
            dve.sem_inc(s_freed[(turned.n - 1) % 2], 1)
            bank = read()
            op(dve.tensor_copy(soft[:, 0, :], bank[0:IMAGES, 0:P]))
            op(dve.tensor_reduce(soft_s[:, 0:1], soft[:, 0, :], AX.X, ALU.max))
            dve.tensor_scalar(soft_s[:, 1:2], soft_s[:, 0:1], -1.0, None, ALU.mult).then_inc(s_exp_in, 1)
            dve.wait_ge(s_exp, 1)
            op(dve.reciprocal(soft_s[:, 3:4], soft_s[:, 2:3]))
            op(dve.tensor_scalar(soft[:, 2, :], soft[:, 1, :], soft_s[:, 3:4], None, ALU.mult))
            dve.sem_inc(s_ready, 1)
            dve.sem_inc(s_freed[(turned.n - 1) % 2], 1)
            bank = read()
            op(dve.tensor_copy(gates[:, 2, :], bank[:, 0:IMAGES]))
            dve.sem_inc(s_freed[(turned.n - 1) % 2], 1)

            def gate(b):
                dve.scalar_tensor_tensor(state[b][:], work[b][:], gates[:, 2, b:b + 1], state[b][:],
                                         ALU.mult, ALU.add).then_inc(s_state, 1)

            def one_hot(k):
                op(dve.tensor_reduce(top[:, 1, :], zb[:], AX.X, ALU.max))
                op(dve.tensor_tensor(chosen[:, k, :, :].rearrange("p e t -> p t e"), zb[:],
                                     bc(top[:, 1, :].unsqueeze(2), [P, BLOCKS, EXPERTS]), ALU.is_equal))

            def route(u):
                layer, b = divmod(u, IMAGES)
                hot = u % 2
                full = [P, BLOCKS, EXPERTS]
                ranks = bc(rank_no[:].unsqueeze(1), full)
                to_tokens(b)
                token_stats(1e-5)
                dve.wait_ge(s_acc, u + 1)
                op(dve.tensor_tensor(z[:], acc_ps[:, 0:BLOCKS * EXPERTS].rearrange("p (t e) -> p t e", e=EXPERTS),
                                     bc(rstd[:].unsqueeze(2), full), ALU.mult))
                dve.sem_inc(s_acc_free, 1)
                op(dve.tensor_tensor(z[:], z[:], bc(router_b[:, layer, :].unsqueeze(1), full), ALU.add))
                op(dve.tensor_reduce(top[:, 0, :], z[:], AX.X, ALU.max))
                op(dve.tensor_tensor(za[:], z[:], bc(top[:, 0, :].unsqueeze(2), full), ALU.subtract))
                dve.sem_inc(s_exp_in, 1)
                op(dve.scalar_tensor_tensor(zb[:], za[:], 0.0, ranks, ALU.is_ge, ALU.mult))
                one_hot(0)
                first = chosen[:, 0, :, :].rearrange("p e t -> p t e")
                op(dve.scalar_tensor_tensor(z[:], first, -3.0e38, z[:], ALU.mult, ALU.add))
                op(dve.tensor_reduce(top[:, 1, :], z[:], AX.X, ALU.max))
                op(dve.tensor_tensor(zb[:], z[:], bc(top[:, 1, :].unsqueeze(2), full), ALU.is_ge))
                op(dve.tensor_tensor(zb[:], zb[:], ranks, ALU.mult))
                one_hot(1)
                dve.tensor_tensor(chosen_any[:], chosen[:, 0, :, :], chosen[:, 1, :, :], ALU.add).then_inc(s_ready, 1)
                bank = read()
                op(dve.tensor_copy(prefix[:].rearrange("p e t -> p (e t)"), bank[:, 0:EXPERTS * BLOCKS]))
                dve.sem_inc(s_freed[(turned.n - 1) % 2], 1)
                bank = read()
                op(dve.tensor_copy(total[:].rearrange("p e t -> p (e t)"), bank[:, 0:EXPERTS * BLOCKS]))
                dve.sem_inc(s_freed[(turned.n - 1) % 2], 1)
                op(dve.tensor_tensor_scan(upto[:].rearrange("p e t -> p (e t)"), resets[:].rearrange("p e t -> p (e t)"),
                                          total[:].rearrange("p e t -> p (e t)"), 0.0, ALU.mult, ALU.add))
                counts = upto[:, :, BLOCKS - 1]
                op(dve.tensor_scalar(n_tiles_i[:], counts, float(SLOTS - 1), None, ALU.add))
                op(dve.tensor_scalar(n_tiles_i[:], n_tiles_i[:], SLOTS.bit_length() - 1, None, ALU.logical_shift_right))
                op(dve.tensor_copy(n_tiles[:, 0, :], n_tiles_i[:]))
                op(dve.memset(n_tiles[:, 1, :], 1.0))
                op(dve.tensor_tensor_scan(n_tiles[:, 2, :], n_tiles[:, 1, :], n_tiles[:, 0, :], 0.0, ALU.mult, ALU.add))
                op(dve.tensor_tensor(n_tiles[:, 3, :], n_tiles[:, 2, :], n_tiles[:, 0, :], ALU.subtract))
                op(dve.tensor_scalar(n_tiles[:, 3, :], n_tiles[:, 3, :], float(SLOTS), None, ALU.mult))
                op(dve.tensor_tensor(upto[:], upto[:], total[:], ALU.subtract))
                op(dve.tensor_tensor(upto[:], upto[:], prefix[:], ALU.add))
                op(dve.tensor_tensor(upto[:], upto[:], bc(n_tiles[:, 3, :].unsqueeze(2), [P, EXPERTS, BLOCKS]), ALU.add))
                for k in range(CHOICES):
                    op(dve.tensor_tensor(total[:], upto[:], chosen[:, k, :, :], ALU.mult))
                    op(dve.tensor_reduce(place[:, 0, :], total[:].rearrange("p e t -> p t e"), AX.X, ALU.add))
                    op(dve.tensor_copy(place_i[:, 0, :], place[:, 0, :]))
                    op(dve.tensor_scalar(place_i[:, 1, :], place_i[:, 0, :], P - 1, None, ALU.bitwise_and))
                    op(dve.tensor_scalar(place_i[:, 2, :], place_i[:, 0, :], P.bit_length() - 1, None,
                                         ALU.logical_shift_right))
                    op(dve.tensor_copy(place_b[:], place_i[:, 1:3, :]))
                    if u or k:
                        dve.wait_ge(s_hot_used, u * CHOICES + k)
                    n = TILES * HALVES
                    dve.tensor_tensor(hot_lane, lane[:], bc(place_b[:, 0, :].unsqueeze(1), [P, P, BLOCKS]),
                                      ALU.is_equal)
                    op(dve.tensor_tensor(hot_block[:, 0, :, :], block_no[:],
                                         bc(place_b[:, 1, :].unsqueeze(1), [P, n, BLOCKS]), ALU.is_equal))
                    op(dve.tensor_tensor(hot_block[:, 1, :, :], hot_block[:, 0, :, :],
                                         bc(row_lo[:].unsqueeze(1), [P, n, BLOCKS]), ALU.mult))
                    dve.tensor_scalar(hot_block[:, 0, :, :], hot_block[:, 0, :, :], row_hi[:, k:k + 1], None,
                                      ALU.mult).then_inc(s_hot, 1)
                if u:
                    dve.wait_ge(s_xn_st[u - 1], 16)
                normalise(tok[b], work_tok[0], False)
                dve.sem_inc(s_xn, 1)
                dve.wait_ge(s_exp, u + 2)
                op(dve.tensor_reduce(top[:, 2, :], prob[:], AX.X, ALU.add))
                op(dve.reciprocal(top[:, 2, :], top[:, 2, :]))
                op(dve.tensor_tensor(prob[:], prob[:], bc(top[:, 2, :].unsqueeze(2), full), ALU.mult))
                for k in range(CHOICES):
                    op(dve.tensor_tensor(za[:], prob[:], chosen[:, k, :, :].rearrange("p e t -> p t e"), ALU.mult))
                    op(dve.tensor_reduce(share[b][:, k, :], za[:], AX.X, ALU.add))
                if layer == 0:
                    op(dve.tensor_tensor(top[:, 3, :], share[b][:, 0, :], share[b][:, 1, :], ALU.add))
                    op(dve.reciprocal(top[:, 3, :], top[:, 3, :]))
                    op(dve.tensor_tensor(share[b][:], share[b][:], bc(top[:, 3, :].unsqueeze(1), [P, CHOICES, BLOCKS]),
                                         ALU.mult))
                op(dve.tensor_tensor(tile_cmp[:], bc(n_tiles[:, 2, :].unsqueeze(1), [P, TILES, EXPERTS]),
                                     bc(tile_no[:].unsqueeze(2), [P, TILES, EXPERTS]), ALU.is_le))
                op(dve.tensor_reduce(tile_e[:], tile_cmp[:], AX.X, ALU.add))
                op(dve.tensor_scalar(tile_e[:], tile_e[:], float(EXPERTS - 1), None, ALU.min))
                op(dve.tensor_copy(tile_expert[hot][:], tile_e[:]))
                op(dve.tensor_tensor(tile_cmp[:], bc(tile_e[:].unsqueeze(2), [P, TILES, EXPERTS]),
                                     bc(expert_no[:].unsqueeze(1), [P, TILES, EXPERTS]), ALU.is_equal))
                for c in range(BIAS):
                    op(dve.tensor_tensor(bias_mul[:], tile_cmp[:],
                                         bc(bias[layer][:, c, :].unsqueeze(1), [P, TILES, EXPERTS]), ALU.mult))
                    op(dve.tensor_reduce(tile_bias[hot][:, :, c], bias_mul[:], AX.X, ALU.add))
                dve.wait_ge(s_hot_used, (u + 1) * CHOICES)
                n = TILES * HALVES
                op(dve.tensor_copy(rows_f[:, 0:2, :], acc_ps[:, 0:2 * n].rearrange("p (a q) -> p a q", a=2)))
                dve.sem_inc(s_acc_free, 1)
                op(dve.tensor_tensor(rows_f[:, 0, :], rows_f[:, 0, :], rows_f[:, 1, :], ALU.add))
                op(dve.tensor_scalar(rows_f[:, 1, :], rows_f[:, 0, :], 0.0, float(EMPTY), ALU.is_equal, ALU.mult))
                op(dve.scalar_tensor_tensor(rows_f[:, 0, :], rows_f[:, 0, :], -1.0, rows_f[:, 1, :], ALU.add, ALU.add))
                op(dve.tensor_copy(tile_rows[hot][:, :, 1, :], rows_f[:, 0, :].rearrange("p (j h) -> p j h", h=HALVES)))
                op(dve.tensor_scalar(rows_f[:, 1, :], rows_f[:, 0, :], float(TOKENS), -float(TOKENS), ALU.is_ge, ALU.mult))
                op(dve.tensor_tensor(rows_f[:, 1, :], rows_f[:, 1, :], rows_f[:, 0, :], ALU.add))
                op(dve.tensor_scalar(tile_rows[hot][:, :, 0, :], rows_f[:, 1, :].rearrange("p (j h) -> p j h", h=HALVES),
                                     float(TOKENS - 1), None, ALU.min))
                dve.sem_inc(s_table, 1)

            def combine(u):
                b = u % IMAGES
                dve.wait_ge(s_y_in[u], 16 * CHOICES)
                for k in range(CHOICES):
                    last = k == CHOICES - 1 and u >= IMAGES
                    for t in range(BLOCKS):
                        ins = dve.scalar_tensor_tensor(tok[b][:, t, :], work_tok[1 + k][:, t, :],
                                                       share[b][:, k, t:t + 1], tok[b][:, t, :], ALU.mult, ALU.add)
                        if last and t % GROUP == GROUP - 1:
                            ins.then_inc(s_ln, 1)
                    if not last:
                        op(ins)

            def mix(b):
                for t in range(BLOCKS):
                    ins = dve.bn_stats(stats[:, t, :], tok[b][:, t, :])
                op(ins)
                token_stats(1e-6)
                dve.wait_ge(s_xn_st[1 + b], 16)
                normalise(tok[b], work_tok[0], True)
                to_channels(work[1])
                for g in range(GROUPS):
                    ap = tok[b][:, g * GROUP:(g + 1) * GROUP, :]
                    dve.tensor_tensor(ap, ap, work_tok[0][:, g * GROUP:(g + 1) * GROUP, :], ALU.add).then_inc(s_ln, 1)
                to_channels(state[b])
                op(dve.tensor_reduce(gap[:], work[1][:], AX.X, ALU.add))
                dve.tensor_scalar(gap[:], gap[:], 1.0 / TOKENS, None, ALU.mult).then_inc(s_ready, 1)
                bank = read()
                op(dve.tensor_scalar(mix_h[:], bank[0:EXPERTS, 0:1], mix_b1[:], 0.0, ALU.add, ALU.max))
                dve.sem_inc(s_freed[(turned.n - 1) % 2], 1)
                dve.sem_inc(s_ready, 1)
                bank = read()
                op(dve.tensor_scalar(mix_s[:, 0:1], bank[:, 0:1], mix_b2[:], 0.0, ALU.add, ALU.max))
                dve.sem_inc(s_freed[(turned.n - 1) % 2], 1)
                op(dve.tensor_scalar(mix_hot[:, 0, :], step_no[:], mix_s[:, 0:1], None, ALU.is_le))
                op(dve.tensor_reduce(mix_s[:, 1:2], mix_hot[:, 0, 1:KERNELS - 1], AX.X, ALU.add))
                op(dve.tensor_tensor(mix_s[:, 2:3], mix_s[:, 0:1], mix_s[:, 1:2], ALU.subtract))
                op(dve.tensor_scalar(mix_s[:, 3:4], mix_s[:, 1:2], 1.0, mix_s[:, 0:1], ALU.add, ALU.subtract))
                op(dve.tensor_scalar(mix_hot[:, 0, :], step_no[:], mix_s[:, 1:2], mix_s[:, 3:4], ALU.is_equal, ALU.mult))
                op(dve.tensor_scalar(mix_hot[:, 1, :], step_no[:], -1.0, mix_s[:, 1:2], ALU.add, ALU.is_equal))
                op(dve.tensor_scalar(mix_hot[:, 1, :], mix_hot[:, 1, :], mix_s[:, 2:3], None, ALU.mult))
                op(dve.tensor_tensor(mix_hot[:, 0, :], mix_hot[:, 0, :], mix_hot[:, 1, :], ALU.add))
                op(dve.scalar_tensor_tensor(state[b][:], work[1][:], mix_hot[:, 0, 0:1], state[b][:], ALU.mult, ALU.add))
                pool_in = work[1][:].rearrange("p (h w) -> p h w", h=SIDE)
                across = work[2][:].rearrange("p (h w) -> p h w", h=SIDE)
                last, edge = SIDE - 1, SIDE - 2

                def grow(k):
                    dve.tensor_tensor(across[:, :, 1:last], pool_in[:, :, 0:edge], pool_in[:, :, 2:SIDE], ALU.max)
                    op(dve.tensor_copy(across[:, :, 0:SIDE:last], pool_in[:, :, 1:last:edge - 1]))
                    if k == 1:
                        op(dve.tensor_tensor(across, across, pool_in, ALU.max))
                    dve.tensor_tensor(pool_in[:, 1:last, :], across[:, 0:edge, :], across[:, 2:SIDE, :], ALU.max)
                    op(dve.tensor_copy(pool_in[:, 0:SIDE:last, :], across[:, 1:last:edge - 1, :]))
                    if k == 1:
                        op(dve.tensor_tensor(pool_in, across, pool_in, ALU.max))
                    ins = dve.scalar_tensor_tensor(state[b][:], work[1][:], mix_hot[:, 0, k:k + 1], state[b][:],
                                                   ALU.mult, ALU.add)
                    op(ins)
                for k in range(1, KERNELS):
                    grow(k)
                dve.sem_inc(s_state, 1)

            for b in range(IMAGES):
                gate(b)
                route(b)
            dve.sem_inc(s_buf, 1)
            for b in range(IMAGES):
                combine(b)
                mix(b)
                dve.sem_inc(s_buf, 1)
                route(2 + b)
            for b in range(IMAGES):
                combine(2 + b)
                to_channels(state[b])
                dve.sem_inc(s_out, 1)
                if b == 0:
                    dve.sem_inc(s_buf, 1)


_INS = ['x', 'L0_conv_w1', 'L0_conv_w2', 'L0_conv_g1', 'L0_conv_b1', 'L0_conv_g2', 'L0_conv_b2', 'L0_conv_lw1',
        'L0_conv_lb1', 'L0_conv_lw2', 'L0_conv_lb2', 'L0_ffn_Wr', 'L0_ffn_br', 'L0_ffn_W1', 'L0_ffn_b1', 'L0_ffn_W2',
        'L0_ffn_b2', 'L1_conv_w1', 'L1_conv_b1', 'L1_conv_w2', 'L1_conv_b2', 'L1_ffn_gate_w', 'L1_ffn_gate_b',
        'L1_ffn_w1', 'L1_ffn_b1', 'L1_ffn_w2', 'L1_ffn_b2']


def kernel(**inputs):
    import concourse.bacc as bacc
    from concourse.bass_utils import run_bass_kernel_spmd

    nc = bacc.Bacc("TRN2", target_bir_lowering=False, num_devices=1)
    arrays, args = {}, {}
    for name in _INS:
        a = np.ascontiguousarray(inputs[name])
        arrays[f"in_{name}"] = a
        args[name] = nc.dram_tensor(f"in_{name}", a.shape, mybir.dt.from_np(a.dtype), kind="ExternalInput").ap()
    out = nc.dram_tensor("out_0", (IMAGES, P, SIDE, SIDE), F32, kind="ExternalOutput").ap()
    build(nc, out=out, **args)
    r = run_bass_kernel_spmd(nc, [arrays], core_ids=[0])
    return r.results[0]["out_0"]
```

```python
from contextlib import ExitStack, contextmanager

import numpy as np

import concourse.bass as bass
from concourse import mybir

ALU = mybir.AluOpType
ACT = mybir.ActivationFunctionType
AX = mybir.AxisListType
F32 = mybir.dt.float32
BF16 = mybir.dt.bfloat16
I32 = mybir.dt.int32
U32 = mybir.dt.uint32

P = 128
IMAGES, SIDE = 2, 64
TOKENS = SIDE * SIDE
BLOCKS = TOKENS // P
GROUP = 4
GROUPS = BLOCKS // GROUP
EXPERTS, CHOICES, HIDDEN = 8, 2, 512
CHUNKS = HIDDEN // P
PAIRS = CHOICES * TOKENS
SLOTS = 256
HALVES = SLOTS // P
TILES = (PAIRS - EXPERTS) // SLOTS + EXPERTS
EMPTY = 2 * PAIRS
RING = 4
QUARTERS = 4
KERNELS = 7
UNITS = 4
BIAS = CHUNKS + 1
PEEL = 7
W_AHEAD = 3
G_AHEAD = 4
AHEAD = G_AHEAD + 1

RUNS = [(0, 1), (2,), (3,)]

WHEN = [
    [(8, "route_turn", 1, 0), (9, "route_turn", 1, 1), (10, "route_products", 1, 0), (11, "route_products", 1, 1),
     (14, "route_slots", 1), (14, "route_exp", 1), (15, "route_rows", 1, 0), (17, "route_rows", 1, 1),
     (19, "route_rows", 1, 2), (21, "route_rows", 1, 3), (21, "route_store", 1), (26, "route_invert", 1, 0),
     (30, "route_invert", 1, 1)],
    [(2, "outputs", 0, 0, 1), (4, "outputs", 0, 2, 3), (7, "mix_state", 0), (9, "mix_norm", 0), (10, "mix_score", 0),
     (33, "route_turn", 2, 0), (35, "route_turn", 2, 1), (35, "route_products", 2, 0), (35, "route_products", 2, 1),
     (35, "route_rows", 2, 0), (36, "route_rows", 2, 1), (37, "route_slots", 2), (37, "route_rows", 2, 2),
     (38, "route_rows", 2, 3), (39, "route_exp", 2), (39, "route_invert", 2, 0), (39, "route_invert", 2, 1)],
    [(0, "route_store", 2), (0, "outputs", 1, 0, 1), (0, "first_gathers", 2), (0, "outputs", 1, 2, 3),
     (5, "mix_state", 1), (8, "mix_norm", 1), (10, "mix_score", 1), (33, "route_turn", 3, 0),
     (33, "route_turn", 3, 1), (33, "route_products", 3, 0), (33, "route_products", 3, 1), (34, "route_rows", 3, 0),
     (35, "route_rows", 3, 1), (36, "route_slots", 3), (36, "route_rows", 3, 2), (37, "route_rows", 3, 3),
     (39, "route_exp", 3), (39, "route_invert", 3, 0), (39, "route_invert", 3, 1)],
    [(0, "route_store", 3), (8, "outputs", 2, 0), (10, "outputs", 2, 1), (12, "outputs", 2, 2), (14, "outputs", 2, 3),
     (20, "last_turn", 0), (24, "last_store", 0), (39, "outputs", 3, 0, 1, 2, 3), (39, "last_turn", 1),
     (39, "last_store", 1)],
]


class Count:

    def __init__(self, sem=None, eng=None, start=0):
        self.sem, self.eng, self.n, self.x = sem, eng, start, None

    def value(self, back=0):
        n = self.n - back
        return n if self.x is None else self.x + n

    def step(self, ins=None):
        self.n += 1
        if ins is not None:
            ins.then_inc(self.sem, 1)

    def wait(self, back=0):
        self.eng.wait_ge(self.sem, self.value(back))


@contextmanager
def rounds(eng, times, *counts):
    first = [c.n for c, _ in counts]
    with eng.Fori(0, times) as i:
        for c, per in counts:
            c.x = i * per
        yield i
    for (c, per), n in zip(counts, first):
        assert c.n - n == per, (c.sem, c.n - n, per)
        c.x, c.n = None, n + per * times


class Tile:

    def __init__(self, unit, j, i=None):
        self.s, self.i = unit * TILES + j, i
        run = next(r for r in RUNS if unit in r)
        self.first, self.last = run[0] * TILES, (run[-1] + 1) * TILES - 1
        self.loop_unit, self.loop_at = unit, j

    def at(self, d=0):
        if self.i is not None:
            return self.loop_unit, self.i * RING + (self.loop_at + d)
        return divmod(self.s + d, TILES)

    def has(self, d=0):
        return self.i is not None or self.first <= self.s + d <= self.last

    def old(self, d):
        return self.s + d >= 0

    def done(self, d=0, per=1, part=None):
        n = (self.s + d) * per + (per if part is None else part)
        return n if self.i is None else self.i * (RING * per) + n

    def slot(self, n, d=0):
        return (self.s + d) % n

    def landed(self, d=0, each=1):
        n = ((self.s + d) // RING + 1) * 16 * each
        return n if self.i is None else self.i * (16 * each) + n


def tile_steps(eng, unit, step, between):
    def insert(j):
        if j in between:
            between[j]()

    j = 0
    while j < TILES + 2 * ends_run(unit):
        if j < TILES:
            insert(j)
        end = min([p for p in between if p > j] + [TILES - AHEAD])
        if j >= PEEL and end - j >= 2 * RING:
            times = (end - j) // RING
            with eng.Fori(0, times) as i:
                for k in range(RING):
                    step(Tile(unit, j + k, i))
            j += times * RING
        else:
            step(Tile(unit, j))
            j += 1
    insert(TILES)


def begins_run(u):
    return any(u == r[0] for r in RUNS)


def ends_run(u):
    return any(u == r[-1] for r in RUNS)


def plan(u, **work):
    found = {}
    for at, name, *args in WHEN[u]:
        if name in work:
            before = found.get(at)
            found[at] = (lambda before=before, f=work[name], args=args: (before and before(), f(*args)))
    return found


def build(nc, x, L0_conv_w1, L0_conv_w2, L0_conv_g1, L0_conv_b1, L0_conv_g2, L0_conv_b2, L0_conv_lw1, L0_conv_lb1,
          L0_conv_lw2, L0_conv_lb2, L0_ffn_Wr, L0_ffn_br, L0_ffn_W1, L0_ffn_b1, L0_ffn_W2, L0_ffn_b2, L1_conv_w1,
          L1_conv_b1, L1_conv_w2, L1_conv_b2, L1_ffn_gate_w, L1_ffn_gate_b, L1_ffn_w1, L1_ffn_b1, L1_ffn_w2,
          L1_ffn_b2, out):
    with ExitStack() as ctx:
        def sb(name, shape, dt=F32):
            return ctx.enter_context(nc.sbuf_tensor(name, shape, dt))

        def ps(name, shape, dt=F32):
            return ctx.enter_context(nc.psum_tensor(name, shape, dt))

        def sem(name):
            return ctx.enter_context(nc.semaphore(name))

        xn_rows = [nc.dram_tensor(f"xn_rows{u}", [TOKENS, P], F32).ap() for u in range(UNITS)]
        bias_rows = nc.dram_tensor("bias_rows", [2, EXPERTS, P, BIAS], F32).ap()
        y_rows = [nc.dram_tensor(f"y_rows{u}", [PAIRS, P], F32).ap() for u in range(UNITS)]

        state = [sb(f"state{b}", [P, TOKENS]) for b in range(IMAGES)]
        tok = [sb(f"tok{b}", [P, BLOCKS, P]) for b in range(IMAGES)]
        work = [sb(f"work{i}", [P, TOKENS]) for i in range(3)]
        tok_flat = [t[:].rearrange("p t c -> p (t c)") for t in tok]
        work_tok = [w[:].rearrange("p (t c) -> p t c", t=BLOCKS) for w in work]

        ident = sb("ident", [P, P])
        ones = sb("ones", [P, P], BF16)
        before = sb("before", [P, P], BF16)
        lane = sb("lane", [P, P, BLOCKS], BF16)
        block_no = sb("block_no", [P, TILES * HALVES, BLOCKS], BF16)
        tile_no = sb("tile_no", [P, TILES])
        expert_no = sb("expert_no", [P, EXPERTS])
        rank_no = sb("rank_no", [P, EXPERTS])
        resets = sb("resets", [P, EXPERTS, BLOCKS])
        row_hi = sb("row_hi", [P, CHOICES])
        row_lo = sb("row_lo", [P, BLOCKS], BF16)
        step_no = sb("step_no", [P, KERNELS])
        conv_w = sb("conv_w", [P, 2, SIDE])
        gamma = sb("gamma", [P, 2])
        beta = sb("beta", [P, 2])
        lb1 = sb("lb1", [P, 2])
        lb2 = sb("lb2", [P, 1])
        router = sb("router", [EXPERTS, 2, P])
        gate_w = sb("gate_w", [P, EXPERTS])
        router_sum = sb("router_sum", [EXPERTS, 2])
        routerT = sb("routerT", [P, 2, EXPERTS])
        router_b = sb("router_b", [P, 2, EXPERTS])
        bias = sb("bias", [P, 2, EXPERTS, BIAS])
        bias1 = [sb(f"bias1_{l}", [P, EXPERTS, CHUNKS]) for l in range(2)]
        bias2 = [sb(f"bias2_{l}", [EXPERTS, P]) for l in range(2)]
        mix_w1 = sb("mix_w1", [EXPERTS, P])
        mix_w1T = sb("mix_w1T", [P, EXPERTS])
        mix_w2 = sb("mix_w2", [P, EXPERTS])
        mix_w2T = sb("mix_w2T", [EXPERTS, P])
        mix_b1 = sb("mix_b1", [EXPERTS, 1])
        mix_b2 = sb("mix_b2", [P, 1])

        stats = sb("stats", [P, BLOCKS, 6])
        mean = sb("mean", [P, BLOCKS])
        rstd = sb("rstd", [P, BLOCKS])
        var = sb("var", [P, BLOCKS])
        shift = sb("shift", [P, BLOCKS])
        first_shift = [shift, sb("shift1", [P, BLOCKS])]
        first_rstd = [rstd, sb("rstd1", [P, BLOCKS])]
        tmp_s = sb("tmp_s", [P, BLOCKS])
        line_mul = sb("line_mul", [P, 2])
        line_add = sb("line_add", [P, 2])
        dots = sb("dots", [P, IMAGES])
        gates = sb("gates", [P, 5, IMAGES])
        soft = sb("soft", [IMAGES, 3, P])
        soft_s = sb("soft_s", [IMAGES, 4])
        hid = sb("hid", [P, 2, IMAGES])
        z = sb("z", [P, BLOCKS, EXPERTS])
        za = sb("za", [P, BLOCKS, EXPERTS])
        zb = sb("zb", [P, BLOCKS, EXPERTS])
        prob = sb("prob", [P, BLOCKS, EXPERTS])
        top = sb("top", [P, 4, BLOCKS])
        chosen = sb("chosen", [P, CHOICES, EXPERTS, BLOCKS])
        chosen_any = sb("chosen_any", [P, EXPERTS, BLOCKS], BF16)
        share = [sb(f"share{b}", [P, CHOICES, BLOCKS]) for b in range(IMAGES)]
        prefix = sb("prefix", [P, EXPERTS, BLOCKS])
        upto = sb("upto", [P, EXPERTS, BLOCKS])
        total = sb("total", [P, EXPERTS, BLOCKS])
        n_tiles = sb("n_tiles", [P, 4, EXPERTS])
        n_tiles_i = sb("n_tiles_i", [P, EXPERTS], I32)
        place = sb("place", [P, CHOICES, BLOCKS])
        place_i = sb("place_i", [P, 3, CHOICES, BLOCKS], I32)
        shared = sb("shared", [P, P * BLOCKS // 2])
        lw1, lw2, lw1T, lw2T = [shared[:, i * 2 * P:(i + 1) * 2 * P].rearrange("p (a j) -> p a j", a=2)
                                for i in range(4)]
        spread = shared[:, 8 * P:12 * P].rearrange("p (a b j) -> p a b j", a=IMAGES, b=IMAGES)
        lines = shared[:, 12 * P:14 * P].rearrange("p (k b s) -> p k b s", k=2, b=IMAGES)
        hot_blocks = sb("hot_blocks", [P, TILES * HALVES * BLOCKS])
        place_b = sb("place_b", [P, 2, CHOICES, BLOCKS], BF16)
        tile_cmp = sb("tile_cmp", [P, TILES, EXPERTS])
        tile_e = sb("tile_e", [P, TILES])
        rows_f = sb("rows_f", [P, 2, TILES * HALVES])
        tile_expert = [sb(f"tile_expert{i}", [P, TILES], I32) for i in range(2)]
        tile_rows = [sb(f"tile_rows{i}", [P, TILES, 2, HALVES]) for i in range(2)]
        gap_parts = sb("gap_parts", [P, GROUPS])
        gap = sb("gap", [P, 1])
        mix_h = sb("mix_h", [EXPERTS, 1])
        mix_s = sb("mix_s", [P, 4])
        mix_hot = sb("mix_hot", [P, 3, KERNELS])

        g_slot = sb("g_slot", [P, RING, HALVES], U32)
        s_slot = sb("s_slot", [P, RING, HALVES], U32)
        b_slot = sb("b_slot", [P, RING, BIAS])
        xg = sb("xg", [P, RING, HALVES, P])
        xT = sb("xT", [P, 2, SLOTS])
        w1s = sb("w1s", [P, RING, HIDDEN])
        w2s = sb("w2s", [P, RING, CHUNKS, P])
        hT = sb("hT", [P, 2, CHUNKS, SLOTS])
        yT = sb("yT", [P, 2, SLOTS])
        yr = sb("yr", [P, RING, HALVES, P])

        def one_hots(u, k):
            lanes = shared if k == 0 else hT if u == 0 else work[1]
            blocks = hot_blocks if k == 0 else work[2]
            if lanes is hT:
                lanes = hT[:].rearrange("p a c s -> p (a c s)")
            return (lanes[:, 0:P * BLOCKS // 2].bitcast(BF16).rearrange("p (q t) -> p q t", t=BLOCKS),
                    blocks[:, 0:TILES * HALVES * BLOCKS].bitcast(BF16).rearrange("p (a q t) -> p a q t", a=2, t=BLOCKS))

        xT_ps = ps("xT_ps", [P, 512])
        h_ps = [ps(f"h_ps{i}", [P, 2, SLOTS]) for i in range(2)]
        yT_ps = ps("yT_ps", [P, 512])
        yr_ps = ps("yr_ps", [P, 4, P])
        turn_ps = ps("turn_ps", [P, 2, 512])
        acc_ps = ps("acc_ps", [P, 512])

        s_par = sem("params_loaded")
        s_x = [[sem(f"image{b}_part{q}_loaded") for q in range(2)] for b in range(IMAGES)]
        s_const = sem("constants_made")
        s_own = sem("vector_steps")
        s_bias = sem("biases_stored")
        s_bias_in = sem("biases_gathered")
        s_turned = sem("turn_bank_filled")
        s_freed = [sem(f"turn_bank{i}_freed") for i in range(2)]
        s_acc = sem("acc_bank_filled")
        s_acc_free = sem("acc_bank_freed")
        s_ready = sem("vector_result_for_tensor")
        s_ln_odd = sem("odd_group_normalised_by_scalar")
        s_ln = sem("normalised_group_for_tensor")
        s_state = sem("state_for_tensor")
        s_exp_in = sem("exp_input_ready")
        s_exp = sem("exp_done")
        s_stats = sem("token_statistics_ready")
        s_mul = sem("product_with_conv_weights_made")
        s_mul_used = sem("product_in_work2_summed")
        s_xn = sem("normalised_rows_ready")
        s_xn_st = [sem(f"normalised_rows_stored{u}") for u in range(UNITS)]
        s_experts = sem("tile_experts_ready")
        s_rows = sem("tile_rows_ready")
        s_hot = sem("one_hots_ready")
        s_hot_used = sem("one_hots_used")
        s_g_idx = sem("gather_rows_set")
        s_gath = [sem(f"gathered{i}") for i in range(RING)]
        s_w = [sem(f"weights_loaded{i}") for i in range(RING)]
        s_xt_ps = sem("x_turned")
        s_xt_sb = sem("x_turned_copied")
        s_h_ps = sem("hidden_made")
        s_h_sb = sem("hidden_activated")
        s_y_ps = sem("expert_out_made")
        s_y_sb = sem("expert_out_copied")
        s_yr_ps = sem("out_rows_turned")
        s_yr_sb = sem("out_rows_copied")
        s_scat = [sem(f"scattered{i}") for i in range(RING)]
        s_begun = sem("indirect_dmas_begun")
        s_buf = sem("work_buffers_free")
        s_y_in = [[sem(f"outputs{u}_quarter{q}_loaded") for q in range(QUARTERS)] for u in range(UNITS)]
        s_shared = sem("last_outputs_times_shares")
        s_done = sem("output_stored")

        W1 = [L0_ffn_W1, L1_ffn_w1]
        W2 = [L0_ffn_W2, L1_ffn_w2]

        small = [
            (conv_w[:, 0, :], L0_conv_w1.rearrange("c a h b -> c (a h b)")),
            (conv_w[:, 1, :], L0_conv_w2.rearrange("c a b w -> c (a b w)")),
            (gamma[:, 0:1], L0_conv_g1.rearrange("(c a) -> c a", a=1)),
            (gamma[:, 1:2], L0_conv_g2.rearrange("(c a) -> c a", a=1)),
            (beta[:, 0:1], L0_conv_b1.rearrange("(c a) -> c a", a=1)),
            (beta[:, 1:2], L0_conv_b2.rearrange("(c a) -> c a", a=1)),
            (lw1[:, 0, :], L0_conv_lw1[0:P, :]),
            (lw1[:, 1, :], L0_conv_lw1[P:2 * P, :]),
            (lw2[:, :, :], L0_conv_lw2.rearrange("c (a j) -> c a j", a=2)),
            (lb1[:, 0:1], L0_conv_lb1[0:P].rearrange("(c a) -> c a", a=1)),
            (lb1[:, 1:2], L0_conv_lb1[P:2 * P].rearrange("(c a) -> c a", a=1)),
            (lb2[:, :], L0_conv_lb2.rearrange("(c a) -> c a", a=1)),
            (router[:, 0, :], L0_ffn_Wr),
            (gate_w[:, :], L1_ffn_gate_w),
            (router_b[:, 0, :], L0_ffn_br.partition_broadcast(P)),
            (router_b[:, 1, :], L1_ffn_gate_b.partition_broadcast(P)),
            (bias1[0][:, :, :], L0_ffn_b1.rearrange("e (p c) -> p e c", c=CHUNKS)),
            (bias1[1][:, :, :], L1_ffn_b1.rearrange("e (p c) -> p e c", c=CHUNKS)),
            (bias2[0][:, :], L0_ffn_b2),
            (bias2[1][:, :], L1_ffn_b2),
            (mix_w1[:, :], L1_conv_w1),
            (mix_w2[:, :], L1_conv_w2),
            (mix_b1[:, :], L1_conv_b1.rearrange("(c a) -> c a", a=1)),
            (mix_b2[:, :], L1_conv_b2.rearrange("(c a) -> c a", a=1)),
        ]
        IDENT, CONSTS = 2, 16

        BANKS = (4 * GROUPS + 3 + 5) + UNITS * (GROUPS + 2) + IMAGES * (2 * GROUPS + 2) + IMAGES * GROUPS

        def quarter(q):
            return slice(q * BLOCKS // QUARTERS, (q + 1) * BLOCKS // QUARTERS)

        def banks_read(eng, n):
            for i in range(2):
                eng.wait_ge(s_freed[i], (n + 1 - i) // 2 + 1)

        block = ctx.enter_context(nc.Block())

        @block.sync
        def _(sp):
            def load_weights(t, d):
                unit, at = t.at(d)
                layer, i = divmod(unit, IMAGES)
                if t.old(d - RING):
                    sp.wait_ge(s_y_sb, t.done(d - RING))
                e = sp.value_load(tile_expert[i][0:1, bass.ds(at, 1)], min_val=0, max_val=EXPERTS - 1)
                s = t.slot(RING, d)
                sp.dma_start(w1s[:, s, :], W1[layer][bass.ds(e, 1)].rearrange("a d f -> (a d) f")) \
                    .then_inc(s_w[s], 16)
                sp.dma_start(b_slot[:, s, :], bias_rows[layer][bass.ds(e, 1)].rearrange("a p n -> (a p) n")) \
                    .then_inc(s_w[s], 16)
                sp.dma_start(w2s[:, s, :, :], W2[layer][bass.ds(e, 1)].rearrange("a (p c) d -> (a p) c d", c=CHUNKS)) \
                    .then_inc(s_w[s], 16)

            def store_normalised(u):
                for q in range(QUARTERS):
                    sp.wait_ge(s_xn, u * QUARTERS + q + 1)
                    sp.dma_start(xn_rows[u].rearrange("(p t) c -> p t c", t=BLOCKS)[:, quarter(q), :],
                                 work_tok[0][:, quarter(q), :]).then_inc(s_xn_st[u], 16)

            def first_gathers(u):
                t = Tile(u, 0)
                for d in range(G_AHEAD):
                    sp.wait_ge(s_gath[t.slot(RING, d)], t.landed(d, HALVES))

            def load_outputs(u, *quarters):
                if quarters[0] == 0:
                    last = Tile(u, TILES - 1)
                    for d in range(RING):
                        sp.wait_ge(s_scat[last.slot(RING, -d)], last.landed(-d, HALVES))
                    sp.wait_ge(s_buf, u + 1)
                for q in quarters:
                    for k in range(CHOICES):
                        sp.dma_start(work_tok[1 + k][:, quarter(q), :],
                                     y_rows[u].rearrange("(k p t) c -> k p t c", k=CHOICES, t=BLOCKS)[k][:, quarter(q), :]) \
                            .then_inc(s_y_in[u][q], 16)

            def store_image(b):
                for q in range(QUARTERS):
                    part = slice(q * TOKENS // QUARTERS, (q + 1) * TOKENS // QUARTERS)
                    banks_read(sp, BANKS - (IMAGES - b) * GROUPS + (q + 1) * GROUPS // QUARTERS)
                    sp.dma_start(out[b].rearrange("c h w -> c (h w)")[:, part], state[b][:, part]).then_inc(s_done, 16)

            def weights(u):
                if begins_run(u):
                    sp.wait_ge(s_experts, u + 1)
                    for d in range(W_AHEAD):
                        load_weights(Tile(u, 0), d)

                def step(t):
                    if t.has(W_AHEAD):
                        if t.i is None and t.at(W_AHEAD) == (u + 1, 0):
                            sp.wait_ge(s_experts, u + 2)
                        load_weights(t, W_AHEAD)
                tile_steps(sp, u, step, plan(u, route_store=store_normalised, first_gathers=first_gathers, outputs=load_outputs,
                                             last_store=store_image))

            for b in range(IMAGES):
                for q in range(2):
                    h = TOKENS // 2
                    sp.dma_start(state[b][:, q * h:(q + 1) * h],
                                 x[b].rearrange("c h w -> c (h w)")[:, q * h:(q + 1) * h]).then_inc(s_x[b][q], 16)
            for to, source in small:
                sp.dma_start(to, source).then_inc(s_par, 16)
            sp.wait_ge(s_bias_in, 1)
            sp.dma_start(bias_rows.rearrange("l e p n -> p l e n"), bias[:]).then_inc(s_bias, 16)
            store_normalised(0)
            sp.wait_ge(s_bias, 16)
            for u in range(UNITS):
                weights(u)
            sp.wait_ge(s_done, 16 * QUARTERS * IMAGES)

        @block.gpsimd
        def _(pool):
            big = dict(allow_small_or_imprecise_dtypes=True)
            pool.memset(ident[:], 0.0).then_inc(s_const, 1)
            pool.wait_ge(s_const, 1)
            pool.affine_select(out=ident[:], in_=ident[:], compare_op=ALU.not_equal, fill=1.0, base=0,
                               pattern=[[-1, P]], channel_multiplier=1).then_inc(s_const, 1)
            pool.memset(ones[:], 1.0).then_inc(s_const, 1)
            pool.memset(spread, 0.0).then_inc(s_const, 1)
            pool.memset(resets[:], 1.0).then_inc(s_const, 1)
            pool.wait_ge(s_const, IDENT + 3)
            pool.affine_select(out=before[:], in_=ones[:], compare_op=ALU.is_ge, fill=0.0, base=-1,
                               pattern=[[1, P]], channel_multiplier=-1).then_inc(s_const, 1)
            pool.affine_select(out=spread, in_=spread, compare_op=ALU.not_equal, fill=1.0, base=0,
                               pattern=[[P, IMAGES], [-1, IMAGES], [1, P]], channel_multiplier=-2).then_inc(s_const, 1)
            pool.memset(resets[:, :, 0:1], 0.0).then_inc(s_const, 1)
            pool.iota(lane[:], [[1, P], [0, BLOCKS]], base=0, channel_multiplier=0, **big).then_inc(s_const, 1)
            pool.iota(block_no[:], [[1, TILES * HALVES], [0, BLOCKS]], base=0, channel_multiplier=0, **big).then_inc(s_const, 1)
            pool.iota(tile_no[:], [[1, TILES]], base=0, channel_multiplier=0, **big).then_inc(s_const, 1)
            pool.iota(row_hi[:], [[TOKENS, CHOICES]], base=0, channel_multiplier=BLOCKS, **big).then_inc(s_const, 1)
            pool.iota(row_lo[:], [[1, BLOCKS]], base=1, channel_multiplier=0, **big).then_inc(s_const, 1)
            pool.iota(rank_no[:], [[-1, EXPERTS]], base=EXPERTS, channel_multiplier=0, **big).then_inc(s_const, 1)
            pool.iota(expert_no[:], [[1, EXPERTS]], base=0, channel_multiplier=0, **big).then_inc(s_const, 1)
            pool.iota(step_no[:], [[1, KERNELS]], base=0, channel_multiplier=0, **big).then_inc(s_const, 1)

            pool.wait_ge(s_par, 16 * len(small))
            for b in range(IMAGES):
                banks_read(pool, (3 + b) * GROUPS)
                img, by_h = (m.rearrange("p (h w) -> p h w", h=SIDE) for m in (work[b][:], tok_flat[b]))
                pool.tensor_tensor(by_h, img, conv_w[:, 0, :].unsqueeze(2).to_broadcast([P, SIDE, SIDE]), ALU.mult) \
                    .then_inc(s_mul, 1)
            pool.wait_ge(s_mul_used, 1)
            pool.tensor_tensor(work[2][:].rearrange("p (h w) -> p h w", h=SIDE), img,
                               conv_w[:, 1, :].unsqueeze(1).to_broadcast([P, SIDE, SIDE]), ALU.mult).then_inc(s_mul, 1)

            def gather(t, d):
                s = t.slot(RING, d)
                pool.wait_ge(s_g_idx, t.done(d))
                pool.sem_inc(s_begun, 1)
                for h in range(HALVES):
                    pool.indirect_dma_start(xg[:, s, h, :], None, xn_rows[t.at(d)[0]],
                                            bass.IndirectOffsetOnAxis(ap=g_slot[:, s, h:h + 1], axis=0)) \
                        .then_inc(s_gath[s], 16)

            def scatter(t, d):
                s = t.slot(RING, d)
                pool.wait_ge(s_yr_sb, t.done(d))
                pool.sem_inc(s_begun, 1)
                for h in range(HALVES):
                    pool.indirect_dma_start(y_rows[t.at(d)[0]],
                                            bass.IndirectOffsetOnAxis(ap=s_slot[:, s, h:h + 1], axis=0),
                                            yr[:, s, h, :], None, bounds_check=PAIRS - 1, oob_is_err=False) \
                        .then_inc(s_scat[s], 16)

            for u in range(UNITS):
                if begins_run(u):
                    pool.wait_ge(s_xn_st[u], 16 * QUARTERS)
                    for d in range(G_AHEAD):
                        gather(Tile(u, 0), d)

                def step(t):
                    if t.has(G_AHEAD):
                        if t.i is None and t.at(G_AHEAD) == (u + 1, 0):
                            pool.wait_ge(s_xn_st[u + 1], 16 * QUARTERS)
                        gather(t, G_AHEAD)
                    if t.has(-2):
                        scatter(t, -2)
                tile_steps(pool, u, step, plan(u))

            for q in range(QUARTERS):
                pool.wait_ge(s_y_in[UNITS - 1][q], 16 * CHOICES)
                rows = work_tok[CHOICES][:, quarter(q), :]
                pool.tensor_tensor(rows, rows, share[(UNITS - 1) % IMAGES][:, CHOICES - 1, quarter(q)].unsqueeze(2)
                                   .to_broadcast([P, BLOCKS // QUARTERS, P]), ALU.mult).then_inc(s_shared, 1)

        @block.scalar
        def _(act):
            turned = Count(s_turned, act)

            def next_bank():
                s = turned.n % 2
                turned.step()
                turned.wait()
                return s, turn_ps[:, s, :]

            def to_tokens(b, *parts):
                for g in [g for part in parts for g in range(part * GROUPS // 2, (part + 1) * GROUPS // 2)]:
                    s, bank = next_bank()
                    act.activation(tok[b][:, g * GROUP:(g + 1) * GROUP, :], bank.rearrange("p (t c) -> p t c", t=GROUP),
                                   ACT.Copy).then_inc(s_freed[s], 1)

            def copy_group(dst, g, sums=None):
                s, bank = next_bank()
                more = {} if sums is None else dict(accum_out=sums[:, g:g + 1])
                act.activation(dst[:, g * 512:(g + 1) * 512], bank, ACT.Copy, **more).then_inc(s_freed[s], 1)

            def to_channels(dst, sums=None):
                for g in range(GROUPS):
                    copy_group(dst, g, sums)

            def set_gather(t, d):
                unit, at = t.at(d)
                act.activation(g_slot[:, t.slot(RING, d), :], tile_rows[unit % 2][:, bass.ds(at, 1), 0, :]
                               .rearrange("p a h -> p (a h)"), ACT.Copy).then_inc(s_g_idx, 1)

            def copy_x(t, d):
                act.wait_ge(s_xt_ps, t.done(d))
                if t.old(d - 2):
                    act.wait_ge(s_h_ps, t.done(d - 2, 2))
                act.activation(xT[:, t.slot(2, d), :], xT_ps[:, 0:SLOTS], ACT.Copy).then_inc(s_xt_sb, 1)

            def activate(t):
                s = t.slot(2)
                unit, at = t.at()
                if t.old(-2):
                    act.wait_ge(s_y_ps, t.done(-2))
                func = ACT.Gelu if unit // IMAGES else ACT.Gelu_apprx_tanh
                for c in range(CHUNKS):
                    if c % 2 == 0:
                        act.wait_ge(s_h_ps, t.done(0, 2, c // 2 + 1))
                    ins = act.activation(hT[:, s, c, :], h_ps[c // 2][:, c % 2, :], func,
                                         bias=b_slot[:, t.slot(RING), c:c + 1])
                    if c % 2:
                        ins.then_inc(s_h_sb, 1)

            def copy_y(t, d):
                s = t.slot(2, d)
                act.wait_ge(s_y_ps, t.done(d))
                if t.old(d - 2):
                    act.wait_ge(s_yr_ps, t.done(d - 2))
                act.activation(yT[:, s, :], yT_ps[:, 0:SLOTS], ACT.Identity, 
                               bias=b_slot[:, t.slot(RING, d), CHUNKS:BIAS]) \
                    .then_inc(s_y_sb, 1)

            def copy_rows(t, d):
                s = t.slot(RING, d)
                unit, at = t.at(d)
                if t.old(d - RING):
                    act.wait_ge(s_scat[s], t.landed(d - RING, HALVES))
                act.activation(s_slot[:, s, :], tile_rows[unit % 2][:, bass.ds(at, 1), 1, :]
                               .rearrange("p a h -> p (a h)"), ACT.Copy)
                act.wait_ge(s_yr_ps, t.done(d))
                act.activation(yr[:, s, :, :], yr_ps[:, 0:HALVES, :], ACT.Copy).then_inc(s_yr_sb, 1)

            def route_exp(u):
                act.wait_ge(s_exp_in, 2 + u)
                act.activation(prob[:], za[:], ACT.Exp).then_inc(s_exp, 1)
                turned.n += 2

            def route_turn(u, *parts):
                to_tokens(u % IMAGES, *parts)

            def route_rows(u, *parts):
                if parts[0] == 0:
                    if u:
                        act.wait_ge(s_xn_st[u - 1], 16 * QUARTERS)
                    act.wait_ge(s_stats, IMAGES + u + 1)
                for part in parts:
                    for t in range(BLOCKS)[quarter(part)]:
                        ins = act.activation(work_tok[0][:, t, :], tok[u % IMAGES][:, t, :], ACT.Identity,
                                             bias=shift[:, t:t + 1], scale=rstd[:, t:t + 1])
                    ins.then_inc(s_xn, 1)

            def mix_state(b):
                to_channels(state[b])

            def mix_norm(b):
                to_channels(work[1], gap_parts)

            def mix_score(b):
                turned.n += 2

            def last_turn(b):
                to_channels(state[b])

            def tiles(u):
                if begins_run(u):
                    act.wait_ge(s_rows, u + 1)
                    for d in range(G_AHEAD):
                        set_gather(Tile(u, 0), d)
                    copy_x(Tile(u, 0), 0)
                    set_gather(Tile(u, 0), G_AHEAD)

                def step(t):
                    if t.has(1):
                        copy_x(t, 1)
                    if t.has(AHEAD):
                        if t.i is None and t.at(AHEAD) == (u + 1, 0):
                            act.wait_ge(s_rows, u + 2)
                        set_gather(t, AHEAD)
                    if t.has(0):
                        activate(t)
                    if t.has(-1):
                        copy_y(t, -1)
                    if t.has(-2):
                        copy_rows(t, -2)
                tile_steps(act, u, step, plan(u, route_turn=route_turn, route_exp=route_exp, mix_state=mix_state, mix_norm=mix_norm,
                                              route_rows=route_rows, mix_score=mix_score, last_turn=last_turn))

            for b in range(IMAGES):
                to_tokens(b, 0, 1)
            for b in range(IMAGES):
                act.wait_ge(s_stats, b + 1)
                for g in range(GROUPS + 1):
                    if g < GROUPS:
                        if g % 2:
                            for t in range(g * GROUP, (g + 1) * GROUP):
                                ins = act.activation(tok[b][:, t, :], tok[b][:, t, :], ACT.Identity,
                                                     bias=first_shift[b][:, t:t + 1], scale=first_rstd[b][:, t:t + 1])
                            ins.then_inc(s_ln_odd, 1)
                    if g:
                        copy_group(work[b], g - 1)
            turned.n += 3
            act.wait_ge(s_exp_in, 1)
            act.activation(soft[:, 1, :], soft[:, 0, :], ACT.Exp, bias=soft_s[:, 1:2], accum_out=soft_s[:, 2:3]) \
                .then_inc(s_exp, 1)
            turned.n += 5
            route_turn(0, 0, 1)
            route_exp(0)
            route_rows(0, *range(QUARTERS))
            for u in range(UNITS):
                tiles(u)
            assert turned.n == BANKS

        @block.tensor
        def _(pe):
            used = [0]

            def use():
                n = used[0]
                used[0] += 1
                pe.wait_ge(s_freed[n % 2], n // 2 + 1)
                return turn_ps[:, n % 2, :]

            def turn_blocks(source, group, to_tokens=True):
                bank = use()
                for k in range(GROUP):
                    t = group * GROUP + k
                    mm = pe.transpose(bank[:, k * P:(k + 1) * P], source(t), ident[:])
                mm.then_inc(s_turned, 1)

            def channel(b):
                return lambda t: state[b][:, t * P:(t + 1) * P]

            def route_turn(u, *parts):
                for part in parts:
                    pe.wait_ge(s_state, 2 * u + 1 + part)
                    for g in range(part * GROUPS // 2, (part + 1) * GROUPS // 2):
                        turn_blocks(channel(u % IMAGES), g)

            def route_products(u, *parts):
                layer, b = divmod(u, IMAGES)
                if parts[0] == 0:
                    pe.wait_ge(s_acc_free, 2 * u + 1)
                for t in [t for part in parts for t in range(part * BLOCKS // 2, (part + 1) * BLOCKS // 2)]:
                    mm = pe.matmul(acc_ps[:, t * EXPERTS:(t + 1) * EXPERTS], channel(b)(t), routerT[:, layer, :],
                                   start=True, stop=True)
                if parts[-1] == 1:
                    mm.then_inc(s_acc, 1)

            def route_slots(u):
                wait_ready()
                for lhs in (before, ones):
                    bank = use()
                    pe.matmul(bank[:, 0:EXPERTS * BLOCKS], lhs[:], chosen_any[:].rearrange("p e t -> p (e t)"),
                              start=True, stop=True).then_inc(s_turned, 1)

            def route_invert(u, k):
                pe.wait_ge(s_acc_free, 2 * u + 2)
                n = TILES * HALVES
                pe.wait_ge(s_hot, u * CHOICES + k + 1)
                hot_lane, hot_block = one_hots(u, k)
                for t in range(BLOCKS):
                    mm = pe.matmul(acc_ps[:, 0:2 * n], hot_lane[:, :, t], hot_block[:, :, :, t]
                                   .rearrange("p a q -> p (a q)"), start=(k == 0 and t == 0),
                                   stop=(k == CHOICES - 1 and t == BLOCKS - 1))
                mm.then_inc(s_hot_used, 1)

            ready = [0]

            def wait_ready():
                ready[0] += 1
                pe.wait_ge(s_ready, ready[0])

            def turn_x(t, d):
                pe.wait_ge(s_gath[t.slot(RING, d)], t.landed(d, HALVES))
                if t.old(d - 1):
                    pe.wait_ge(s_xt_sb, t.done(d - 1))
                for h in range(HALVES):
                    mm = pe.transpose(xT_ps[:, h * P:(h + 1) * P], xg[:, t.slot(RING, d), h, :], ident[:])
                mm.then_inc(s_xt_ps, 1)

            def up(t):
                pe.wait_ge(s_xt_sb, t.done())
                pe.wait_ge(s_w[t.slot(RING)], t.landed(0, 3))
                for c in range(CHUNKS):
                    if c % 2 == 0 and t.old(-1):
                        pe.wait_ge(s_h_sb, t.done(-1, 2, c // 2 + 1))
                    mm = pe.matmul(h_ps[c // 2][:, c % 2, :], w1s[:, t.slot(RING), c:HIDDEN:CHUNKS],
                                   xT[:, t.slot(2), :], start=True, stop=True)
                    if c % 2:
                        mm.then_inc(s_h_ps, 1)

            def down(t, d):
                s = t.slot(2, d)
                if t.old(d - 1):
                    pe.wait_ge(s_y_sb, t.done(d - 1))
                for c in range(CHUNKS):
                    if c % 2 == 0:
                        pe.wait_ge(s_h_sb, t.done(d, 2, c // 2 + 1))
                    mm = pe.matmul(yT_ps[:, 0:SLOTS], w2s[:, t.slot(RING, d), c, :], hT[:, s, c, :],
                                   start=(c == 0), stop=(c == CHUNKS - 1))
                mm.then_inc(s_y_ps, 1)

            def turn_y(t, d):
                s = t.slot(2, d)
                pe.wait_ge(s_y_sb, t.done(d))
                if t.old(d - 1):
                    pe.wait_ge(s_yr_sb, t.done(d - 1))
                for h in range(HALVES):
                    mm = pe.transpose(yr_ps[:, h, :], yT[:, s, h * P:(h + 1) * P], ident[:])
                mm.then_inc(s_yr_ps, 1)

            def mix_state(b):
                turn_back(lambda t: tok[b][:, t, :])

            def mix_norm(b):
                turn_back(lambda t: work_tok[0][:, t, :])

            def mix_score(b):
                wait_ready()
                bank = use()
                pe.matmul(bank[0:EXPERTS, 0:1], mix_w1T[:], gap[:], start=True, stop=True).then_inc(s_turned, 1)
                wait_ready()
                bank = use()
                pe.matmul(bank[:, 0:1], mix_w2T[:], mix_h[:], start=True, stop=True).then_inc(s_turned, 1)

            def last_turn(b):
                turn_back(lambda t: tok[b][:, t, :])

            def tiles(u):
                if begins_run(u):
                    turn_x(Tile(u, 0), 0)

                def step(t):
                    if t.has(1):
                        turn_x(t, 1)
                    if t.has(0):
                        up(t)
                    if t.has(-1):
                        down(t, -1)
                    if t.has(-2):
                        turn_y(t, -2)
                tile_steps(pe, u, step, plan(u, route_turn=route_turn, route_products=route_products,
                                             route_slots=route_slots,
                                             route_invert=route_invert, mix_state=mix_state, mix_norm=mix_norm, mix_score=mix_score,
                                             last_turn=last_turn))

            ln = [0]

            def turn_back(source, groups=range(GROUPS)):
                for g in groups:
                    ln[0] += 1
                    pe.wait_ge(s_ln, ln[0])
                    turn_blocks(source, g)

            pe.wait_ge(s_const, IDENT)
            for b in range(IMAGES):
                for g in range(GROUPS):
                    if g % (GROUPS // 2) == 0:
                        pe.wait_ge(s_x[b][g // (GROUPS // 2)], 16)
                    turn_blocks(channel(b), g)

            def turn_first(b):
                for g in range(GROUPS):
                    if g % 2:
                        pe.wait_ge(s_ln_odd, (b * GROUPS + g + 1) // 2)
                    else:
                        ln[0] += 1
                        pe.wait_ge(s_ln, ln[0])
                    turn_blocks(lambda t: tok[b][:, t, :], g)

            turn_first(0)
            turn_first(1)
            pe.wait_ge(s_par, 16 * len(small))
            bank = use()
            for j in range(2):
                pe.transpose(bank[:, j * P:(j + 1) * P], lw1[:, j, :], ident[:])
                mm = pe.transpose(bank[:, (2 + j) * P:(3 + j) * P], lw2[:, j, :], ident[:])
            mm.then_inc(s_turned, 1)
            bank = use()
            pe.transpose(bank[0:EXPERTS, 0:P], gate_w[:], ident[:])
            pe.transpose(bank[:, P:P + EXPERTS], mix_w1[:], ident[0:EXPERTS, 0:EXPERTS])
            pe.transpose(bank[0:EXPERTS, 2 * P:3 * P], mix_w2[:], ident[:])
            pe.transpose(bank[:, 3 * P:3 * P + EXPERTS], bias2[0][:], ident[0:EXPERTS, 0:EXPERTS])
            pe.transpose(bank[:, 3 * P + EXPERTS:3 * P + 2 * EXPERTS], bias2[1][:], ident[0:EXPERTS, 0:EXPERTS]) \
                .then_inc(s_turned, 1)
            wait_ready()
            bank = use()
            for layer in range(2):
                mm = pe.transpose(bank[:, layer * EXPERTS:(layer + 1) * EXPERTS], router[:, layer, :],
                                  ident[0:EXPERTS, 0:EXPERTS])
            mm.then_inc(s_turned, 1)

            pe.wait_ge(s_const, CONSTS)
            wait_ready()
            bank = use()
            for row in range(IMAGES):
                for b in range(IMAGES):
                    mm = pe.matmul(bank[:, row:row + 1], spread[:, row, b, :], dots[:, b:b + 1],
                                   start=(b == 0), stop=(b == IMAGES - 1))
            mm.then_inc(s_turned, 1)
            wait_ready()
            bank = use()
            for j in range(2):
                mm = pe.matmul(bank[:, j * IMAGES:(j + 1) * IMAGES], lw1T[:, j, :], gates[:, 0, :], start=True, stop=True)
            mm.then_inc(s_turned, 1)
            wait_ready()
            bank = use()
            for j in range(2):
                mm = pe.matmul(bank[:, 0:IMAGES], lw2T[:, j, :], hid[:, j, :], start=(j == 0), stop=(j == 1))
            mm.then_inc(s_turned, 1)
            wait_ready()
            bank = use()
            pe.transpose(bank[0:IMAGES, 0:P], gates[:, 1, :], ident[:]).then_inc(s_turned, 1)
            wait_ready()
            bank = use()
            pe.transpose(bank[:, 0:IMAGES], soft[:, 2, :], ident[0:IMAGES, 0:IMAGES]).then_inc(s_turned, 1)

            route_turn(0, 0, 1)
            route_products(0, 0, 1)
            route_slots(0)
            for k in range(CHOICES):
                route_invert(0, k)
            for u in range(UNITS):
                tiles(u)

        @block.vector
        def _(dve):
            own = Count(s_own, dve)
            groups = Count(s_ln, dve)
            turned = Count(s_turned, dve)

            def op(ins):
                own.step(ins)
                own.wait()

            def read(n=None):
                bank = turned.n % 2
                turned.step()
                turned.wait()
                return turn_ps[:, bank, :]

            def rsqrt(v, y, tmp):
                op(dve.tensor_scalar(tmp.bitcast(I32), v.bitcast(I32), 1, None, ALU.logical_shift_right))
                op(dve.tensor_scalar(y.bitcast(I32), tmp.bitcast(I32), -1.0, float(0x5F3759DF), ALU.mult, ALU.add))
                for _ in range(3):
                    op(dve.tensor_tensor(tmp, y, y, ALU.mult))
                    op(dve.scalar_tensor_tensor(tmp, tmp, -0.5, v, ALU.mult, ALU.mult))
                    op(dve.scalar_tensor_tensor(y, tmp, 1.5, y, ALU.add, ALU.mult))

            def moments(st, n, m, v, tmp, eps):
                op(dve.tensor_tensor(tmp, st[:, :, 1], st[:, :, 4], ALU.subtract))
                op(dve.tensor_tensor(m, st[:, :, 1], st[:, :, 4], ALU.add))
                op(dve.tensor_scalar(m, m, 0.5, None, ALU.mult))
                op(dve.scalar_tensor_tensor(tmp, tmp, 0.25, tmp, ALU.mult, ALU.mult))
                op(dve.tensor_tensor(v, st[:, :, 2], st[:, :, 5], ALU.add))
                op(dve.scalar_tensor_tensor(v, v, 1.0 / (2 * n), tmp, ALU.mult, ALU.add))
                op(dve.tensor_scalar(v, v, eps, None, ALU.add))

            def token_stats(eps, to=rstd):
                moments(stats[:], P // 2, mean[:], var[:], tmp_s[:], eps)
                rsqrt(var[:], to[:], tmp_s[:])

            def set_shift(to=shift, scale=rstd):
                op(dve.scalar_tensor_tensor(to[:], mean[:], -1.0, scale[:], ALU.mult, ALU.mult))
                dve.sem_inc(s_stats, 1)

            def to_tokens(b):
                for g in range(GROUPS):
                    s = turned.n % 2
                    turned.step()
                    dve.wait_ge(s_freed[s], (turned.n - 1) // 2 + 2)
                    for t in range(g * GROUP, (g + 1) * GROUP):
                        ins = dve.bn_stats(stats[:, t, :], tok[b][:, t, :])
                op(ins)

            def to_channels(groups=GROUPS):
                turned.n += groups
                banks_read(dve, turned.n)

            def normalise(src, dst):
                for g in range(GROUPS):
                    for t in range(g * GROUP, (g + 1) * GROUP):
                        ins = dve.tensor_scalar(dst[:, t, :], src[:, t, :], mean[:, t:t + 1], rstd[:, t:t + 1],
                                                ALU.subtract, ALU.mult)
                    groups.step(ins)

            def bc(ap, shape):
                return ap.to_broadcast(shape)

            for i in range(2):
                dve.sem_inc(s_freed[i], 1)
            dve.sem_inc(s_acc_free, 1)
            for b in range(IMAGES):
                to_tokens(b)
                token_stats(1e-6, first_rstd[b])
                set_shift(first_shift[b], first_rstd[b])
                for g in range(0, GROUPS, 2):
                    for t in range(g * GROUP, (g + 1) * GROUP):
                        ins = dve.tensor_scalar(tok[b][:, t, :], tok[b][:, t, :], mean[:, t:t + 1],
                                                first_rstd[b][:, t:t + 1], ALU.subtract, ALU.mult)
                    groups.step(ins)

            def parameters():
                dve.wait_ge(s_par, 16 * len(small))
                bank = read()
                dve.tensor_copy(lw1T.rearrange("p a j -> p (a j)"), bank[:, 0:2 * P])
                dve.tensor_copy(lw2T.rearrange("p a j -> p (a j)"), bank[:, 2 * P:4 * P]).then_inc(s_freed[(turned.n - 1) % 2], 1)
                bank = read()
                dve.tensor_copy(router[:, 1, :], bank[0:EXPERTS, 0:P])
                dve.tensor_copy(mix_w1T[:], bank[:, P:P + EXPERTS])
                dve.tensor_copy(mix_w2T[:], bank[0:EXPERTS, 2 * P:3 * P])
                for layer in range(2):
                    at = 3 * P + layer * EXPERTS
                    op(dve.tensor_copy(bias[:, layer, :, CHUNKS], bank[:, at:at + EXPERTS]))
                for layer in range(2):
                    op(dve.tensor_copy(bias[:, layer, :, 0:CHUNKS], bias1[layer][:]))
                dve.sem_inc(s_freed[(turned.n - 1) % 2], 1)
                dve.sem_inc(s_bias_in, 1)
                op(dve.tensor_reduce(router_sum[:], router[:], AX.X, ALU.add))
                op(dve.tensor_scalar(router_sum[:], router_sum[:], -1.0 / P, None, ALU.mult))
                dve.tensor_scalar(router[:, 0, :], router[:, 0, :], router_sum[:, 0:1], None, ALU.add)
                dve.tensor_scalar(router[:, 1, :], router[:, 1, :], router_sum[:, 1:2], None, ALU.add).then_inc(s_ready, 1)
                bank = read()
                dve.tensor_copy(routerT[:].rearrange("p l e -> p (l e)"), bank[:, 0:2 * EXPERTS]).then_inc(s_freed[(turned.n - 1) % 2], 1)

            dve.wait_ge(s_par, 16 * len(small))
            for b in range(IMAGES):
                turned.n += GROUPS
                banks_read(dve, turned.n)
                img, by_h, by_w = (m.rearrange("p (h w) -> p h w", h=SIDE) for m in (work[b][:], tok_flat[b], work[2][:]))
                if b == 0:
                    op(dve.tensor_tensor(by_w, img, bc(conv_w[:, 1, :].unsqueeze(1), [P, SIDE, SIDE]), ALU.mult))
                    op(dve.tensor_reduce(lines[:, 1, b, :], by_w, AX.X, ALU.add))
                    dve.sem_inc(s_mul_used, 1)
                if b == 1:
                    parameters()
                dve.wait_ge(s_mul, b + 1)
                op(dve.tensor_reduce(lines[:, 0, b, :], by_h.rearrange("p h w -> p w h"), AX.X, ALU.add))
                if b == 1:
                    dve.wait_ge(s_mul, b + 2)
                    op(dve.tensor_reduce(lines[:, 1, b, :], by_w, AX.X, ALU.add))
            for k in range(2):
                op(dve.bn_stats(stats[:, k, :], lines[:, k, :, :].rearrange("p b s -> p (b s)")))
            moments(stats[:, 0:2, :], SIDE, mean[:, 0:2], var[:, 0:2], tmp_s[:, 0:2], 1e-5)
            rsqrt(var[:, 0:2], rstd[:, 0:2], tmp_s[:, 0:2])
            op(dve.tensor_tensor(line_mul[:], gamma[:], rstd[:, 0:2], ALU.mult))
            op(dve.tensor_tensor(line_add[:], mean[:, 0:2], line_mul[:], ALU.mult))
            op(dve.tensor_tensor(line_add[:], beta[:], line_add[:], ALU.subtract))
            for k in range(2):
                line = lines[:, k, :, :].rearrange("p b s -> p (b s)")
                op(dve.tensor_scalar(line, line, line_mul[:, k:k + 1], line_add[:, k:k + 1], ALU.mult, ALU.add))
                op(dve.tensor_scalar(line, line, 0.0, None, ALU.max))
            op(dve.tensor_tensor(lines[:, 0, :, :], lines[:, 0, :, :], lines[:, 1, :, :], ALU.mult))
            dve.tensor_reduce(dots[:], lines[:, 0, :, :], AX.X, ALU.add).then_inc(s_ready, 1)
            bank = read()
            op(dve.tensor_copy(gates[:, 0, :], bank[:, 0:IMAGES]))
            dve.sem_inc(s_freed[(turned.n - 1) % 2], 1)
            dve.sem_inc(s_ready, 1)
            bank = read()
            op(dve.tensor_tensor(hid[:], bank[:, 0:2 * IMAGES].rearrange("p (a b) -> p a b", a=2),
                                 bc(lb1[:].unsqueeze(2), [P, 2, IMAGES]), ALU.add))
            dve.sem_inc(s_ready, 1)
            dve.sem_inc(s_freed[(turned.n - 1) % 2], 1)
            bank = read()
            op(dve.tensor_scalar(gates[:, 1, :], bank[:, 0:IMAGES], lb2[:], None, ALU.add))
            dve.sem_inc(s_ready, 1)
            dve.sem_inc(s_freed[(turned.n - 1) % 2], 1)
            bank = read()
            op(dve.tensor_copy(soft[:, 0, :], bank[0:IMAGES, 0:P]))
            op(dve.tensor_reduce(soft_s[:, 0:1], soft[:, 0, :], AX.X, ALU.max))
            dve.tensor_scalar(soft_s[:, 1:2], soft_s[:, 0:1], -1.0, None, ALU.mult).then_inc(s_exp_in, 1)
            dve.wait_ge(s_exp, 1)
            op(dve.reciprocal(soft_s[:, 3:4], soft_s[:, 2:3]))
            op(dve.tensor_scalar(soft[:, 2, :], soft[:, 1, :], soft_s[:, 3:4], None, ALU.mult))
            dve.sem_inc(s_ready, 1)
            dve.sem_inc(s_freed[(turned.n - 1) % 2], 1)
            bank = read()
            op(dve.tensor_copy(gates[:, 2, :], bank[:, 0:IMAGES]))
            dve.sem_inc(s_freed[(turned.n - 1) % 2], 1)

            def halves():
                for q in range(2):
                    yield slice(q * TOKENS // 2, (q + 1) * TOKENS // 2)

            def gate(b):
                for half in halves():
                    dve.scalar_tensor_tensor(state[b][:, half], work[b][:, half], gates[:, 2, b:b + 1],
                                             state[b][:, half], ALU.mult, ALU.add).then_inc(s_state, 1)

            def one_hot(k):
                op(dve.tensor_reduce(top[:, 1, :], zb[:], AX.X, ALU.max))
                op(dve.tensor_tensor(chosen[:, k, :, :].rearrange("p e t -> p t e"), zb[:],
                                     bc(top[:, 1, :].unsqueeze(2), [P, BLOCKS, EXPERTS]), ALU.is_equal))

            def route(u):
                layer, b = divmod(u, IMAGES)
                hot = u % 2
                full = [P, BLOCKS, EXPERTS]
                ranks = bc(rank_no[:].unsqueeze(1), full)
                to_tokens(b)
                if u:
                    dve.wait_ge(s_xn, u * QUARTERS)
                token_stats(1e-5)
                set_shift()
                dve.wait_ge(s_acc, u + 1)
                op(dve.tensor_tensor(z[:], acc_ps[:, 0:BLOCKS * EXPERTS].rearrange("p (t e) -> p t e", e=EXPERTS),
                                     bc(rstd[:].unsqueeze(2), full), ALU.mult))
                dve.sem_inc(s_acc_free, 1)
                op(dve.tensor_tensor(z[:], z[:], bc(router_b[:, layer, :].unsqueeze(1), full), ALU.add))
                op(dve.tensor_reduce(top[:, 0, :], z[:], AX.X, ALU.max))
                op(dve.tensor_tensor(za[:], z[:], bc(top[:, 0, :].unsqueeze(2), full), ALU.subtract))
                dve.sem_inc(s_exp_in, 1)
                op(dve.scalar_tensor_tensor(zb[:], za[:], 0.0, ranks, ALU.is_ge, ALU.mult))
                one_hot(0)
                first = chosen[:, 0, :, :].rearrange("p e t -> p t e")
                op(dve.scalar_tensor_tensor(z[:], first, -3.0e38, z[:], ALU.mult, ALU.add))
                op(dve.tensor_reduce(top[:, 1, :], z[:], AX.X, ALU.max))
                op(dve.tensor_tensor(zb[:], z[:], bc(top[:, 1, :].unsqueeze(2), full), ALU.is_ge))
                op(dve.tensor_tensor(zb[:], zb[:], ranks, ALU.mult))
                one_hot(1)
                dve.tensor_tensor(chosen_any[:], chosen[:, 0, :, :], chosen[:, 1, :, :], ALU.add).then_inc(s_ready, 1)
                bank = read()
                op(dve.tensor_copy(prefix[:].rearrange("p e t -> p (e t)"), bank[:, 0:EXPERTS * BLOCKS]))
                dve.sem_inc(s_freed[(turned.n - 1) % 2], 1)
                bank = read()
                op(dve.tensor_copy(total[:].rearrange("p e t -> p (e t)"), bank[:, 0:EXPERTS * BLOCKS]))
                dve.sem_inc(s_freed[(turned.n - 1) % 2], 1)
                op(dve.tensor_tensor_scan(upto[:].rearrange("p e t -> p (e t)"), resets[:].rearrange("p e t -> p (e t)"),
                                          total[:].rearrange("p e t -> p (e t)"), 0.0, ALU.mult, ALU.add))
                counts = upto[:, :, BLOCKS - 1]
                op(dve.tensor_scalar(n_tiles_i[:], counts, float(SLOTS - 1), None, ALU.add))
                op(dve.tensor_scalar(n_tiles_i[:], n_tiles_i[:], SLOTS.bit_length() - 1, None, ALU.logical_shift_right))
                op(dve.tensor_copy(n_tiles[:, 0, :], n_tiles_i[:]))
                op(dve.memset(n_tiles[:, 1, :], 1.0))
                op(dve.tensor_tensor_scan(n_tiles[:, 2, :], n_tiles[:, 1, :], n_tiles[:, 0, :], 0.0, ALU.mult, ALU.add))
                op(dve.tensor_tensor(n_tiles[:, 3, :], n_tiles[:, 2, :], n_tiles[:, 0, :], ALU.subtract))
                op(dve.tensor_scalar(n_tiles[:, 3, :], n_tiles[:, 3, :], float(SLOTS), None, ALU.mult))
                op(dve.tensor_tensor(upto[:], upto[:], total[:], ALU.subtract))
                op(dve.tensor_tensor(upto[:], upto[:], prefix[:], ALU.add))
                op(dve.tensor_tensor(upto[:], upto[:], bc(n_tiles[:, 3, :].unsqueeze(2), [P, EXPERTS, BLOCKS]), ALU.add))

                def tile_experts():
                    op(dve.tensor_tensor(tile_cmp[:], bc(n_tiles[:, 2, :].unsqueeze(1), [P, TILES, EXPERTS]),
                                         bc(tile_no[:].unsqueeze(2), [P, TILES, EXPERTS]), ALU.is_le))
                    op(dve.tensor_reduce(tile_e[:], tile_cmp[:], AX.X, ALU.add))
                    op(dve.tensor_scalar(tile_e[:], tile_e[:], float(EXPERTS - 1), None, ALU.min))
                    op(dve.tensor_copy(tile_expert[hot][:], tile_e[:]))
                    dve.sem_inc(s_experts, 1)

                pair = work[2][:, 0:CHOICES * EXPERTS * BLOCKS].rearrange("p (k e t) -> p k e t", k=CHOICES, e=EXPERTS)
                op(dve.tensor_tensor(pair, chosen[:], bc(upto[:].unsqueeze(1), [P, CHOICES, EXPERTS, BLOCKS]), ALU.mult))
                op(dve.tensor_reduce(place[:], pair.rearrange("p k e t -> p k t e"), AX.X, ALU.add))
                op(dve.tensor_copy(place_i[:, 0, :, :], place[:]))
                op(dve.tensor_scalar(place_i[:, 1, :, :], place_i[:, 0, :, :], P - 1, None, ALU.bitwise_and))
                op(dve.tensor_scalar(place_i[:, 2, :, :], place_i[:, 0, :, :], P.bit_length() - 1, None,
                                     ALU.logical_shift_right))
                op(dve.tensor_copy(place_b[:], place_i[:, 1:3, :, :]))
                tile_experts()
                n = TILES * HALVES
                for k in range(CHOICES):
                    hot_lane, hot_block = one_hots(u, k)
                    dve.tensor_tensor(hot_lane, lane[:], bc(place_b[:, 0, k, :].unsqueeze(1), [P, P, BLOCKS]),
                                      ALU.is_equal)
                    op(dve.tensor_tensor(hot_block[:, 0, :, :], block_no[:],
                                         bc(place_b[:, 1, k, :].unsqueeze(1), [P, n, BLOCKS]), ALU.is_equal))
                    op(dve.tensor_tensor(hot_block[:, 1, :, :], hot_block[:, 0, :, :],
                                         bc(row_lo[:].unsqueeze(1), [P, n, BLOCKS]), ALU.mult))
                    dve.tensor_scalar(hot_block[:, 0, :, :], hot_block[:, 0, :, :], row_hi[:, k:k + 1], None,
                                      ALU.mult).then_inc(s_hot, 1)
                dve.wait_ge(s_exp, u + 2)
                op(dve.tensor_reduce(top[:, 2, :], prob[:], AX.X, ALU.add))
                op(dve.reciprocal(top[:, 2, :], top[:, 2, :]))
                op(dve.tensor_tensor(prob[:], prob[:], bc(top[:, 2, :].unsqueeze(2), full), ALU.mult))
                for k in range(CHOICES):
                    op(dve.tensor_tensor(za[:], prob[:], chosen[:, k, :, :].rearrange("p e t -> p t e"), ALU.mult))
                    op(dve.tensor_reduce(share[b][:, k, :], za[:], AX.X, ALU.add))
                if layer == 0:
                    op(dve.tensor_tensor(top[:, 3, :], share[b][:, 0, :], share[b][:, 1, :], ALU.add))
                    op(dve.reciprocal(top[:, 3, :], top[:, 3, :]))
                    op(dve.tensor_tensor(share[b][:], share[b][:], bc(top[:, 3, :].unsqueeze(1), [P, CHOICES, BLOCKS]),
                                         ALU.mult))
                dve.wait_ge(s_hot_used, (u + 1) * CHOICES)
                if layer:
                    dve.sem_inc(s_buf, 1)
                op(dve.tensor_copy(rows_f[:, 0:2, :], acc_ps[:, 0:2 * n].rearrange("p (a q) -> p a q", a=2)))
                dve.sem_inc(s_acc_free, 1)
                op(dve.tensor_tensor(rows_f[:, 0, :], rows_f[:, 0, :], rows_f[:, 1, :], ALU.add))
                op(dve.tensor_scalar(rows_f[:, 1, :], rows_f[:, 0, :], 0.0, float(EMPTY), ALU.is_equal, ALU.mult))
                op(dve.scalar_tensor_tensor(rows_f[:, 0, :], rows_f[:, 0, :], -1.0, rows_f[:, 1, :], ALU.add, ALU.add))
                op(dve.tensor_copy(tile_rows[hot][:, :, 1, :], rows_f[:, 0, :].rearrange("p (j h) -> p j h", h=HALVES)))
                op(dve.tensor_scalar(rows_f[:, 1, :], rows_f[:, 0, :], float(TOKENS), -float(TOKENS), ALU.is_ge, ALU.mult))
                op(dve.tensor_tensor(rows_f[:, 1, :], rows_f[:, 1, :], rows_f[:, 0, :], ALU.add))
                op(dve.tensor_scalar(tile_rows[hot][:, :, 0, :], rows_f[:, 1, :].rearrange("p (j h) -> p j h", h=HALVES),
                                     float(TOKENS - 1), None, ALU.min))
                dve.sem_inc(s_rows, 1)

            def combine(u):
                b = u % IMAGES
                for q in range(QUARTERS):
                    dve.wait_ge(s_y_in[u][q], 16 * CHOICES)
                    for k in range(CHOICES):
                        if k == CHOICES - 1 and u == UNITS - 1:
                            dve.wait_ge(s_shared, q + 1)
                            for g in range(q * GROUPS // QUARTERS, (q + 1) * GROUPS // QUARTERS):
                                ap = tok[b][:, g * GROUP:(g + 1) * GROUP, :]
                                groups.step(dve.tensor_tensor(ap, ap, work_tok[1 + k][:, g * GROUP:(g + 1) * GROUP, :],
                                                              ALU.add))
                            continue
                        for t in range(BLOCKS)[quarter(q)]:
                            ins = dve.scalar_tensor_tensor(tok[b][:, t, :], work_tok[1 + k][:, t, :],
                                                           share[b][:, k, t:t + 1], tok[b][:, t, :], ALU.mult, ALU.add)
                            if k == CHOICES - 1 and t % GROUP == GROUP - 1:
                                groups.step(ins)
                        if k < CHOICES - 1:
                            op(ins)
                groups.wait()

            def mix(b):
                for t in range(BLOCKS):
                    ins = dve.bn_stats(stats[:, t, :], tok[b][:, t, :])
                op(ins)
                dve.wait_ge(s_xn_st[1 + b], 16 * QUARTERS)
                token_stats(1e-6)
                normalise(tok[b], work_tok[0])
                turned.n += 2 * GROUPS
                banks_read(dve, turned.n)
                op(dve.tensor_reduce(gap[:], gap_parts[:], AX.X, ALU.add))
                dve.tensor_scalar(gap[:], gap[:], 1.0 / TOKENS, None, ALU.mult).then_inc(s_ready, 1)
                pool_in = work[1][:].rearrange("p (h w) -> p h w", h=SIDE)
                across = work[2][:].rearrange("p (h w) -> p h w", h=SIDE)
                last, edge = SIDE - 1, SIDE - 2

                def grow_across(k):
                    dve.tensor_tensor(across[:, :, 1:last], pool_in[:, :, 0:edge], pool_in[:, :, 2:SIDE], ALU.max)
                    op(dve.tensor_copy(across[:, :, 0:SIDE:last], pool_in[:, :, 1:last:edge - 1]))

                grow_across(1)
                bank = read()
                op(dve.tensor_scalar(mix_h[:], bank[0:EXPERTS, 0:1], mix_b1[:], 0.0, ALU.add, ALU.max))
                dve.sem_inc(s_freed[(turned.n - 1) % 2], 1)
                dve.sem_inc(s_ready, 1)
                bank = read()
                op(dve.tensor_scalar(mix_s[:, 0:1], bank[:, 0:1], mix_b2[:], 0.0, ALU.add, ALU.max))
                dve.sem_inc(s_freed[(turned.n - 1) % 2], 1)
                op(dve.tensor_scalar(mix_hot[:, 0, :], step_no[:], mix_s[:, 0:1], None, ALU.is_le))
                op(dve.tensor_reduce(mix_s[:, 1:2], mix_hot[:, 0, 1:KERNELS - 1], AX.X, ALU.add))
                op(dve.tensor_tensor(mix_s[:, 2:3], mix_s[:, 0:1], mix_s[:, 1:2], ALU.subtract))
                op(dve.tensor_scalar(mix_s[:, 3:4], mix_s[:, 1:2], 1.0, mix_s[:, 0:1], ALU.add, ALU.subtract))
                op(dve.tensor_scalar(mix_hot[:, 0, :], step_no[:], mix_s[:, 1:2], mix_s[:, 3:4], ALU.is_equal, ALU.mult))
                op(dve.tensor_scalar(mix_hot[:, 1, :], step_no[:], -1.0, mix_s[:, 1:2], ALU.add, ALU.is_equal))
                op(dve.tensor_scalar(mix_hot[:, 1, :], mix_hot[:, 1, :], mix_s[:, 2:3], None, ALU.mult))
                op(dve.tensor_tensor(mix_hot[:, 0, :], mix_hot[:, 0, :], mix_hot[:, 1, :], ALU.add))
                op(dve.tensor_scalar(mix_hot[:, 0, 0:1], mix_hot[:, 0, 0:1], 1.0, None, ALU.add))
                op(dve.scalar_tensor_tensor(state[b][:], work[1][:], mix_hot[:, 0, 0:1], state[b][:], ALU.mult, ALU.add))
                for k in range(1, KERNELS):
                    if k > 1:
                        grow_across(k)
                    else:
                        op(dve.tensor_tensor(across, across, pool_in, ALU.max))
                    dve.tensor_tensor(pool_in[:, 1:last, :], across[:, 0:edge, :], across[:, 2:SIDE, :], ALU.max)
                    op(dve.tensor_copy(pool_in[:, 0:SIDE:last, :], across[:, 1:last:edge - 1, :]))
                    if k == 1:
                        op(dve.tensor_tensor(pool_in, across, pool_in, ALU.max))
                    for half in halves() if k == KERNELS - 1 else [slice(0, TOKENS)]:
                        ins = dve.scalar_tensor_tensor(state[b][:, half], work[1][:, half], mix_hot[:, 0, k:k + 1],
                                                       state[b][:, half], ALU.mult, ALU.add)
                        if k < KERNELS - 1:
                            op(ins)
                        else:
                            ins.then_inc(s_state, 1)

            for b in range(IMAGES):
                gate(b)
                route(b)
            dve.sem_inc(s_buf, 1)
            for b in range(IMAGES):
                combine(b)
                mix(b)
                route(2 + b)
            for b in range(IMAGES):
                combine(2 + b)
                if b == 0:
                    dve.sem_inc(s_buf, 1)


_INS = ['x', 'L0_conv_w1', 'L0_conv_w2', 'L0_conv_g1', 'L0_conv_b1', 'L0_conv_g2', 'L0_conv_b2', 'L0_conv_lw1',
        'L0_conv_lb1', 'L0_conv_lw2', 'L0_conv_lb2', 'L0_ffn_Wr', 'L0_ffn_br', 'L0_ffn_W1', 'L0_ffn_b1', 'L0_ffn_W2',
        'L0_ffn_b2', 'L1_conv_w1', 'L1_conv_b1', 'L1_conv_w2', 'L1_conv_b2', 'L1_ffn_gate_w', 'L1_ffn_gate_b',
        'L1_ffn_w1', 'L1_ffn_b1', 'L1_ffn_w2', 'L1_ffn_b2']


def kernel(**inputs):
    import concourse.bacc as bacc
    from concourse.bass_utils import run_bass_kernel_spmd

    nc = bacc.Bacc("TRN2", target_bir_lowering=False, num_devices=1)
    arrays, args = {}, {}
    for name in _INS:
        a = np.ascontiguousarray(inputs[name])
        arrays[f"in_{name}"] = a
        args[name] = nc.dram_tensor(f"in_{name}", a.shape, mybir.dt.from_np(a.dtype), kind="ExternalInput").ap()
    out = nc.dram_tensor("out_0", (IMAGES, P, SIDE, SIDE), F32, kind="ExternalOutput").ap()
    build(nc, out=out, **args)
    r = run_bass_kernel_spmd(nc, [arrays], core_ids=[0])
    return r.results[0]["out_0"]
```
